# Optimizing a Trainium2 kernel written in Bass

```python
import numpy as np
import jax
import jax.numpy as jnp

def _softmax(x, axis=-1):
    return jax.nn.softmax(x, axis=axis)

def _gelu(x):
    return jax.nn.gelu(x, approximate=True)

def _silu(x):
    return jax.nn.silu(x)

def _sigmoid(x):
    return jax.nn.sigmoid(x)

def _layernorm(x, axis=-1, eps=1e-05):
    m = jnp.mean(x, axis=axis, keepdims=True)
    v = jnp.var(x, axis=axis, keepdims=True)
    return (x - m) / jnp.sqrt(v + eps)

def _scatter_add(tgt, idx, src, axis=0):
    return tgt.at[idx].add(src)

def _segment_sum(src, seg, n):
    return jax.ops.segment_sum(src, seg, n)
kernel_name = 'mk_macaron_d1_jaxref_r8_ecf08a'

def setup_inputs(seed: int=0):
    np.random.seed(seed)
    _w = jnp.asarray

    def _L0_attn_setup():
        import jax, jax.numpy as jnp
        import numpy as np
        B, L, D, H, W = (2, 512, 128, 16, 128)
        E = D // H

        def _ln(x, g, b):
            m = jnp.mean(x, axis=-1, keepdims=True)
            v = jnp.mean((x - m) ** 2, axis=-1, keepdims=True)
            return (x - m) / jnp.sqrt(v + 1e-05) * g + b

        def _swa(xn, Wqkv, bqkv, Wp, bp):
            b_, l_, d_ = xn.shape
            nb = l_ // W
            qkv = xn @ Wqkv + bqkv
            q, k, v = jnp.split(qkv, 3, axis=-1)

            def heads(t):
                return t.reshape(b_, l_, H, E).transpose(0, 2, 1, 3)
            q, k, v = (heads(q), heads(k), heads(v))

            def blk(t):
                return t.reshape(b_, H, nb, W, E)
            qb, kb, vb = (blk(q), blk(k), blk(v))
            kprev = jnp.pad(kb, ((0, 0), (0, 0), (1, 0), (0, 0), (0, 0)))[:, :, :nb]
            vprev = jnp.pad(vb, ((0, 0), (0, 0), (1, 0), (0, 0), (0, 0)))[:, :, :nb]
            kc = jnp.concatenate([kprev, kb], axis=3)
            vc = jnp.concatenate([vprev, vb], axis=3)
            scores = jnp.einsum('bhnre,bhnse->bhnrs', qb, kc) / np.float32(np.sqrt(E))
            r = jnp.arange(W)[:, None]
            s = jnp.arange(2 * W)[None, :]
            band = (s >= r + 1) & (s <= r + W)
            first = band & (s >= W)
            mask = jnp.concatenate([first[None], jnp.broadcast_to(band, (nb - 1, W, 2 * W))], axis=0)
            scores = jnp.where(mask[None, None], scores, jnp.float32(-1e+30))
            attn = jax.nn.softmax(scores, axis=-1)
            out = jnp.einsum('bhnrs,bhnse->bhnre', attn, vc)
            out = out.reshape(b_, H, l_, E).transpose(0, 2, 1, 3).reshape(b_, l_, d_)
            return out @ Wp + bp

        def _linattn(xn, Wqkv, bqkv, Wo, bo):
            b_, l_, d_ = xn.shape
            C = 128
            nc = l_ // C
            qkv = xn @ Wqkv + bqkv
            q, k, v = jnp.split(qkv, 3, axis=-1)
            q = q.reshape(b_, l_, H, E)
            k = k.reshape(b_, l_, H, E)
            v = v.reshape(b_, l_, H, E)
            q = jax.nn.elu(q * np.float32(E ** (-0.5))) + np.float32(1.0001)
            k = jax.nn.elu(k) + np.float32(1.0001)

            def chunks(t):
                return t.reshape(b_, nc, C, H, E).transpose(1, 0, 3, 2, 4)
            qc, kc, vc = (chunks(q), chunks(k), chunks(v))
            tril = jnp.tril(jnp.ones((C, C), jnp.float32))

            def step(carry, inp):
                S, z = carry
                qi, ki, vi = inp
                A = jnp.einsum('bhce,bhde->bhcd', qi, ki) * tril
                num = jnp.einsum('bhce,bhef->bhcf', qi, S) + jnp.einsum('bhcd,bhdf->bhcf', A, vi)
                den = jnp.einsum('bhce,bhe->bhc', qi, z) + A.sum(-1)
                o = num / (den[..., None] + 1e-06)
                S = S + jnp.einsum('bhce,bhcf->bhef', ki, vi)
                z = z + ki.sum(2)
                return ((S, z), o)
            S0 = jnp.zeros((b_, H, E, E), jnp.float32)
            z0 = jnp.zeros((b_, H, E), jnp.float32)
            _, out = jax.lax.scan(step, (S0, z0), (qc, kc, vc))
            out = out.transpose(1, 0, 3, 2, 4).reshape(b_, l_, d_)
            return out @ Wo + bo
        key = jax.random.key(seed)
        ks = jax.random.split(key, 9)

        def w(k, shape, s=0.02):
            return jax.random.normal(k, shape, jnp.float32) * s
        return {'x': jax.random.normal(ks[0], (B, L, D), jnp.float32), 'g1': jnp.ones((D,), jnp.float32), 'b1': jnp.zeros((D,), jnp.float32), 'Wqkv_a': w(ks[1], (D, 3 * D)), 'bqkv_a': jnp.zeros((3 * D,), jnp.float32), 'Wp_a': w(ks[2], (D, D)), 'bp_a': jnp.zeros((D,), jnp.float32), 'Wqkv_s': w(ks[3], (D, 3 * D)), 'bqkv_s': jnp.zeros((3 * D,), jnp.float32), 'Wo_s': w(ks[4], (D, D)), 'bo_s': jnp.zeros((D,), jnp.float32), 'Wo': w(ks[5], (D, D)), 'bo': jnp.zeros((D,), jnp.float32), 'gm': jnp.ones((D,), jnp.float32), 'bm': jnp.zeros((D,), jnp.float32), 'W1': w(ks[6], (D, 4 * D)), 'b1m': jnp.zeros((4 * D,), jnp.float32), 'W2': w(ks[7], (4 * D, D)), 'b2m': jnp.zeros((D,), jnp.float32)}
    _L0_attn_in = _L0_attn_setup()

    def _L0_ffn_setup():
        import math
        import jax
        import jax.numpy as jnp
        import numpy as np
        B, T, D = (1, 256, 128)
        H, KV, DH = (16, 4, 64)
        E, TOPK, DFF = (32, 4, 128)
        WINDOW = 128
        EPS = 1e-05
        ROPE_BASE = 150000.0
        ROPE_SCALE = 32.0

        def _rmsnorm(x, w):
            rms = jax.lax.rsqrt(jnp.mean(x * x, axis=-1, keepdims=True) + EPS)
            return w * (x * rms)

        def _apply_rope(x, sin, cos):
            x1, x2 = (x[..., ::2], x[..., 1::2])
            out = jnp.stack([x1 * cos - x2 * sin, x1 * sin + x2 * cos], axis=-1)
            return out.reshape(x.shape)
        key = jax.random.key(seed)
        ks = jax.random.split(key, 12)
        s = 0.02
        return {'x': jax.random.normal(ks[0], (B, T, D), jnp.float32), 'attn_norm_w': 1.0 + 0.02 * jax.random.normal(ks[1], (D,), jnp.float32), 'ffn_norm_w': 1.0 + 0.02 * jax.random.normal(ks[2], (D,), jnp.float32), 'qkv_w': s * jax.random.normal(ks[3], (D, H * DH + 2 * KV * DH), jnp.float32), 'qkv_b': s * jax.random.normal(ks[4], (H * DH + 2 * KV * DH,), jnp.float32), 'proj_w': s * jax.random.normal(ks[5], (H * DH, D), jnp.float32), 'proj_b': s * jax.random.normal(ks[6], (D,), jnp.float32), 'attn_sink': 0.5 * jax.random.normal(ks[7], (H,), jnp.float32), 'gate_w': s * jax.random.normal(ks[8], (D, E), jnp.float32), 'gate_b': s * jax.random.normal(ks[9], (E,), jnp.float32), 'W_up': s * jax.random.normal(ks[10], (E, D, 2 * DFF), jnp.float32), 'W_down': s * jax.random.normal(ks[11], (E, DFF, D), jnp.float32)}
    _L0_ffn_in = _L0_ffn_setup()
    _d = {'L0_attn_x': _L0_attn_in['x'], 'L0_attn_g1': _L0_attn_in['g1'], 'L0_attn_b1': _L0_attn_in['b1'], 'L0_attn_Wqkv_a': _L0_attn_in['Wqkv_a'], 'L0_attn_bqkv_a': _L0_attn_in['bqkv_a'], 'L0_attn_Wp_a': _L0_attn_in['Wp_a'], 'L0_attn_bp_a': _L0_attn_in['bp_a'], 'L0_attn_Wqkv_s': _L0_attn_in['Wqkv_s'], 'L0_attn_bqkv_s': _L0_attn_in['bqkv_s'], 'L0_attn_Wo_s': _L0_attn_in['Wo_s'], 'L0_attn_bo_s': _L0_attn_in['bo_s'], 'L0_attn_Wo': _L0_attn_in['Wo'], 'L0_attn_bo': _L0_attn_in['bo'], 'L0_attn_gm': _L0_attn_in['gm'], 'L0_attn_bm': _L0_attn_in['bm'], 'L0_attn_W1': _L0_attn_in['W1'], 'L0_attn_b1m': _L0_attn_in['b1m'], 'L0_attn_W2': _L0_attn_in['W2'], 'L0_attn_b2m': _L0_attn_in['b2m'], 'L0_ffn_attn_norm_w': _L0_ffn_in['attn_norm_w'], 'L0_ffn_ffn_norm_w': _L0_ffn_in['ffn_norm_w'], 'L0_ffn_qkv_w': _L0_ffn_in['qkv_w'], 'L0_ffn_qkv_b': _L0_ffn_in['qkv_b'], 'L0_ffn_proj_w': _L0_ffn_in['proj_w'], 'L0_ffn_proj_b': _L0_ffn_in['proj_b'], 'L0_ffn_attn_sink': _L0_ffn_in['attn_sink'], 'L0_ffn_gate_w': _L0_ffn_in['gate_w'], 'L0_ffn_gate_b': _L0_ffn_in['gate_b'], 'L0_ffn_W_up': _L0_ffn_in['W_up'], 'L0_ffn_W_down': _L0_ffn_in['W_down']}
    _x0 = _d['L0_attn_x']
    _d['L0_attn_x'] = jax.random.normal(jax.random.fold_in(jax.random.key(seed), 1), (4, 512, 128), dtype=_x0.dtype)
    del _x0
    return _d

def reference(L0_attn_x, L0_attn_g1, L0_attn_b1, L0_attn_Wqkv_a, L0_attn_bqkv_a, L0_attn_Wp_a, L0_attn_bp_a, L0_attn_Wqkv_s, L0_attn_bqkv_s, L0_attn_Wo_s, L0_attn_bo_s, L0_attn_Wo, L0_attn_bo, L0_attn_gm, L0_attn_bm, L0_attn_W1, L0_attn_b1m, L0_attn_W2, L0_attn_b2m, L0_ffn_attn_norm_w, L0_ffn_ffn_norm_w, L0_ffn_qkv_w, L0_ffn_qkv_b, L0_ffn_proj_w, L0_ffn_proj_b, L0_ffn_attn_sink, L0_ffn_gate_w, L0_ffn_gate_b, L0_ffn_W_up, L0_ffn_W_down):

    def _L0_attn_ref(x, g1, b1, Wqkv_a, bqkv_a, Wp_a, bp_a, Wqkv_s, bqkv_s, Wo_s, bo_s, Wo, bo, gm, bm, W1, b1m, W2, b2m):
        import jax, jax.numpy as jnp
        import numpy as np
        B, L, D, H, W = (2, 512, 128, 16, 128)
        E = D // H

        def _ln(x, g, b):
            m = jnp.mean(x, axis=-1, keepdims=True)
            v = jnp.mean((x - m) ** 2, axis=-1, keepdims=True)
            return (x - m) / jnp.sqrt(v + 1e-05) * g + b

        def _swa(xn, Wqkv, bqkv, Wp, bp):
            b_, l_, d_ = xn.shape
            nb = l_ // W
            qkv = xn @ Wqkv + bqkv
            q, k, v = jnp.split(qkv, 3, axis=-1)

            def heads(t):
                return t.reshape(b_, l_, H, E).transpose(0, 2, 1, 3)
            q, k, v = (heads(q), heads(k), heads(v))

            def blk(t):
                return t.reshape(b_, H, nb, W, E)
            qb, kb, vb = (blk(q), blk(k), blk(v))
            kprev = jnp.pad(kb, ((0, 0), (0, 0), (1, 0), (0, 0), (0, 0)))[:, :, :nb]
            vprev = jnp.pad(vb, ((0, 0), (0, 0), (1, 0), (0, 0), (0, 0)))[:, :, :nb]
            kc = jnp.concatenate([kprev, kb], axis=3)
            vc = jnp.concatenate([vprev, vb], axis=3)
            scores = jnp.einsum('bhnre,bhnse->bhnrs', qb, kc) / np.float32(np.sqrt(E))
            r = jnp.arange(W)[:, None]
            s = jnp.arange(2 * W)[None, :]
            band = (s >= r + 1) & (s <= r + W)
            first = band & (s >= W)
            mask = jnp.concatenate([first[None], jnp.broadcast_to(band, (nb - 1, W, 2 * W))], axis=0)
            scores = jnp.where(mask[None, None], scores, jnp.float32(-1e+30))
            attn = jax.nn.softmax(scores, axis=-1)
            out = jnp.einsum('bhnrs,bhnse->bhnre', attn, vc)
            out = out.reshape(b_, H, l_, E).transpose(0, 2, 1, 3).reshape(b_, l_, d_)
            return out @ Wp + bp

        def _linattn(xn, Wqkv, bqkv, Wo, bo):
            b_, l_, d_ = xn.shape
            C = 128
            nc = l_ // C
            qkv = xn @ Wqkv + bqkv
            q, k, v = jnp.split(qkv, 3, axis=-1)
            q = q.reshape(b_, l_, H, E)
            k = k.reshape(b_, l_, H, E)
            v = v.reshape(b_, l_, H, E)
            q = jax.nn.elu(q * np.float32(E ** (-0.5))) + np.float32(1.0001)
            k = jax.nn.elu(k) + np.float32(1.0001)

            def chunks(t):
                return t.reshape(b_, nc, C, H, E).transpose(1, 0, 3, 2, 4)
            qc, kc, vc = (chunks(q), chunks(k), chunks(v))
            tril = jnp.tril(jnp.ones((C, C), jnp.float32))

            def step(carry, inp):
                S, z = carry
                qi, ki, vi = inp
                A = jnp.einsum('bhce,bhde->bhcd', qi, ki) * tril
                num = jnp.einsum('bhce,bhef->bhcf', qi, S) + jnp.einsum('bhcd,bhdf->bhcf', A, vi)
                den = jnp.einsum('bhce,bhe->bhc', qi, z) + A.sum(-1)
                o = num / (den[..., None] + 1e-06)
                S = S + jnp.einsum('bhce,bhcf->bhef', ki, vi)
                z = z + ki.sum(2)
                return ((S, z), o)
            S0 = jnp.zeros((b_, H, E, E), jnp.float32)
            z0 = jnp.zeros((b_, H, E), jnp.float32)
            _, out = jax.lax.scan(step, (S0, z0), (qc, kc, vc))
            out = out.transpose(1, 0, 3, 2, 4).reshape(b_, l_, d_)
            return out @ Wo + bo
        xn = _ln(x, g1, b1)
        attn_out = _swa(xn, Wqkv_a, bqkv_a, Wp_a, bp_a)
        ssm_out = _linattn(xn, Wqkv_s, bqkv_s, Wo_s, bo_s)
        mixed = (attn_out + ssm_out) @ Wo + bo
        x1 = x + mixed
        h = _ln(x1, gm, bm)
        mlp = jax.nn.gelu(h @ W1 + b1m, approximate=False) @ W2 + b2m
        return x1 + mlp

    def _L0_ffn_ref(x, attn_norm_w, ffn_norm_w, qkv_w, qkv_b, proj_w, proj_b, attn_sink, gate_w, gate_b, W_up, W_down):
        import math
        import jax
        import jax.numpy as jnp
        import numpy as np
        B, T, D = (1, 256, 128)
        H, KV, DH = (16, 4, 64)
        E, TOPK, DFF = (32, 4, 128)
        WINDOW = 128
        EPS = 1e-05
        ROPE_BASE = 150000.0
        ROPE_SCALE = 32.0

        def _rmsnorm(x, w):
            rms = jax.lax.rsqrt(jnp.mean(x * x, axis=-1, keepdims=True) + EPS)
            return w * (x * rms)

        def _apply_rope(x, sin, cos):
            x1, x2 = (x[..., ::2], x[..., 1::2])
            out = jnp.stack([x1 * cos - x2 * sin, x1 * sin + x2 * cos], axis=-1)
            return out.reshape(x.shape)
        Bx, Tx, Dx = x.shape
        h = _rmsnorm(x, attn_norm_w)
        qkv = h @ qkv_w + qkv_b
        q = qkv[..., :H * DH].reshape(Bx, Tx, H, DH).transpose(0, 2, 1, 3)
        k = qkv[..., H * DH:H * DH + KV * DH].reshape(Bx, Tx, KV, DH).transpose(0, 2, 1, 3)
        v = qkv[..., H * DH + KV * DH:].reshape(Bx, Tx, KV, DH).transpose(0, 2, 1, 3)
        pos = jnp.arange(Tx, dtype=jnp.float32) / ROPE_SCALE
        inv_freq = 1.0 / ROPE_BASE ** (jnp.arange(0, DH, 2, dtype=jnp.float32) / DH)
        freqs = pos[:, None] * inv_freq[None, :]
        sin, cos = (jnp.sin(freqs), jnp.cos(freqs))
        q = _apply_rope(q, sin, cos)
        k = _apply_rope(k, sin, cos)
        rep = H // KV
        k = jnp.repeat(k, rep, axis=1)
        v = jnp.repeat(v, rep, axis=1)
        logits = jnp.einsum('bhqd,bhkd->bhqk', q, k) / math.sqrt(DH)
        i = jnp.arange(Tx)[:, None]
        j = jnp.arange(Tx)[None, :]
        mask = (j > i) | (i - j > WINDOW)
        logits = jnp.where(mask, -jnp.inf, logits)
        lse = jax.nn.logsumexp(logits, axis=-1, keepdims=True)
        denom_log = jnp.logaddexp(lse, attn_sink.reshape(1, H, 1, 1))
        attn = jnp.exp(logits - denom_log)
        y = jnp.einsum('bhqk,bhkd->bhqd', attn, v)
        y = y.transpose(0, 2, 1, 3).reshape(Bx, Tx, H * DH)
        x = x + (y @ proj_w + proj_b)
        h2 = _rmsnorm(x, ffn_norm_w).reshape(Bx * Tx, Dx)
        glogits = h2 @ gate_w + gate_b
        topv, topi = jax.lax.top_k(glogits, TOPK)
        gw = jax.nn.softmax(topv, axis=-1)
        N = Bx * Tx
        combine = jnp.zeros((N, E), x.dtype).at[jnp.arange(N)[:, None], topi].add(gw)

        def body(acc, we):
            wu, wd, ce = we
            ug = h2 @ wu
            u, g = (ug[:, :DFF], ug[:, DFF:])
            return (acc + ce[:, None] * (jax.nn.silu(g) * u @ wd), None)
        y2, _ = jax.lax.scan(body, jnp.zeros_like(h2), (W_up, W_down, combine.T))
        return x + y2.reshape(Bx, Tx, Dx)
    x = L0_attn_x
    x = x + 0.5 * _L0_ffn_ref(_layernorm(x, axis=-1), L0_ffn_attn_norm_w, L0_ffn_ffn_norm_w, L0_ffn_qkv_w, L0_ffn_qkv_b, L0_ffn_proj_w, L0_ffn_proj_b, L0_ffn_attn_sink, L0_ffn_gate_w, L0_ffn_gate_b, L0_ffn_W_up, L0_ffn_W_down)
    x = x + _L0_attn_ref(_layernorm(x, axis=-1), L0_attn_g1, L0_attn_b1, L0_attn_Wqkv_a, L0_attn_bqkv_a, L0_attn_Wp_a, L0_attn_bp_a, L0_attn_Wqkv_s, L0_attn_bqkv_s, L0_attn_Wo_s, L0_attn_bo_s, L0_attn_Wo, L0_attn_bo, L0_attn_gm, L0_attn_bm, L0_attn_W1, L0_attn_b1m, L0_attn_W2, L0_attn_b2m)
    x = x + 0.5 * _L0_ffn_ref(_layernorm(x, axis=-1), L0_ffn_attn_norm_w, L0_ffn_ffn_norm_w, L0_ffn_qkv_w, L0_ffn_qkv_b, L0_ffn_proj_w, L0_ffn_proj_b, L0_ffn_attn_sink, L0_ffn_gate_w, L0_ffn_gate_b, L0_ffn_W_up, L0_ffn_W_down)
    return x

_drawn_inputs = setup_inputs


def setup_inputs(seed=0):
    import zlib

    import numpy as np

    out = dict(_drawn_inputs(seed))
    spreads = {'L0_attn_g1': (1.0, 0.6),
     'L0_attn_b1': (0.0, 0.8),
     'L0_attn_bqkv_a': (0.0, 0.8),
     'L0_attn_bp_a': (0.0, 0.8),
     'L0_attn_bqkv_s': (0.0, 0.8),
     'L0_attn_bo_s': (0.0, 0.8),
     'L0_attn_bo': (0.0, 0.387),
     'L0_attn_gm': (1.0, 0.6),
     'L0_attn_bm': (0.0, 2.0),
     'L0_attn_b1m': (0.0, 0.8),
     'L0_attn_b2m': (0.0, 0.359)}
    factors = {'L0_attn_Wqkv_a': 8.0,
     'L0_attn_Wp_a': 8.0,
     'L0_attn_Wqkv_s': 8.0,
     'L0_attn_Wo_s': 8.0,
     'L0_attn_Wo': 4.077,
     'L0_ffn_attn_norm_w': 8.0,
     'L0_ffn_ffn_norm_w': 8.0,
     'L0_ffn_qkv_w': 6.905,
     'L0_ffn_qkv_b': 8.0,
     'L0_ffn_proj_w': 5.614,
     'L0_ffn_proj_b': 5.317,
     'L0_ffn_attn_sink': 8.0,
     'L0_ffn_gate_w': 8.0,
     'L0_ffn_gate_b': 8.0,
     'L0_ffn_W_up': 8.0,
     'L0_ffn_W_down': 8.0}
    for name, (base, spread) in spreads.items():
        noise = np.random.default_rng([zlib.crc32(name.encode()), seed]).standard_normal(out[name].shape)
        drawn = base * np.exp(spread * noise) if base else spread * noise
        out[name] = jnp.asarray(drawn.astype(out[name].dtype))
    for name, factor in factors.items():
        out[name] = (out[name] * factor).astype(out[name].dtype)
    return out
```

```python
from contextlib import ExitStack

import concourse.bass as bass
from concourse import mybir

F32 = mybir.dt.float32
BF16 = mybir.dt.bfloat16
F16 = mybir.dt.float16
I32 = mybir.dt.int32
U32 = mybir.dt.uint32
ALU = mybir.AluOpType
ACT = mybir.ActivationFunctionType
AX = mybir.AxisListType

P = 128
D = 128
NB, SEQ = 4, 512
BPS = SEQ // P
NBLK = NB * BPS
EPS = 1e-5

HEADS, KVH, DH = 16, 4, 64
QCH = HEADS // 2
NCH = QCH + KVH // 2
VW = DH + 1
PAIRS = HEADS // 2
NE, TOPK, DFF = 32, 4, 128
TILES = NBLK * TOPK + NE
AH, AE = 16, 8
AW = AE + 1
DM = 4 * D
KDUP = 4
LIN_ONE = 1.0001

ROWS = {}
_at = 0
for _name, _n in (("bv", KVH * DH), ("proj_b", D), ("gate_b", NE), ("sink", HEADS),
                  ("bk_s", D), ("bv_a", D), ("bv_s", D), ("bo", D), ("b2m", D)):
    ROWS[_name] = (_at, _at + _n)
    _at += _n
NROW = _at
COLS = {n: k for k, n in enumerate(
    ["attn_w", "ffn_w", "g1", "b1", "gm", "bm", "bp_a", "bo_s", "b1m0", "b1m1", "b1m2", "b1m3",
     "q_lo", "k_lo", "part"])}
NCOL = len(COLS)
CONST_F32 = {}
_at = 0
for _name, _n in (("ident", P), ("cos", SEQ), ("sin", SEQ), ("iota_e", NE), ("iota_s", P),
                  ("iota_t", TILES), ("cols", 3), ("token", NBLK), ("scan", NE * NBLK),
                  ("blockdiag", AH * AW), ("causal_t", P)):
    CONST_F32[_name] = (_at, _at + _n)
    _at += _n
NCONST = _at
CONST_BF = {"ident": (0, P), "before": (P, 2 * P), "ones": (2 * P, 3 * P),
            "band": (3 * P, 7 * P), "first": (7 * P, 9 * P), "band_x": (9 * P, 13 * P)}
NCONST_BF = 13 * P


class Shared:
    pass


def chained(eng, sem, start=0):
    count = [start]

    def link(ins):
        count[0] += 1
        ins.then_inc(sem, 1)
        eng.wait_ge(sem, count[0])

    link.count = count
    return link


def setup(nc, g, w, S):
    with ExitStack() as ctx:
        row = ctx.enter_context(nc.sbuf_tensor("rows_1", [1, NROW], F32))
        qkb = ctx.enter_context(nc.sbuf_tensor("qk_bias_row", [1, 2, NCH, P], F32))
        sink = ctx.enter_context(nc.sbuf_tensor("sink_row", [1, HEADS], F32))
        one = ctx.enter_context(nc.sbuf_tensor("ones_row", [1, P], F32))
        masks = ctx.enter_context(nc.sbuf_tensor("masks_f32", [P, NCONST_BF], F32))
        loaded = S("setup_loaded")
        made = S("setup_made")
        turned = S("setup_turned")
        spread = S("setup_spread")
        kept = S("setup_kept")
        n_dma = [0]

        def halves(t):
            half = KVH * DH
            return [(t[:, 0:4, 0:DH], 0), (t[:, 0:4, DH:P], half), (t[:, 4:8, 0:DH], 2 * half),
                    (t[:, 4:8, DH:P], 3 * half)]

        loads = [(g.const[:, :], w["const"]), (masks[:, :], w["const_bf"]),
                 (g.x[:, :, :], w["L0_attn_x"].rearrange("b (n p) d -> p (b n) d", p=P)),
                 (g.w_qk[:, QCH:NCH, :], w["L0_ffn_qkv_w"][:, HEADS * DH:(HEADS + KVH) * DH].rearrange("d (c e) -> d c e", e=P)),
                 (g.w_v[:, :], w["L0_ffn_qkv_w"][:, (HEADS + KVH) * DH:]),
                 (g.gate[:, :], w["L0_ffn_gate_w"])]
        for dst, at in halves(g.w_qk):
            loads.append((dst, w["L0_ffn_qkv_w"][:, at:at + 4 * DH].rearrange("d (c e) -> d c e", e=DH)))
        qb = w["L0_ffn_qkv_b"].rearrange("(o n) -> o n", o=1)
        for dst, at in halves(qkb[:, 0]):
            loads.append((dst, qb[:, at:at + 4 * DH].rearrange("d (c e) -> d c e", e=DH)))
        loads.append((qkb[:, 0, QCH:NCH, :], qb[:, HEADS * DH:(HEADS + KVH) * DH].rearrange("d (c e) -> d c e", e=P)))
        pw = w["L0_ffn_proj_w"]
        for dst, at in ((g.w_proj[0:DH, 0:4, :], 0), (g.w_proj[DH:P, 0:4, :], 256),
                        (g.w_proj[0:DH, 4:8, :], 512), (g.w_proj[DH:P, 4:8, :], 768)):
            loads.append((dst, pw[at:at + 256, :].rearrange("(c e) d -> e c d", e=DH)))

        def rowload(name, src):
            a, b = ROWS[name]
            loads.append((row[:, a:b], src.rearrange("(o n) -> o n", o=1)))

        rowload("bv", w["L0_ffn_qkv_b"][(HEADS + KVH) * DH:])
        rowload("proj_b", w["L0_ffn_proj_b"])
        rowload("gate_b", w["L0_ffn_gate_b"])
        rowload("bk_s", w["L0_attn_bqkv_s"][D:2 * D])
        rowload("bv_a", w["L0_attn_bqkv_a"][2 * D:])
        rowload("bv_s", w["L0_attn_bqkv_s"][2 * D:])
        rowload("bo", w["L0_attn_bo"])
        rowload("b2m", w["L0_attn_b2m"])
        loads.append((sink[:, :], w["L0_ffn_attn_sink"].rearrange("(o n) -> o n", o=1)))
        for name, src in (("attn_w", "L0_ffn_attn_norm_w"), ("ffn_w", "L0_ffn_ffn_norm_w"), ("g1", "L0_attn_g1"),
                          ("b1", "L0_attn_b1"), ("gm", "L0_attn_gm"), ("bm", "L0_attn_bm"),
                          ("bp_a", "L0_attn_bp_a"), ("bo_s", "L0_attn_bo_s")):
            loads.append((g.col[:, COLS[name]:COLS[name] + 1], w[src].rearrange("(p o) -> p o", o=1)))
        k = COLS["b1m0"]
        for j in range(DM // P):
            loads.append((g.col[:, k + j:k + j + 1], w["L0_attn_b1m"][j * P:(j + 1) * P].rearrange("(p o) -> p o", o=1)))
        for half in range(2):
            e0, e1 = half * NE // 2, (half + 1) * NE // 2
            loads.append((g.w_up[:, e0:e1, :], w["L0_ffn_W_up"][e0:e1].rearrange("e d f -> d e f")))
            loads.append((g.w_down[:, e0:e1, :], w["L0_ffn_W_down"][e0:e1].rearrange("e f d -> f e d")))
        total = 16 * len(loads)
        banks = g.bank

        with nc.Block() as block:
            @block.sync
            def _(sp):
                for dst, src in loads[0::2]:
                    sp.dma_start(dst, src).then_inc(loaded, 16)

            @block.scalar
            def _(act):
                for dst, src in loads[1::2]:
                    act.dma_start(dst, src).then_inc(loaded, 16)

            @block.gpsimd
            def _(pool):
                pool.memset(one[:, :], 1.0).then_inc(made, 1)

            @block.vector
            def _(dve):
                dve.wait_ge(loaded, total)
                link = chained(dve, turned)
                link(dve.tensor_copy(g.const_bf[:, :], masks[:, :]))
                link(dve.tensor_scalar(g.w_qk[:, 0:QCH, :], g.w_qk[:, 0:QCH, :], DH ** -0.5, None, ALU.mult))
                link(dve.tensor_scalar(qkb[:, 0, 0:QCH, :], qkb[:, 0, 0:QCH, :], DH ** -0.5, None, ALU.mult))
                for dst, src in ((g.w_rot, g.w_qk[:, :, :]), (qkb[:, 1], qkb[:, 0])):
                    d = (dst[:, :, :] if dst is g.w_rot else dst).rearrange("p c (e t) -> p c e t", t=2)
                    s = src.rearrange("p c (e t) -> p c e t", t=2)
                    link(dve.tensor_scalar(d[:, :, :, 0], s[:, :, :, 1], -1.0, None, ALU.mult))
                    link(dve.tensor_copy(d[:, :, :, 1], s[:, :, :, 0]))
                link(dve.tensor_copy(g.iota16[:, 0:TILES], g.const[:, CONST_F32["iota_t"][0]:CONST_F32["iota_t"][1]]))
                link(dve.tensor_copy(g.iota16[:, TILES:TILES + P], g.const[:, CONST_F32["iota_s"][0]:CONST_F32["iota_s"][1]]))
                a = ROWS["sink"][0]
                for half in range(2):
                    for up in range(2):
                        link(dve.tensor_copy(row[:, a + 8 * up + half:a + 8 * up + 8:2],
                                             sink[:, 8 * up + 4 * half:8 * up + 4 * half + 4]))
                dve.wait_ge(spread, 1)
                dve.tensor_copy(g.qk_bias[:, :], banks[0][:, 0:2 * NCH]).then_inc(kept, 1)
                for j in range(0, NROW, 512):
                    n = min(512, NROW - j)
                    dve.tensor_copy(g.row[:, j:j + n], banks[1 + j // 512][:, 0:n]).then_inc(kept, 1)
                dve.wait_ge(kept, 1 + (NROW + 511) // 512)
                a, b = ROWS["sink"]
                dve.tensor_scalar(g.neg_sink[:, :], g.row[:, a:b], -1.0, None, ALU.mult).then_inc(kept, 1)

            @block.tensor
            def _(pe):
                pe.wait_ge(loaded, total)
                pe.wait_ge(made, 1)
                pe.wait_ge(turned, 13)
                for v in range(2):
                    for c in range(NCH):
                        pe.matmul(banks[0][:, v * NCH + c:v * NCH + c + 1], qkb[:, v, c, :], one[:, 0:1], start=True, stop=True)
                for j in range(0, NROW, 512):
                    n = min(512, NROW - j)
                    last = pe.matmul(banks[1 + j // 512][:, 0:n], one[:, :], row[:, j:j + n], start=True, stop=True)
                last.then_inc(spread, 1)


def normalise(nc, g, S, tag, src, out, plus=None):
    st = g.stat
    with ExitStack():
        roots, v_ready, rooted = S(f"{tag}_norm_chain"), S(f"{tag}_norm_var"), S(f"{tag}_norm_sqrt")
        with nc.Block() as block:
            @block.vector
            def _(dve):
                link = chained(dve, roots)
                for i in range(NBLK):
                    last = dve.bn_stats(st.six[:, i, :], src[:, i, :])
                link(last)
                for i in range(NBLK):
                    last = dve.bn_aggr(st.mv[:, i, :], st.six[:, i, :])
                link(last)
                link(dve.tensor_copy(st.mean[:, :], st.mv[:, :, 0]))
                link(dve.tensor_scalar(st.v[:, :], st.mv[:, :, 1], EPS, None, ALU.add))

                def rsqrt(y, v, n):
                    dve.wait_ge(rooted, n)
                    link(dve.reciprocal(y, st.s[:, :]))
                    link(dve.tensor_tensor(st.t[:, :], y, y, ALU.mult))
                    link(dve.tensor_tensor(st.t[:, :], st.t[:, :], v, ALU.mult))
                    link(dve.tensor_scalar(st.t[:, :], st.t[:, :], -0.5, 1.5, ALU.mult, ALU.add))
                    link(dve.tensor_tensor(y, y, st.t[:, :], ALU.mult))

                rsqrt(st.r[:, :], st.v[:, :], 1)
                link(dve.tensor_tensor(st.v2[:, :], st.r[:, :], st.r[:, :], ALU.mult))
                link(dve.tensor_tensor(st.v2[:, :], st.v2[:, :], st.mv[:, :, 1], ALU.mult))
                link(dve.tensor_scalar(st.v2[:, :], st.v2[:, :], EPS, None, ALU.add))
                rsqrt(st.rr[:, :], st.v2[:, :], 2)
                link(dve.tensor_tensor(st.rr[:, :], st.rr[:, :], st.r[:, :], ALU.mult))
                for i in range(NBLK if out is not None else 0):
                    last = dve.tensor_scalar(out[:, i, :], src[:, i, :], st.mean[:, i:i + 1], st.r[:, i:i + 1],
                                             ALU.subtract, ALU.mult)
                if out is not None:
                    link(last)
                if plus is not None:
                    link(dve.tensor_tensor(out[:, :, :], out[:, :, :],
                                           plus.unsqueeze(1).broadcast_to([P, NBLK, D]), ALU.add))

            @block.scalar
            def _(act):
                act.wait_ge(roots, 4)
                act.activation(st.s[:, :], st.v[:, :], ACT.Sqrt).then_inc(rooted, 1)
                act.wait_ge(roots, 12)
                act.activation(st.s[:, :], st.v2[:, :], ACT.Sqrt).then_inc(rooted, 1)


def sink_attention(nc, g, S, tag):
    with ExitStack() as ctx:
        def sb(name, shape, dt=F32):
            return ctx.enter_context(nc.sbuf_tensor(f"{tag}_{name}", shape, dt))

        hn = sb("hn", [P, BPS, D])
        hT = sb("hT", [P, SEQ])
        qkT = sb("qkT", [P, NCH, SEQ])
        rope_a = sb("rope_a", [P, 2, SEQ])
        rope_b = sb("rope_b", [P, 2, SEQ])
        v = sb("v", [P, BPS, KVH, VW])
        probs = sb("probs", [P, 2, 2, 2 * P])
        probsT = sb("probsT", [P, 2, 4, P])
        neg = sb("neg_max", [P, BPS, HEADS])
        sinks = sb("sinks", [P, BPS, HEADS])
        den = sb("den", [P, 2, 4])
        y = sb("y", [P, 2, HEADS, DH])
        yT = sb("yT", [P, QCH, P])
        scores = g.bank[0:3]
        turned = g.bank[3:5]
        av = g.bank[5:7]
        misc = g.bank[7]
        c = g.c
        ident, ident_bf = c.ident, c.ident_bf
        NP = BPS * PAIRS

        normed, hT_turned, hT_ready = S(tag + "_normed"), S(tag + "_hT_turned"), S(tag + "_hT")
        qk_made, roped_parts, roped = S(tag + "_qk"), S(tag + "_rope_parts"), S(tag + "_roped")
        v_made, v_ready = S(tag + "_v_made"), S(tag + "_v")
        scored, maxed, probed = S(tag + "_scored"), S(tag + "_maxed"), S(tag + "_probs")
        p_turned, p_copied_a, p_copied_v = S(tag + "_p_turned"), S(tag + "_p_copied_a"), S(tag + "_p_copied_v")
        mixed, sink_sum, sinks_exp, y_ready = S(tag + "_mixed"), S(tag + "_sink_sum"), S(tag + "_sinks"), S(tag + "_y")
        y_turned, yT_ready, projected, added = S(tag + "_y_turned"), S(tag + "_yT"), S(tag + "_proj"), S(tag + "_added")
        chain, ones = S(tag + "_chain"), S(tag + "_ones")
        CHAIN = 65

        def keys(blk):
            return P if blk == 0 else 2 * P

        with nc.Block() as block:
            @block.vector
            def _(dve):
                dve.memset(v[:, :, :, DH:VW], 1.0).then_inc(ones, 1)
                with dve.Fori(0, NB) as b:
                    n_link = [0]

                    def link(ins):
                        n_link[0] += 1
                        ins.then_inc(chain, 1)
                        dve.wait_ge(chain, b * CHAIN + n_link[0])

                    blks = bass.DynSlice(b * BPS, BPS)
                    link(dve.tensor_tensor(hn[:, :, :], g.x[:, blks, :],
                                           g.stat.mean[:, blks].unsqueeze(2).broadcast_to([P, BPS, D]), ALU.subtract))
                    dve.tensor_tensor(hn[:, :, :], hn[:, :, :],
                                      g.stat.rr[:, blks].unsqueeze(2).broadcast_to([P, BPS, D]), ALU.mult).then_inc(normed, 1)
                    for k, ch in enumerate(range(NCH)):
                        dve.wait_ge(qk_made, b * NCH + k + 1)
                        if k >= 2:
                            dve.wait_ge(roped, b * NCH + k - 1)
                        ba, bb = (av, turned)[k % 2]
                        dve.scalar_tensor_tensor(rope_a[:, k % 2, :], ba[:, :], g.qk_bias[:, ch:ch + 1], c.cos,
                                                 ALU.add, ALU.mult)
                        dve.scalar_tensor_tensor(rope_b[:, k % 2, :], bb[:, :], g.qk_bias[:, NCH + ch:NCH + ch + 1], c.sin,
                                                 ALU.add, ALU.mult).then_inc(roped_parts, 1)
                        if k in (3, 5):
                            h = (k - 3) // 2
                            dve.wait_ge(v_made, b * 2 + h + 1)
                            vb = (misc, scores[2])[h]
                            for j in range(2):
                                last = dve.tensor_tensor(
                                    v[:, 2 * h + j, :, 0:DH], vb[:, j * KVH * DH:(j + 1) * KVH * DH].rearrange("p (h e) -> p h e", e=DH),
                                    c.row_bv.rearrange("p (h e) -> p h e", e=DH), ALU.add)
                            last.then_inc(v_ready, 1)

                    def row_max(n):
                        blk, pr = divmod(n, PAIRS)
                        k, half = divmod(pr, 2)
                        dve.wait_ge(scored, b * NP + n + 1)
                        w = keys(blk)
                        at = neg[:, blk, 4 * k + half:4 * k + 4:2]
                        link(dve.tensor_reduce(at, scores[n % 3][:, 0:2 * w].rearrange("p (h k) -> p h k", h=2),
                                               AX.X, ALU.max, negate=True))
                        dve.tensor_tensor(at, at, g.neg_sink[:, 4 * k + half:4 * k + 4:2], ALU.min).then_inc(maxed, 1)
                        if half:
                            dve.wait_ge(maxed, b * NP + n + 1)
                            dve.tensor_tensor(sinks[:, blk, 4 * k:4 * k + 4], neg[:, blk, 4 * k:4 * k + 4],
                                              g.neg_sink[:, 4 * k:4 * k + 4], ALU.subtract).then_inc(sink_sum, 1)

                    def copy_probs(n):
                        blk = n // PAIRS
                        dve.wait_ge(p_turned, b * NP + n + 1)
                        if n >= 2:
                            dve.wait_ge(mixed, b * NP + n - 1)
                        m = 2 * keys(blk)
                        dve.tensor_copy(probsT[:, n % 2, 0:m // P, :], turned[n % 2][:, 0:m].rearrange("p (j q) -> p j q", q=P)).then_inc(p_copied_v, 1)

                    def heads_out(m):
                        blk, k = divmod(m, PAIRS // 2)
                        dve.wait_ge(mixed, b * NP + 2 * m + 2)
                        dve.wait_ge(sinks_exp, b * NP // 2 + m + 1)
                        if k == 0 and blk >= 2:
                            dve.wait_ge(y_turned, b * 2 * BPS + 2 * (blk - 2) + 2)
                        a4 = av[m % 2][:, 0:4 * VW].rearrange("p (h e) -> p h e", e=VW)
                        d = den[:, m % 2, :]
                        link(dve.tensor_tensor(d, a4[:, :, DH], sinks[:, blk, 4 * k:4 * k + 4], ALU.add))
                        link(dve.reciprocal(d, d))
                        dve.tensor_tensor(y[:, blk % 2, 4 * k:4 * k + 4, :], a4[:, :, 0:DH],
                                          d.unsqueeze(2).broadcast_to([P, 4, DH]), ALU.mult).then_inc(y_ready, 1)

                    def add_proj(blk):
                        dve.wait_ge(projected, b * BPS + blk + 1)
                        at = g.u[:, bass.DynSlice(b * BPS + blk, 1), :].rearrange("p o d -> p (o d)")
                        dve.tensor_tensor(at, misc[:, 0:D], at, ALU.add).then_inc(added, 1)

                    row_max(0)
                    for n in range(NP + 8):
                        if n + 1 < NP:
                            row_max(n + 1)
                        if (n - 1) % 2 == 1 and 0 <= n - 1 < NP:
                            copy_probs(n - 1)
                        if n >= 3 and (n - 3) % 2 == 0 and (n - 3) // 2 < NP // 2:
                            heads_out((n - 3) // 2)
                        if n >= PAIRS + 6 and (n - PAIRS - 6) % PAIRS == 0 and (n - PAIRS - 6) // PAIRS < BPS:
                            add_proj((n - PAIRS - 6) // PAIRS)
                    assert n_link[0] == CHAIN, n_link[0]

            @block.gpsimd
            def _(pool):
                with pool.Fori(0, NB) as b:
                    for k in range(NCH):
                        pool.wait_ge(roped_parts, b * NCH + k + 1)
                        pool.tensor_tensor(qkT[:, k, :], rope_a[:, k % 2, :], rope_b[:, k % 2, :], ALU.add).then_inc(roped, 1)

            @block.scalar
            def _(act):
                with act.Fori(0, NB) as b:
                    act.wait_ge(hT_turned, b + 1)
                    act.activation(hT[:, :], misc[:, :], ACT.Copy, scale=c.col("attn_w")).then_inc(hT_ready, 1)

                    def exps(n):
                        blk, pr = divmod(n, PAIRS)
                        k, half = divmod(pr, 2)
                        act.wait_ge(maxed, b * NP + n + 1)
                        if n >= 2:
                            act.wait_ge(p_turned, b * NP + n - 1)
                        w = keys(blk)
                        for h in range(2):
                            col = 4 * k + half + 2 * h
                            last = act.activation(probs[:, n % 2, h, 0:w], scores[n % 3][:, h * w:(h + 1) * w], ACT.Exp,
                                                  bias=neg[:, blk, col:col + 1])
                        last.then_inc(probed, 1)
                        if half:
                            act.wait_ge(sink_sum, b * NP // 2 + n // 2 + 1)
                            at = sinks[:, blk, 4 * k:4 * k + 4]
                            act.activation(at, at, ACT.Exp).then_inc(sinks_exp, 1)

                    def copy_probs(n):
                        blk = n // PAIRS
                        act.wait_ge(p_turned, b * NP + n + 1)
                        if n >= 2:
                            act.wait_ge(mixed, b * NP + n - 1)
                        m = 2 * keys(blk)
                        act.activation(probsT[:, n % 2, 0:m // P, :], turned[n % 2][:, 0:m].rearrange("p (j q) -> p j q", q=P),
                                       ACT.Copy).then_inc(p_copied_a, 1)

                    def copy_y(j):
                        act.wait_ge(y_turned, b * 2 * BPS + j + 1)
                        if j % 2 == 0 and j >= 2:
                            act.wait_ge(projected, b * BPS + j // 2)
                        act.activation(yT[:, 4 * (j % 2):4 * (j % 2) + 4, :], misc[:, :].rearrange("p (j q) -> p j q", q=P),
                                       ACT.Copy).then_inc(yT_ready, 1)

                    for n in range(NP + 8):
                        if n < NP:
                            exps(n)
                        if (n - 1) % 2 == 0 and 0 <= n - 1 < NP:
                            copy_probs(n - 1)
                        m = n - PAIRS - 4
                        if m >= 0 and m % PAIRS < 2 and m // PAIRS < BPS:
                            copy_y(2 * (m // PAIRS) + m % PAIRS)

            @block.tensor
            def _(pe):
                pe.wait_ge(ones, 1)
                with pe.Fori(0, NB) as b:
                    pe.wait_ge(normed, b + 1)
                    for j in range(BPS):
                        last = pe.transpose(misc[:, j * P:(j + 1) * P], hn[:, j, :], ident)
                    last.then_inc(hT_turned, 1)
                    pe.wait_ge(hT_ready, b + 1)
                    for k in range(NCH):
                        if k >= 2:
                            pe.wait_ge(roped_parts, b * NCH + k - 1)
                        ba, bb = (av, turned)[k % 2]
                        pe.matmul(ba[:, :], g.w_qk[:, k, :], hT[:, :], start=True, stop=True)
                        pe.matmul(bb[:, :], g.w_rot[:, k, :], hT[:, :], start=True, stop=True).then_inc(qk_made, 1)
                        if k in (1, 2):
                            vb = (misc, scores[2])[k - 1]
                            for j in range(2):
                                blk = 2 * (k - 1) + j
                                last = pe.matmul(vb[:, j * KVH * DH:(j + 1) * KVH * DH], hT[:, blk * P:(blk + 1) * P],
                                                 g.w_v[:, :], start=True, stop=True)
                            last.then_inc(v_made, 1)

                    def score(n):
                        blk, pr = divmod(n, PAIRS)
                        k, half = divmod(pr, 2)
                        if n == 0:
                            pe.wait_ge(roped, b * NCH + NCH)
                            pe.wait_ge(v_ready, b * 2 + 2)
                        w = keys(blk)
                        bank = scores[n % 3]
                        mask = c.first if blk == 0 else c.band
                        pe.matmul(bank[:, 0:2 * w], ident_bf, mask, start=True, stop=False)
                        kch = QCH + (k >= 2)
                        lo = DH * half
                        for h in range(2):
                            last = pe.matmul(bank[:, h * w:(h + 1) * w], qkT[lo:lo + DH, 2 * k + h, blk * P:(blk + 1) * P],
                                             qkT[lo:lo + DH, kch, (blk + 1) * P - w:(blk + 1) * P], start=False, stop=h == 1)
                        last.then_inc(scored, 1)

                    def turn(n):
                        blk = n // PAIRS
                        pe.wait_ge(probed, b * NP + n + 1)
                        if n >= 2:
                            s = (p_copied_a, p_copied_v)[n % 2]
                            pe.wait_ge(s, b * NP // 2 + n // 2)
                        nk = keys(blk) // P
                        for h in range(2):
                            for j in range(nk):
                                at = (h * nk + j) * P
                                last = pe.transpose(turned[n % 2][:, at:at + P], probs[:, n % 2, h, j * P:(j + 1) * P], ident)
                        last.then_inc(p_turned, 1)

                    def mix(n):
                        blk, pr = divmod(n, PAIRS)
                        k, half = divmod(pr, 2)
                        m = n // 2
                        s = (p_copied_a, p_copied_v)[n % 2]
                        pe.wait_ge(s, b * NP // 2 + n // 2 + 1)
                        if half == 0 and m >= 2:
                            pe.wait_ge(y_ready, b * NP // 2 + m - 1)
                        nk = keys(blk) // P
                        kv = 2 * (k >= 2) + half
                        for h in range(2):
                            q = 2 * h + half
                            for j in range(nk):
                                last = pe.matmul(av[m % 2][:, q * VW:(q + 1) * VW], probsT[:, n % 2, h * nk + j, :],
                                                 v[:, blk - nk + 1 + j, kv, :], start=j == 0, stop=j == nk - 1)
                        last.then_inc(mixed, 1)

                    def turn_y(j):
                        blk = j // 2
                        if j % 2 == 0:
                            pe.wait_ge(y_ready, b * NP // 2 + (blk + 1) * PAIRS // 2)
                            if blk:
                                pe.wait_ge(added, b * BPS + blk)
                        else:
                            pe.wait_ge(yT_ready, b * 2 * BPS + j)
                        for q in range(4):
                            ch = 4 * (j % 2) + q
                            last = pe.transpose(misc[:, q * P:(q + 1) * P], y[:, blk % 2, 2 * ch:2 * ch + 2, :].rearrange("p h e -> p (h e)"), ident)
                        last.then_inc(y_turned, 1)

                    def project(blk):
                        pe.wait_ge(yT_ready, b * 2 * BPS + 2 * blk + 2)
                        for ch in range(QCH):
                            last = pe.matmul(misc[:, 0:D], yT[:, ch, :], g.w_proj[:, ch, :], start=ch == 0, stop=ch == QCH - 1)
                        last.then_inc(projected, 1)

                    for n in range(3):
                        score(n)
                    for n in range(NP + 8):
                        if n < NP:
                            turn(n)
                        if n + 3 < NP:
                            score(n + 3)
                        if 1 <= n <= NP:
                            mix(n - 1)
                        m = n - PAIRS - 3
                        if m >= 0 and m // PAIRS < BPS:
                            if m % PAIRS < 2:
                                turn_y(2 * (m // PAIRS) + m % PAIRS)
                            if m % PAIRS == 2:
                                project(m // PAIRS)
                    pe.wait_ge(added, b * BPS + BPS)


def route(nc, g, S, tag):
    c, r = g.c, g.routing
    with ExitStack() as ctx:
        def sb(name, shape, dt=F32):
            return ctx.enter_context(nc.sbuf_tensor(f"{tag}_{name}", shape, dt))

        hn = sb("rms_rows", [P, NBLK, D])
        hT = sb("rms_T", [P, NBLK * P])
        logit = sb("logits", [P, NBLK, NE])
        top = sb("top", [P, NBLK, 8])
        at8 = sb("top_at", [P, NBLK, 8], U32)
        at = sb("top_at_f", [P, NBLK, 8])
        picked = sb("picked", [P, TOPK, NBLK, NE])
        any16 = sb("picked_any", [P, NBLK, NE], BF16)
        any_a = sb("picked_a", [P, NBLK, NE])
        any_b = sb("picked_b", [P, NBLK, NE])
        e4 = sb("top_exp", [P, NBLK, TOPK])
        esum = sb("top_sum", [P, NBLK])
        count = sb("count", [P, NE, NBLK])
        upto = sb("count_upto", [P, NE, NBLK])
        slot_of = sb("slot_of", [P, NBLK, NE])
        work = sb("work", [P, NBLK, NE])
        ntile_i = sb("ntile_i", [P, NE], I32)
        ntile = sb("ntile", [P, NE])
        tile_end = sb("tile_end", [P, NE])
        base = sb("base", [P, NE])
        slot_f = sb("slot_f", [P, NBLK, TOPK])
        hi_i, lo_i = sb("slot_hi_i", [P, NBLK * TOPK], I32), sb("slot_lo_i", [P, NBLK * TOPK], I32)
        hi, lo = sb("slot_hi", [P, NBLK * TOPK]), sb("slot_lo", [P, NBLK * TOPK])
        RING = 8
        in_tile = sb("in_tile", [P, RING, P], F16)
        of_tile = sb("of_tile", [P, RING, TILES], F16)
        le = sb("ended", [P, NE])
        owner = sb("owner", [P, 1])
        square = sb("square", [P, D])

        chain, squared, rooted = S(tag + "_r_chain"), S(tag + "_r_squared"), S(tag + "_r_sqrt")
        rows_ready, rows_out, turned, hT_ready = (S(tag + "_r_" + n) for n in ("rows", "rows_out", "turned", "hT"))
        gated, chosen, counted, exped = (S(tag + "_r_" + n) for n in ("gated", "chosen", "counted", "exp"))
        hot, mapped, owned, owner_row = (S(tag + "_r_" + n) for n in ("hot", "mapped", "owned", "owner"))
        marks = {}

        with nc.Block() as block:
            @block.scalar
            def _(act):
                for i in range(NBLK):
                    if i:
                        act.wait_ge(squared, i)
                    act.activation(square[:, :], g.u[:, i, :], ACT.Square, accum_out=g.stat.v2[:, i:i + 1]).then_inc(squared, 1)
                act.wait_ge(chain, 1)
                act.activation(g.stat.s[:, :], g.stat.v[:, :], ACT.Sqrt).then_inc(rooted, 1)
                for q in range(4):
                    act.wait_ge(turned, q + 1)
                    act.activation(hT[:, q * 512:(q + 1) * 512], g.bank[q][:, :], ACT.Copy, scale=c.col("ffn_w")).then_inc(hT_ready, 1)
                act.wait_ge(exped, 1)
                act.activation(e4[:, :, :], e4[:, :, :], ACT.Exp).then_inc(exped, 1)

            @block.sync
            def _(sp):
                for q in range(4):
                    sp.wait_ge(rows_ready, q + 1)
                    sp.dma_start(g.rows_dram.rearrange("(i p) d -> p i d", p=P)[:, 4 * q:4 * q + 4, :],
                                 hn[:, 4 * q:4 * q + 4, :]).then_inc(rows_out, 16)
                sp.wait_ge(rows_out, 64)

            @block.tensor
            def _(pe):
                for q in range(4):
                    pe.wait_ge(rows_ready, q + 1)
                    for j in range(4):
                        last = pe.transpose(g.bank[q][:, j * P:(j + 1) * P], hn[:, 4 * q + j, :], c.ident)
                    last.then_inc(turned, 1)
                for i in range(NBLK):
                    if i % 4 == 0:
                        pe.wait_ge(hT_ready, i // 4 + 1)
                    last = pe.matmul(g.bank[4][:, i * NE:(i + 1) * NE], hT[:, i * P:(i + 1) * P], g.gate[:, :], start=True, stop=True)
                last.then_inc(gated, 1)
                pe.wait_ge(chosen, 1)
                flat = any16[:, :, :].rearrange("p i e -> p (i e)")
                pe.matmul(g.bank[5][:, :], c.h("ones"), flat, start=True, stop=True).then_inc(counted, 1)
                pe.matmul(g.bank[6][:, :], c.h("before"), flat, start=True, stop=True).then_inc(counted, 1)
                for m in range(NBLK * TOPK):
                    pe.wait_ge(hot, m + 1)
                    pe.matmul(g.bank[7][:, 0:TILES], in_tile[:, m % RING, :], of_tile[:, m % RING, :],
                              start=m == 0, stop=m == NBLK * TOPK - 1).then_inc(mapped, 1)
                pe.wait_ge(owned, 1)
                pe.matmul(g.bank[0][0:1, 0:P], owner[:, :], c.ident, start=True, stop=True).then_inc(owner_row, 1)

            @block.vector
            def _(dve):
                link = chained(dve, chain)
                st = g.stat
                dve.wait_ge(squared, NBLK)
                link(dve.tensor_scalar(st.v[:, :], st.v2[:, :], 1.0 / D, EPS, ALU.mult, ALU.add))
                dve.wait_ge(rooted, 1)
                y = st.r[:, :]
                link(dve.reciprocal(y, st.s[:, :]))
                link(dve.tensor_tensor(st.t[:, :], y, y, ALU.mult))
                link(dve.tensor_tensor(st.t[:, :], st.t[:, :], st.v[:, :], ALU.mult))
                link(dve.tensor_scalar(st.t[:, :], st.t[:, :], -0.5, 1.5, ALU.mult, ALU.add))
                link(dve.tensor_tensor(y, y, st.t[:, :], ALU.mult))
                for i in range(NBLK):
                    last = dve.tensor_scalar(hn[:, i, :], g.u[:, i, :], st.r[:, i:i + 1], None, ALU.mult)
                    if i % 4 == 3:
                        last.then_inc(rows_ready, 1)
                dve.wait_ge(gated, 1)
                link(dve.tensor_tensor(logit[:, :, :], g.bank[4][:, :].rearrange("p (i e) -> p i e", e=NE),
                                       c.row("gate_b").unsqueeze(1).broadcast_to([P, NBLK, NE]), ALU.add))
                for i in range(NBLK):
                    last = dve.max(top[:, i, :], logit[:, i, :])
                link(last)
                for i in range(NBLK):
                    last = dve.max_index(at8[:, i, :], top[:, i, :], logit[:, i, :])
                link(last)
                dve.tensor_tensor(e4[:, :, :], top[:, :, 0:TOPK], top[:, :, 0:1].broadcast_to([P, NBLK, TOPK]), ALU.subtract).then_inc(exped, 1)
                link(dve.tensor_copy(at[:, :, :], at8[:, :, :]))
                iota = c.f("iota_e").unsqueeze(1).broadcast_to([P, NBLK, NE])
                for k in range(TOPK):
                    last = dve.tensor_tensor(picked[:, k], iota, at[:, :, k:k + 1].broadcast_to([P, NBLK, NE]), ALU.is_equal)
                link(last)
                dve.tensor_tensor(any_a[:, :, :], picked[:, 0], picked[:, 1], ALU.add)
                link(dve.tensor_tensor(any_b[:, :, :], picked[:, 2], picked[:, 3], ALU.add))
                dve.tensor_tensor(any16[:, :, :], any_a[:, :, :], any_b[:, :, :], ALU.add).then_inc(chosen, 1)
                dve.wait_ge(exped, 2)
                link(dve.tensor_reduce(esum[:, :], e4[:, :, :], AX.X, ALU.add))
                link(dve.reciprocal(esum[:, :], esum[:, :]))
                link(dve.tensor_scalar(esum[:, :], esum[:, :], 0.5, None, ALU.mult))
                link(dve.tensor_tensor(r.weight[:, :].rearrange("p (i k) -> p i k", k=TOPK), e4[:, :, :],
                                       esum[:, :].unsqueeze(2).broadcast_to([P, NBLK, TOPK]), ALU.mult))
                dve.wait_ge(counted, 1)
                link(dve.tensor_copy(count[:, :, :].rearrange("p e i -> p i e"), g.bank[5][:, :].rearrange("p (i e) -> p i e", e=NE)))
                flat = lambda t: t[:, :, :].rearrange("p e i -> p (e i)")
                link(dve.tensor_tensor_scan(flat(upto), c.f("scan"), flat(count), 0.0, ALU.mult, ALU.add))
                link(dve.tensor_scalar(ntile_i[:, :], upto[:, :, NBLK - 1], float(P - 1), None, ALU.add))
                link(dve.tensor_scalar(ntile_i[:, :], ntile_i[:, :], 7, None, ALU.arith_shift_right))
                link(dve.tensor_copy(ntile[:, :], ntile_i[:, :]))
                link(dve.tensor_tensor_scan(tile_end[:, :], c.f("iota_t")[:, 1:2].broadcast_to([P, NE]), ntile[:, :], 0.0, ALU.mult, ALU.add))
                link(dve.tensor_tensor(base[:, :], tile_end[:, :], ntile[:, :], ALU.subtract))
                link(dve.tensor_scalar(base[:, :], base[:, :], float(P), None, ALU.mult))
                link(dve.tensor_tensor(flat(upto), flat(upto), flat(count), ALU.subtract))
                dve.wait_ge(counted, 2)
                link(dve.tensor_tensor(slot_of[:, :, :], g.bank[6][:, :].rearrange("p (i e) -> p i e", e=NE),
                                       upto[:, :, :].rearrange("p e i -> p i e"), ALU.add))
                link(dve.tensor_tensor(slot_of[:, :, :], slot_of[:, :, :], base[:, :].unsqueeze(1).broadcast_to([P, NBLK, NE]), ALU.add))
                for k in range(TOPK):
                    link(dve.tensor_tensor(work[:, :, :], picked[:, k], slot_of[:, :, :], ALU.mult))
                    link(dve.tensor_reduce(slot_f[:, :, k:k + 1].rearrange("p i o -> p (i o)"), work[:, :, :], AX.X, ALU.add))
                link(dve.tensor_scalar(le[:, :], tile_end[:, :], c.f("cols")[:, 0:1], None, ALU.is_le))
                link(dve.tensor_reduce(owner[:, :], le[:, :], AX.X, ALU.add))
                dve.tensor_scalar(owner[:, :], owner[:, :], float(NE - 1), None, ALU.min).then_inc(owned, 1)
                link(dve.tensor_copy(r.slot[:, :], slot_f[:, :, :].rearrange("p i k -> p (i k)")))
                si = r.slot[:, :].bitcast(I32)
                dve.tensor_scalar(hi_i[:, :], si, 7, None, ALU.arith_shift_right)
                link(dve.tensor_scalar(lo_i[:, :], si, P - 1, None, ALU.bitwise_and))
                dve.tensor_copy(hi[:, :], hi_i[:, :])
                link(dve.tensor_copy(lo[:, :], lo_i[:, :]))
                for m in range(NBLK * TOPK):
                    i = m // TOPK
                    if m >= RING:
                        dve.wait_ge(mapped, m - RING + 1)
                    dve.tensor_scalar(of_tile[:, m % RING, :], c.iota_t16, hi[:, m:m + 1], c.f("token")[:, i:i + 1], ALU.is_equal, ALU.mult)
                    dve.tensor_scalar(in_tile[:, m % RING, :], c.iota_s16, lo[:, m:m + 1], None, ALU.is_equal).then_inc(hot, 1)
                dve.wait_ge(owner_row, 1)
                dve.tensor_copy(r.owner[:, :], g.bank[0][0:1, 0:P])
                dve.wait_ge(mapped, NBLK * TOPK)
                dve.tensor_copy(r.token[:, :], g.bank[7][:, 0:TILES])


def experts(nc, g, S, tag, before):
    c, r = g.c, g.routing
    U = 8
    DEPTH = 3
    TURNS = TILES // U - 1
    gathered_before = before * TILES // U * 16
    with ExitStack() as ctx:
        def sb(name, shape, dt=F32):
            return ctx.enter_context(nc.sbuf_tensor(f"{tag}_{name}", shape, dt))

        idx = sb("tile_tokens", [P, U], U32)
        fence = sb("tile_fence", [1, 1])
        rows = sb("tile_rows", [P, U, D])
        rowsT = sb("tile_rowsT", [P, 2, P])
        silu = sb("tile_silu", [P, 2, DFF])
        act_rows = sb("tile_act", [P, 2, DFF])
        actT = sb("tile_actT", [P, 2, P])
        y = sb("tile_y", [P, U, D])
        b_rows, b_up, b_act, b_y = g.bank[0:2], g.bank[2:4], g.bank[4:6], g.bank[6:8]
        idx_ready = S(tag + "_e_idx")
        gathered = [S(f"{tag}_e_gathered{j}") for j in range(U)]
        stored = [S(f"{tag}_e_stored{j}") for j in range(U)]
        x_turned, x_ready, upped, silued = (S(tag + "_e_" + n) for n in ("x_turned", "x", "upped", "silu"))
        acted, a_turned, a_ready, downed, y_ready = (S(tag + "_e_" + n) for n in ("acted", "a_turned", "a", "downed", "y"))

        def over_steps(eng, step):
            for s in range(DEPTH + U):
                step(s, s % U, s // U, lambda k, s=s: s - k >= 0)
            with eng.Fori(1, TURNS) as t:
                for j in range(U):
                    step(t * U + (DEPTH + j), (DEPTH + j) % U, t + (DEPTH + j) // U, lambda k: True)
            for s in range(DEPTH + TURNS * U, TILES + DEPTH):
                step(s, s % U, s // U, lambda k, s=s: s - k < TILES)

        with nc.Block() as block:
            @block.gpsimd
            def _(pool):
                def gathers(t, first):
                    for q in range(2):
                        for j in range(4 * q, 4 * q + 4):
                            if not first:
                                pool.wait_ge(gathered[j], t * 16 + gathered_before)
                        pool.tensor_copy(idx[:, 4 * q:4 * q + 4], r.token[:, bass.DynSlice(t * U + 4 * q, 4)]).then_inc(idx_ready, 1)
                        if not first:
                            pool.wait_ge(x_turned, t * U - U + 4 * q + 4)
                        pool.wait_ge(idx_ready, t * 4 + 2 * q + 2)
                        pool.tensor_tensor(fence[:, :], fence[:, :], fence[:, :], ALU.add).then_inc(idx_ready, 1)
                        for j in range(4 * q, 4 * q + 4):
                            pool.indirect_dma_start(out=rows[:, j, :], out_offset=None, in_=g.rows_dram,
                                                    in_offset=bass.IndirectOffsetOnAxis(ap=idx[:, j:j + 1], axis=0)).then_inc(gathered[j], 16)

                pool.memset(fence[:, :], 0.0).then_inc(idx_ready, 1)
                gathers(0, True)
                with pool.Fori(1, TILES // U) as t:
                    gathers(t, False)

            @block.tensor
            def _(pe):
                def step(s, r8, q, on):
                    if on(1):
                        e_up = pe.value_load(r.owner[0:1, bass.DynSlice(s - 1, 1)], min_val=0, max_val=NE - 1)
                    if on(3):
                        e_down = pe.value_load(r.owner[0:1, bass.DynSlice(s - 3, 1)], min_val=0, max_val=NE - 1)
                    if on(0):
                        pe.wait_ge(gathered[r8], q * 16 + 16 + gathered_before)
                        if not (isinstance(s, int) and s < 2):
                            pe.wait_ge(x_ready, s - 1)
                        pe.transpose(b_rows[r8 % 2][:, 0:P], rows[:, r8, :], c.ident).then_inc(x_turned, 1)
                    if on(1):
                        pe.wait_ge(x_ready, s)
                        if not (isinstance(s, int) and s < 3):
                            pe.wait_ge(acted, s - 2)
                        up = g.w_up[:, bass.DynSlice(e_up, 1), :].rearrange("p o f -> p (o f)")
                        pe.matmul(b_up[(r8 - 1) % 2][:, 0:2 * DFF], rowsT[:, (r8 - 1) % 2, :], up, start=True, stop=True).then_inc(upped, 1)
                    if on(2):
                        pe.wait_ge(acted, s - 1)
                        if not (isinstance(s, int) and s < 4):
                            pe.wait_ge(a_ready, s - 3)
                        pe.transpose(b_act[r8 % 2][:, 0:P], act_rows[:, r8 % 2, :], c.ident).then_inc(a_turned, 1)
                    if on(3):
                        pe.wait_ge(a_ready, s - 2)
                        if not (isinstance(s, int) and s < 5):
                            pe.wait_ge(y_ready, s - 4)
                        down = g.w_down[:, bass.DynSlice(e_down, 1), :].rearrange("p o f -> p (o f)")
                        pe.matmul(b_y[(r8 - 3) % 2][:, 0:D], actT[:, (r8 - 3) % 2, :], down, start=True, stop=True).then_inc(downed, 1)

                over_steps(pe, step)

            @block.scalar
            def _(act):
                def step(s, r8, q, on):
                    if on(0):
                        act.wait_ge(x_turned, s + 1)
                        if not (isinstance(s, int) and s < 2):
                            act.wait_ge(upped, s - 1)
                        act.activation(rowsT[:, r8 % 2, :], b_rows[r8 % 2][:, 0:P], ACT.Copy, scale=c.col("ffn_w")).then_inc(x_ready, 1)
                    if on(1):
                        act.wait_ge(upped, s)
                        if not (isinstance(s, int) and s < 3):
                            act.wait_ge(acted, s - 2)
                        act.activation(silu[:, (r8 - 1) % 2, :], b_up[(r8 - 1) % 2][:, DFF:2 * DFF], ACT.Silu).then_inc(silued, 1)

                over_steps(act, step)

            @block.vector
            def _(dve):
                def step(s, r8, q, on):
                    if on(1):
                        dve.wait_ge(silued, s)
                        if not (isinstance(s, int) and s < 3):
                            dve.wait_ge(a_turned, s - 2)
                        k = (r8 - 1) % 2
                        dve.tensor_tensor(act_rows[:, k, :], b_up[k][:, 0:DFF], silu[:, k, :], ALU.mult).then_inc(acted, 1)
                    if on(2):
                        dve.wait_ge(a_turned, s - 1)
                        if not (isinstance(s, int) and s < 4):
                            dve.wait_ge(downed, s - 3)
                        dve.tensor_copy(actT[:, r8 % 2, :], b_act[r8 % 2][:, 0:P]).then_inc(a_ready, 1)
                    if on(3):
                        dve.wait_ge(downed, s - 2)
                        if not (isinstance(s, int) and s - 3 < U):
                            dve.wait_ge(stored[(r8 - 3) % U], (q if r8 >= 3 else q - 1) * 16)
                        dve.tensor_copy(y[:, (r8 - 3) % U, :], b_y[(r8 - 3) % 2][:, 0:D]).then_inc(y_ready, 1)

                over_steps(dve, step)

            @block.sync
            def _(sp):
                with sp.Fori(0, TILES // U) as t:
                    for j in range(U):
                        sp.wait_ge(y_ready, t * U + j + 1)
                        sp.dma_start(g.y_dram[bass.DynSlice((t * U + j) * P, P), :], y[:, j, :]).then_inc(stored[j], 16)
                for j in range(U):
                    sp.wait_ge(stored[j], TILES // U * 16)


def combine(nc, g, S, tag, before):
    r = g.routing
    with ExitStack() as ctx:
        def sb(name, shape, dt=F32):
            return ctx.enter_context(nc.sbuf_tensor(f"{tag}_{name}", shape, dt))

        BLKS = 2
        N = BLKS * TOPK
        fetched_before = before * NBLK // BLKS * 16
        idx = sb("c_slots", [P, N], U32)
        fence = sb("c_fence", [1, 1])
        rows = sb("c_rows", [P, N, D])
        weight = sb("c_weight", [P, N])
        idx_ready, added, started = (S(tag + "_c_" + n) for n in ("idx", "added", "started"))
        fetched = [S(f"{tag}_c_fetched{j}") for j in range(N)]

        with nc.Block() as block:
            @block.gpsimd
            def _(pool):
                def turn(t, first):
                    for q in range(BLKS):
                        if not first:
                            pool.wait_ge(added, t * N - N + TOPK * (q + 1))
                        pool.tensor_copy(idx[:, TOPK * q:TOPK * (q + 1)], r.slot[:, bass.DynSlice(t * N + TOPK * q, TOPK)]).then_inc(idx_ready, 1)
                        pool.wait_ge(idx_ready, t * 2 * BLKS + 2 * q + 2)
                        pool.tensor_tensor(fence[:, :], fence[:, :], fence[:, :], ALU.add).then_inc(idx_ready, 1)
                        for j in range(TOPK * q, TOPK * (q + 1)):
                            pool.indirect_dma_start(out=rows[:, j, :], out_offset=None, in_=g.y_dram,
                                                    in_offset=bass.IndirectOffsetOnAxis(ap=idx[:, j:j + 1], axis=0)).then_inc(fetched[j], 16)

                pool.memset(fence[:, :], 0.0).then_inc(idx_ready, 1)
                turn(0, True)
                with pool.Fori(1, NBLK // BLKS) as t:
                    turn(t, False)

            @block.vector
            def _(dve):
                dve.scalar_tensor_tensor(g.x[:, :, :].rearrange("p i d -> p (i d)"), g.u[:, :, :].rearrange("p i d -> p (i d)"), 0.5,
                                         g.x[:, :, :].rearrange("p i d -> p (i d)"), ALU.mult, ALU.add).then_inc(started, 1)
                dve.wait_ge(started, 1)
                with dve.Fori(0, NBLK // BLKS) as t:
                    for j in range(N):
                        dve.wait_ge(fetched[j], t * 16 + 16 + fetched_before)
                        at = g.x[:, bass.DynSlice(t * BLKS + j // TOPK, 1), :].rearrange("p o d -> p (o d)")
                        dve.scalar_tensor_tensor(at, rows[:, j, :], r.weight[:, bass.DynSlice(t * N + j, 1)], at, ALU.mult, ALU.add).then_inc(added, 1)
                        dve.wait_ge(added, t * N + j + 1)


def setup_attention(nc, g, w, S):
    with ExitStack() as ctx:
        wa = ctx.enter_context(nc.sbuf_tensor("l_wqkv_a", [P, 3 * D], F32))
        ws = ctx.enter_context(nc.sbuf_tensor("l_wqkv_s", [P, 3 * D], F32))
        rows = ctx.enter_context(nc.sbuf_tensor("l_bias_rows", [1, 4, D], F32))
        wide = ctx.enter_context(nc.sbuf_tensor("l_bias_wide", [1, 17, P], F32))
        one = ctx.enter_context(nc.sbuf_tensor("l_one", [1, 1], F32))
        loaded, chain, made, spread, kept = (S("l_setup_" + n) for n in ("loaded", "chain", "made", "spread", "kept"))
        loads = [(wa[:, :], w["L0_attn_Wqkv_a"]), (ws[:, :], w["L0_attn_Wqkv_s"]), (g.w_p[:, :], w["L0_attn_Wp_a"]),
                 (g.w_os[:, :], w["L0_attn_Wo_s"]), (g.w_o[:, :], w["L0_attn_Wo"]), (g.w1[:, :], w["L0_attn_W1"]),
                 (g.w2[:, :, :], w["L0_attn_W2"].rearrange("(c f) d -> f c d", f=P))]
        for k, (name, at) in enumerate((("L0_attn_bqkv_a", 0), ("L0_attn_bqkv_a", D), ("L0_attn_bqkv_s", 0), ("L0_attn_bqkv_s", D))):
            loads.append((rows[:, k, :], w[name][at:at + D].rearrange("(o n) -> o n", o=1)))

        with nc.Block() as block:
            @block.sync
            def _(sp):
                for dst, src in loads:
                    sp.dma_start(dst, src).then_inc(loaded, 16)

            @block.vector
            def _(dve):
                dve.wait_ge(loaded, 16 * len(loads))
                link = chained(dve, chain)
                link(dve.memset(one[:, :], 1.0))
                link(dve.tensor_scalar(wa[:, 0:D], wa[:, 0:D], AE ** -0.5, None, ALU.mult))
                link(dve.tensor_scalar(ws[:, 0:D], ws[:, 0:D], AE ** -0.5, None, ALU.mult))
                link(dve.tensor_scalar(rows[:, 0:3:2, :], rows[:, 0:3:2, :], AE ** -0.5, None, ALU.mult))
                for k, (src, at) in enumerate(((wa, 0), (wa, D), (ws, 0), (ws, D))):
                    for t in range(KDUP):
                        dst = g.w_dup[:, k, :].rearrange("p (h t e) -> p h t e", t=KDUP, e=AE)
                        last = dve.tensor_copy(dst[:, :, t, :], src[:, at:at + D].rearrange("p (h e) -> p h e", e=AE))
                        dst = wide[:, 4 * k:4 * k + 4, :].rearrange("p c (h t e) -> p (c h) t e", t=KDUP, e=AE)
                        last = dve.tensor_copy(dst[:, :, t, :], rows[:, k, :].rearrange("p (h e) -> p h e", e=AE))
                dve.tensor_copy(wide[:, 16, :], rows[:, 2, :])
                dve.tensor_copy(g.w_qs[:, :], ws[:, 0:D])
                dve.tensor_copy(g.w_tok[:, 0:D], ws[:, D:2 * D])
                dve.tensor_copy(g.w_tok[:, D:2 * D], wa[:, 2 * D:])
                link(dve.tensor_copy(g.w_tok[:, 2 * D:], ws[:, 2 * D:]))
                link(dve.tensor_tensor(g.col[:, COLS["bp_a"]:COLS["bp_a"] + 1], g.c.col("bp_a"), g.c.col("bo_s"), ALU.add))
                dve.sem_inc(made, 1)
                dve.wait_ge(spread, 1)
                link(dve.tensor_copy(g.dup_bias[:, 0:17], g.bank[0][:, 0:17]))
                dve.tensor_scalar(g.dup_bias[:, 17:34], g.dup_bias[:, 0:17], LIN_ONE - 1.0, None, ALU.add).then_inc(kept, 1)

            @block.tensor
            def _(pe):
                pe.wait_ge(made, 1)
                for k in range(17):
                    last = pe.matmul(g.bank[0][:, k:k + 1], wide[:, k, :], one[:, :], start=True, stop=True)
                last.then_inc(spread, 1)


def window_and_linear(nc, g, S):
    with ExitStack() as ctx:
        def sb(name, shape, dt=F32):
            return ctx.enter_context(nc.sbuf_tensor("l_" + name, shape, dt))

        QA, KA, QS, KS = range(4)
        NCK = 4
        hn = sb("hn", [P, BPS, D])
        xT = sb("xT", [P, SEQ])
        dup = sb("dup", [P, 4, NCK, SEQ], F16)
        whole = sb("whole", [P, 2, SEQ])
        high = sb("high", [P, 2, SEQ], F16)
        raised = sb("raised", [P, 2, SEQ])
        floor = sb("floor", [P, 2, SEQ])
        qcT = sb("qcT", [P, SEQ])
        ktok = sb("ktok", [P, BPS, D])
        kz = sb("kz", [P, BPS, D])
        ke = sb("ke", [P, BPS, D])
        kf = sb("kf", [P, 2, D])
        va = sb("va", [P, BPS, AH, AW])
        vs = sb("vs", [P, BPS, AH, AW])
        state = sb("state", [P, BPS - 1, AH * AW])
        probs = sb("probs", [P, 2, 2, 2 * P])
        probsT = sb("probsT", [P, 2, 4, P])
        linT = sb("linT", [P, 2, 4, P])
        neg = sb("neg_max", [P, BPS, PAIRS, 2])
        den = sb("den", [P, 2, AH])
        yy = sb("yy", [P, 2, 2, D])
        yT = sb("yT", [P, 2, P])
        mT = sb("mT", [P, P])
        scores, turned = g.bank[0:2], g.bank[2:4]
        lin_bank, win_out, lin_out, misc = g.bank[4:8]
        zbank = (turned[0], turned[1], lin_bank, win_out)
        tbank = (scores[0], scores[1], lin_out, misc)
        c = g.c
        NP, NQ, NZ, NS = BPS * PAIRS, BPS * 4, 17, 16
        ones, normed, x_turned, x_ready = (S("l_" + n) for n in ("ones", "normed", "x_turned", "x"))
        z_made, z_copied, z_used, q_made = (S("l_" + n) for n in ("z_made", "z_copied", "z_used", "q_made"))
        high_made, dup_made = S("l_high"), S("l_dup")
        t_made, t_biased, k_exped, t_ready = (S("l_" + n) for n in ("t_made", "t_biased", "k_exped", "t_ready"))
        st_made, st_ready = S("l_st_made"), S("l_st")
        scored, maxed, probed, p_turned = (S("l_" + n) for n in ("scored", "maxed", "probs", "p_turned"))
        p_copied_a, p_copied_v, mixed = (S("l_" + n) for n in ("p_copied_a", "p_copied_v", "mixed"))
        l_scored, l_masked, l_mixed, l_out, w_out = (S("l_" + n) for n in ("l_scored", "l_masked", "l_mixed", "l_out", "w_out"))
        y_turned, yT_ready, m_made, m_ready, projected, added = (
            S("l_" + n) for n in ("y_turned", "yT", "m_made", "m", "projected", "added"))
        chain = S("l_chain")
        CHAIN = 17

        def keys(blk):
            return P if blk == 0 else 2 * P

        def pair_heads(pr):
            j, up = pr % 4, pr // 4
            return j, 2 * up, (8 * up + j, 8 * up + 4 + j)

        with nc.Block() as block:
            @block.vector
            def _(dve):
                dve.memset(va[:, :, :, AE:AW], 1.0).then_inc(ones, 1)
                dve.memset(vs[:, :, :, AE:AW], 1.0).then_inc(ones, 1)
                with dve.Fori(0, NB) as b:
                    n_link = [0]

                    def link(ins):
                        n_link[0] += 1
                        ins.then_inc(chain, 1)
                        dve.wait_ge(chain, b * CHAIN + n_link[0])

                    blks = bass.DynSlice(b * BPS, BPS)
                    link(dve.tensor_tensor(hn[:, :, :], g.x[:, blks, :],
                                           g.stat.mean[:, blks].unsqueeze(2).broadcast_to([P, BPS, D]), ALU.subtract))
                    dve.tensor_tensor(hn[:, :, :], hn[:, :, :],
                                      g.stat.rr[:, blks].unsqueeze(2).broadcast_to([P, BPS, D]), ALU.mult).then_inc(normed, 1)

                    def split(k):
                        dve.wait_ge(high_made, b * NS + k + 1)
                        if k < 2 * NCK:
                            dve.wait_ge(z_copied, b * NZ + k + 1)
                        kind, ck = divmod(k, NCK)
                        sign = c.f("cols")[:, 1:2] if kind in (QA, QS) else c.f("cols")[:, 2:3]
                        dve.scalar_tensor_tensor(dup[:, kind, ck, :], high[:, k % 2, :], sign, whole[:, k % 2, :],
                                                 ALU.mult, ALU.add).then_inc(dup_made, 1)

                    def token_rows(blk):
                        dve.wait_ge(t_made, b * BPS + blk + 1)
                        a = ROWS["bk_s"][0]
                        bank = tbank[blk]
                        for k, dst in ((1, va), (2, vs)):
                            dve.tensor_tensor(dst[:, blk, :, 0:AE], bank[:, k * D:(k + 1) * D].rearrange("p (h e) -> p h e", e=AE),
                                              g.row[:, a + k * D:a + (k + 1) * D].rearrange("p (h e) -> p h e", e=AE), ALU.add)
                        dve.tensor_tensor(kz[:, blk, :], bank[:, 0:D], g.row[:, a:a + D], ALU.add).then_inc(t_biased, 1)

                    def token_keys(blk):
                        dve.wait_ge(k_exped, b * BPS + blk + 1)
                        i = blk % 2
                        link(dve.tensor_scalar(kf[:, i, :], kz[:, blk, :], LIN_ONE - 1.0, LIN_ONE - 1.0, ALU.add, ALU.max))
                        dve.scalar_tensor_tensor(ktok[:, blk, :], ke[:, blk, :], 1.0, kf[:, i, :], ALU.min, ALU.add).then_inc(t_ready, 1)

                    for k in range(NZ):
                        if k >= 2 * NCK:
                            dve.wait_ge(z_copied, b * NZ + k + 1)
                            i = k % 2
                            dve.tensor_scalar(floor[:, i, :], zbank[k % 4][:, :], g.dup_bias[:, 17 + k:18 + k], LIN_ONE - 1.0,
                                              ALU.add, ALU.max).then_inc(z_used, 1)
                            dve.wait_ge(z_used, b * 9 + k - 8 + 1)
                            dst = whole[:, i, :] if k < NS else qcT[:, :]
                            dve.scalar_tensor_tensor(dst, raised[:, i, :], 1.0, floor[:, i, :], ALU.min, ALU.add).then_inc(q_made, 1)
                        if 1 <= k:
                            split(k - 1)
                        if k in (4, 5, 6, 7):
                            token_rows(k - 4)
                        if k in (6, 7, 8, 9):
                            token_keys(k - 6)
                    dve.wait_ge(st_made, b + 1)
                    dve.tensor_tensor(state[:, :, :], misc[:, 0:(BPS - 1) * AH * AW].rearrange("p (m n) -> p m n", n=AH * AW),
                                      c.f("blockdiag").unsqueeze(1).broadcast_to([P, BPS - 1, AH * AW]), ALU.mult).then_inc(st_ready, 1)

                    def row_max(n):
                        blk, pr = divmod(n, PAIRS)
                        dve.wait_ge(scored, b * NP + n + 1)
                        w = keys(blk)
                        dve.tensor_reduce(neg[:, blk, pr, :], scores[n % 2][:, 0:2 * w].rearrange("p (h k) -> p h k", h=2),
                                          AX.X, ALU.max, negate=True).then_inc(maxed, 1)

                    def copy_probs(n):
                        blk = n // PAIRS
                        dve.wait_ge(p_turned, b * NP + n + 1)
                        if n >= 2:
                            dve.wait_ge(mixed, b * NP + n - 1)
                        m = 2 * keys(blk)
                        dve.tensor_copy(probsT[:, n % 2, 0:m // P, :], turned[n % 2][:, 0:m].rearrange("p (j q) -> p j q", q=P)).then_inc(p_copied_v, 1)

                    def causal(m):
                        dve.wait_ge(l_scored, b * NQ + m + 1)
                        if m >= 2:
                            dve.wait_ge(l_mixed, b * NQ + m - 1)
                        dve.tensor_tensor(linT[:, m % 2], lin_bank[:, :].rearrange("p (h q) -> p h q", q=P),
                                          c.f("causal_t").unsqueeze(1).broadcast_to([P, 4, P]), ALU.mult).then_inc(l_masked, 1)

                    def outs(blk):
                        i = blk % 2
                        dve.wait_ge(mixed, b * NP + (blk + 1) * PAIRS)
                        if blk >= 2:
                            dve.wait_ge(y_turned, b * BPS + blk - 1)
                        a = win_out[:, 0:AH * AW].rearrange("p (h e) -> p h e", e=AW)
                        link(dve.reciprocal(den[:, 0, :], a[:, :, AE]))
                        dve.tensor_tensor(yy[:, i, 0, :].rearrange("p (h e) -> p h e", e=AE), a[:, :, 0:AE],
                                          den[:, 0, :].unsqueeze(2).broadcast_to([P, AH, AE]), ALU.mult).then_inc(w_out, 1)
                        dve.wait_ge(l_mixed, b * NQ + 4 * blk + 4)
                        a = lin_out[:, 0:AH * AW].rearrange("p (h e) -> p h e", e=AW)
                        link(dve.tensor_scalar(den[:, 1, :], a[:, :, AE], 1e-6, None, ALU.add))
                        link(dve.reciprocal(den[:, 1, :], den[:, 1, :]))
                        dve.tensor_tensor(yy[:, i, 1, :].rearrange("p (h e) -> p h e", e=AE), a[:, :, 0:AE],
                                          den[:, 1, :].unsqueeze(2).broadcast_to([P, AH, AE]), ALU.mult).then_inc(l_out, 1)

                    def add_proj(blk):
                        dve.wait_ge(projected, b * BPS + blk + 1)
                        at = g.u[:, bass.DynSlice(b * BPS + blk, 1), :].rearrange("p o d -> p (o d)")
                        ins = dve.tensor_tensor(at, misc[:, 0:D], at, ALU.add)
                        ins.then_inc(added, 1)

                    row_max(0)
                    for n in range(NP + 6):
                        if n + 1 < NP:
                            row_max(n + 1)
                        if (n - 1) % 2 == 1 and 0 <= n - 1 < NP:
                            copy_probs(n - 1)
                        if n < NP and n % 2 == 0:
                            causal(n // 2)
                        if n >= PAIRS + 1 and (n - PAIRS - 1) % PAIRS == 0:
                            outs((n - PAIRS - 1) // PAIRS)
                        if n >= PAIRS + 5 and (n - PAIRS - 5) % PAIRS == 0:
                            add_proj((n - PAIRS - 5) // PAIRS)
                    assert n_link[0] == CHAIN, n_link[0]

            @block.scalar
            def _(act):
                with act.Fori(0, NB) as b:
                    act.wait_ge(x_turned, b + 1)
                    act.activation(xT[:, :], misc[:, :], ACT.Identity, scale=c.col("g1"), bias=c.col("b1")).then_inc(x_ready, 1)
                    for k in range(NZ):
                        act.wait_ge(z_made, b * NZ + k + 1)
                        bias = g.dup_bias[:, k:k + 1]
                        if k < 2 * NCK:
                            if k >= 2:
                                act.wait_ge(dup_made, b * NS + k - 1)
                            act.activation(high[:, k % 2, :], zbank[k % 4][:, :], ACT.Identity, bias=bias).then_inc(high_made, 1)
                            act.activation(whole[:, k % 2, :], zbank[k % 4][:, :], ACT.Identity, bias=bias).then_inc(z_copied, 1)
                        else:
                            if k >= 10:
                                act.wait_ge(q_made, b * 9 + k - 10 + 1)
                            act.activation(raised[:, k % 2, :], zbank[k % 4][:, :], ACT.Exp, bias=bias).then_inc(z_copied, 1)
                        if k > 2 * NCK:
                            act.wait_ge(q_made, b * 9 + k - 8)
                            act.wait_ge(dup_made, b * NS + k - 2)
                            act.activation(high[:, (k - 1) % 2, :], whole[:, (k - 1) % 2, :], ACT.Copy).then_inc(high_made, 1)
                        if k in (5, 6, 7, 8):
                            blk = k - 5
                            act.wait_ge(t_biased, b * BPS + blk + 1)
                            if blk >= 2:
                                act.wait_ge(t_ready, b * BPS + blk - 1)
                            act.activation(ke[:, blk, :], kz[:, blk, :], ACT.Exp).then_inc(k_exped, 1)

                    def exps(n):
                        blk, pr = divmod(n, PAIRS)
                        act.wait_ge(maxed, b * NP + n + 1)
                        if n >= 2:
                            act.wait_ge(p_turned, b * NP + n - 1)
                        w = keys(blk)
                        for h in range(2):
                            last = act.activation(probs[:, n % 2, h, 0:w], scores[n % 2][:, h * w:(h + 1) * w], ACT.Exp,
                                                  bias=neg[:, blk, pr, h:h + 1])
                        last.then_inc(probed, 1)

                    def copy_probs(n):
                        blk = n // PAIRS
                        act.wait_ge(p_turned, b * NP + n + 1)
                        if n >= 2:
                            act.wait_ge(mixed, b * NP + n - 1)
                        m = 2 * keys(blk)
                        act.activation(probsT[:, n % 2, 0:m // P, :], turned[n % 2][:, 0:m].rearrange("p (j q) -> p j q", q=P),
                                       ACT.Copy).then_inc(p_copied_a, 1)

                    for n in range(NP + 6):
                        if n < NP:
                            exps(n)
                        if (n - 1) % 2 == 0 and 0 <= n - 1 < NP:
                            copy_probs(n - 1)
                        m = n - PAIRS - 2
                        if m >= 0 and m % PAIRS == 0:
                            blk = m // PAIRS
                            act.wait_ge(y_turned, b * BPS + blk + 1)
                            act.activation(yT[:, :, :], misc[:, 0:2 * P].rearrange("p (j q) -> p j q", q=P), ACT.Copy).then_inc(yT_ready, 1)
                        if m >= 0 and m % PAIRS == 1:
                            blk = m // PAIRS
                            act.wait_ge(m_made, b * BPS + blk + 1)
                            act.activation(mT[:, :], misc[:, 0:P], ACT.Identity, bias=c.col("bp_a")).then_inc(m_ready, 1)

            @block.tensor
            def _(pe):
                pe.wait_ge(ones, 2)
                with pe.Fori(0, NB) as b:
                    pe.wait_ge(normed, b + 1)
                    for j in range(BPS):
                        last = pe.transpose(misc[:, j * P:(j + 1) * P], hn[:, j, :], c.ident)
                    last.then_inc(x_turned, 1)
                    pe.wait_ge(x_ready, b + 1)
                    for k in range(NZ):
                        if 4 <= k < 12:
                            pe.wait_ge(z_copied, b * NZ + k - 3)
                        elif k >= 12:
                            pe.wait_ge(z_used, b * 9 + k - 12 + 1)
                        kind, ck = divmod(k, NCK)
                        lhs = g.w_dup[:, kind, ck * P:(ck + 1) * P] if k < NS else g.w_qs[:, :]
                        pe.matmul(zbank[k % 4][:, :], lhs, xT[:, :], start=True, stop=True).then_inc(z_made, 1)
                        if k in (2, 3, 4, 5):
                            blk = k - 2
                            pe.matmul(tbank[blk][:, 0:3 * D], xT[:, blk * P:(blk + 1) * P], g.w_tok[:, :], start=True, stop=True).then_inc(t_made, 1)
                    pe.wait_ge(t_ready, b * BPS + BPS)
                    for m in range(BPS - 1):
                        for j in range(m + 1):
                            last = pe.matmul(misc[:, m * AH * AW:(m + 1) * AH * AW], ktok[:, j, :],
                                             vs[:, j].rearrange("p h e -> p (h e)"), start=j == 0, stop=j == m)
                    last.then_inc(st_made, 1)

                    def score(n):
                        blk, pr = divmod(n, PAIRS)
                        j, ck, _ = pair_heads(pr)
                        if n == 0:
                            pe.wait_ge(dup_made, b * NS + NS)
                        w = keys(blk)
                        bank = scores[n % 2]
                        pe.matmul(bank[:, 0:2 * w], c.ident_bf, c.first if blk == 0 else c.h("band_x"), start=True, stop=False)
                        rows = slice(32 * j, 32 * j + 32)
                        for h in range(2):
                            last = pe.matmul(bank[:, h * w:(h + 1) * w], dup[rows, QA, ck + h, blk * P:(blk + 1) * P],
                                             dup[rows, KA, ck + h, (blk + 1) * P - w:(blk + 1) * P], start=False, stop=h == 1)
                        last.then_inc(scored, 1)

                    def turn(n):
                        blk = n // PAIRS
                        pe.wait_ge(probed, b * NP + n + 1)
                        if n >= 2:
                            s = (p_copied_a, p_copied_v)[n % 2]
                            pe.wait_ge(s, b * NP // 2 + n // 2)
                        nk = keys(blk) // P
                        for h in range(2):
                            for j in range(nk):
                                at = (h * nk + j) * P
                                last = pe.transpose(turned[n % 2][:, at:at + P], probs[:, n % 2, h, j * P:(j + 1) * P], c.ident)
                        last.then_inc(p_turned, 1)

                    def mix(n):
                        blk, pr = divmod(n, PAIRS)
                        s = (p_copied_a, p_copied_v)[n % 2]
                        pe.wait_ge(s, b * NP // 2 + n // 2 + 1)
                        if pr == 0 and blk:
                            pe.wait_ge(w_out, b * BPS + blk)
                        nk = keys(blk) // P
                        for h, head in enumerate(pair_heads(pr)[2]):
                            for j in range(nk):
                                last = pe.matmul(win_out[:, head * AW:(head + 1) * AW], probsT[:, n % 2, h * nk + j, :],
                                                 va[:, blk - nk + 1 + j, head, :], start=j == 0, stop=j == nk - 1)
                        last.then_inc(mixed, 1)

                    def lin_score(m):
                        blk, j = divmod(m, 4)
                        if m >= 1:
                            pe.wait_ge(l_masked, b * NQ + m)
                        rows = slice(32 * j, 32 * j + 32)
                        cols = slice(blk * P, (blk + 1) * P)
                        for ck in range(4):
                            last = pe.matmul(lin_bank[:, ck * P:(ck + 1) * P], dup[rows, KS, ck, cols], dup[rows, QS, ck, cols],
                                             start=True, stop=True)
                        last.then_inc(l_scored, 1)

                    def lin_mix(m):
                        blk, j = divmod(m, 4)
                        pe.wait_ge(l_masked, b * NQ + m + 1)
                        if j == 0 and blk:
                            pe.wait_ge(l_out, b * BPS + blk)
                            pe.matmul(lin_out[:, 0:AH * AW], qcT[:, blk * P:(blk + 1) * P], state[:, blk - 1, :], start=True, stop=False)
                        for ck in range(4):
                            head = 4 * ck + j
                            last = pe.matmul(lin_out[:, head * AW:(head + 1) * AW], linT[:, m % 2, ck, :], vs[:, blk, head, :],
                                             start=blk == 0, stop=blk == 0 or (ck == 3 and j == 3))
                        last.then_inc(l_mixed, 1)

                    score(0)
                    score(1)
                    pe.wait_ge(st_ready, b + 1)
                    pe.wait_ge(q_made, b * 9 + 9)
                    for n in range(NP + 6):
                        if n < NP:
                            turn(n)
                        if n + 2 < NP:
                            score(n + 2)
                        if n < NP and n % 2 == 0:
                            lin_score(n // 2)
                        if 1 <= n <= NP:
                            mix(n - 1)
                        if 1 <= n <= NP and n % 2 == 1:
                            lin_mix(n // 2)
                        m = n - PAIRS - 1
                        if m >= 0 and m // PAIRS < BPS:
                            blk = m // PAIRS
                            if m % PAIRS == 0:
                                pe.wait_ge(l_out, b * BPS + blk + 1)
                                if blk:
                                    pe.wait_ge(added, b * BPS + blk)
                                for q in range(2):
                                    last = pe.transpose(misc[:, q * P:(q + 1) * P], yy[:, blk % 2, q, :], c.ident)
                                last.then_inc(y_turned, 1)
                            if m % PAIRS == 1:
                                pe.wait_ge(yT_ready, b * BPS + blk + 1)
                                pe.matmul(misc[:, 0:P], g.w_p[:, :], yT[:, 0, :], start=True, stop=False)
                                pe.matmul(misc[:, 0:P], g.w_os[:, :], yT[:, 1, :], start=False, stop=True).then_inc(m_made, 1)
                            if m % PAIRS == 2:
                                pe.wait_ge(m_ready, b * BPS + blk + 1)
                                pe.matmul(misc[:, 0:D], mT[:, :], g.w_o[:, :], start=True, stop=True).then_inc(projected, 1)
                    pe.wait_ge(added, b * BPS + BPS)


def mlp(nc, g, S):
    with ExitStack() as ctx:
        def sb(name, shape, dt=F32):
            return ctx.enter_context(nc.sbuf_tensor("m_" + name, shape, dt))

        NCK = DM // P
        hn = sb("hn", [P, BPS, D])
        hT = sb("hT", [P, SEQ])
        mid = sb("mid", [P, NCK, SEQ])
        c = g.c
        start, normed, turned, hT_ready, upped, gelued, downed, added, chain = (
            S("m_" + n) for n in ("start", "normed", "turned", "hT", "upped", "gelu", "downed", "added", "chain"))
        rows, ups, downs = g.bank[0], g.bank[1:5], g.bank[5:7]

        with nc.Block() as block:
            @block.vector
            def _(dve):
                dve.tensor_tensor(g.x[:, :, :], g.x[:, :, :], g.u[:, :, :], ALU.add).then_inc(start, 1)
                dve.wait_ge(start, 1)
                dve.tensor_tensor(g.x[:, :, :], g.x[:, :, :], c.row("b2m").unsqueeze(1).broadcast_to([P, NBLK, D]), ALU.add).then_inc(start, 1)
                dve.wait_ge(start, 2)
                with dve.Fori(0, NB) as b:
                    blks = bass.DynSlice(b * BPS, BPS)
                    dve.tensor_tensor(hn[:, :, :], g.u[:, blks, :],
                                      g.stat.mean[:, blks].unsqueeze(2).broadcast_to([P, BPS, D]), ALU.subtract).then_inc(chain, 1)
                    dve.wait_ge(chain, b + 1)
                    dve.tensor_tensor(hn[:, :, :], hn[:, :, :],
                                      g.stat.r[:, blks].unsqueeze(2).broadcast_to([P, BPS, D]), ALU.mult).then_inc(normed, 1)
                    dve.wait_ge(turned, b + 1)
                    dve.tensor_scalar(hT[:, :], rows[:, :], c.col("gm"), c.col("bm"), ALU.mult, ALU.add).then_inc(hT_ready, 1)
                    for blk in range(BPS):
                        dve.wait_ge(downed, b * BPS + blk + 1)
                        at = g.x[:, bass.DynSlice(b * BPS + blk, 1), :].rearrange("p o d -> p (o d)")
                        dve.tensor_tensor(at, downs[blk % 2][:, 0:D], at, ALU.add).then_inc(added, 1)

            @block.scalar
            def _(act):
                with act.Fori(0, NB) as b:
                    for k in range(NCK):
                        act.wait_ge(upped, b * NCK + k + 1)
                        act.activation(mid[:, k, :], ups[k][:, :], ACT.Gelu, bias=c.col(f"b1m{k}")).then_inc(gelued, 1)

            @block.tensor
            def _(pe):
                with pe.Fori(0, NB) as b:
                    pe.wait_ge(normed, b + 1)
                    for j in range(BPS):
                        last = pe.transpose(rows[:, j * P:(j + 1) * P], hn[:, j, :], c.ident)
                    last.then_inc(turned, 1)
                    pe.wait_ge(hT_ready, b + 1)
                    for k in range(NCK):
                        pe.matmul(ups[k][:, :], g.w1[:, k * P:(k + 1) * P], hT[:, :], start=True, stop=True).then_inc(upped, 1)
                    pe.wait_ge(gelued, b * NCK + NCK)
                    for blk in range(BPS):
                        if blk >= 2:
                            pe.wait_ge(added, b * BPS + blk - 1)
                        for k in range(NCK):
                            last = pe.matmul(downs[blk % 2][:, 0:D], mid[:, k, blk * P:(blk + 1) * P], g.w2[:, k, :],
                                             start=k == 0, stop=k == NCK - 1)
                        last.then_inc(downed, 1)
                    pe.wait_ge(added, b * BPS + BPS)


def build(nc, w, out):
    with ExitStack() as ctx:
        g = Shared()

        def sb(name, shape, dt=F32):
            return ctx.enter_context(nc.sbuf_tensor(name, shape, dt))

        half_sems = {}

        def S(name):
            if name[:3] not in ("f1_", "f2_"):
                return ctx.enter_context(nc.semaphore(name))
            if name[3:] not in half_sems:
                half_sems[name[3:]] = ctx.enter_context(nc.semaphore("ffn_" + name[3:]))
            return half_sems[name[3:]]

        g.x = sb("x", [P, NBLK, D])
        g.u = sb("u", [P, NBLK, D])
        g.w_qk = sb("w_qk", [P, NCH, P])
        g.w_rot = sb("w_rot", [P, NCH, P])
        g.w_v = sb("w_v", [P, KVH * DH])
        g.w_proj = sb("w_proj", [P, QCH, D])
        g.gate = sb("gate", [P, NE])
        g.w_up = sb("w_up", [P, NE, 2 * DFF])
        g.w_down = sb("w_down", [P, NE, D])
        g.w_dup = sb("w_dup", [P, 4, 4 * P])
        g.dup_bias = sb("dup_bias", [P, 34])
        g.w_qs = sb("w_qs", [P, D])
        g.w_tok = sb("w_tok", [P, 3 * D])
        g.w_p = sb("w_p", [P, D])
        g.w_os = sb("w_os", [P, D])
        g.w_o = sb("w_o", [P, D])
        g.w1 = sb("w1", [P, DM])
        g.w2 = sb("w2", [P, DM // P, D])
        g.const = sb("const", [P, NCONST])
        g.const_bf = sb("const_bf", [P, NCONST_BF], BF16)
        g.col = sb("col", [P, NCOL])
        g.row = sb("row", [P, NROW])
        g.neg_sink = sb("neg_sink", [P, HEADS])
        g.qk_bias = sb("qk_bias", [P, 2 * NCH])
        g.bank = [ctx.enter_context(nc.psum_tensor(f"bank{i}", [P, 512], F32)) for i in range(8)]
        st = g.stat = Shared()
        st.six = sb("st_six", [P, NBLK, 6])
        st.mv = sb("st_mv", [P, NBLK, 2])
        st.mean, st.v, st.v2, st.s, st.t, st.r, st.rr = (
            sb("st_" + n, [P, NBLK]) for n in ("mean", "var", "var2", "root", "work", "r", "rr"))

        r = g.routing = Shared()
        r.weight = ctx.enter_context(nc.sbuf_tensor("route_weight", [P, NBLK * TOPK], F32))
        r.slot = ctx.enter_context(nc.sbuf_tensor("route_slot", [P, NBLK * TOPK], U32))
        r.token = ctx.enter_context(nc.sbuf_tensor("route_token", [P, TILES], U32))
        r.owner = ctx.enter_context(nc.sbuf_tensor("route_owner", [1, P], I32))
        iota16 = g.iota16 = sb("iota16", [P, TILES + P], F16)
        g.rows_dram = nc.dram_tensor("rows", (NBLK * P, D), F32, kind="Internal").ap()
        g.y_dram = nc.dram_tensor("expert_rows", (TILES * P, D), F32, kind="Internal").ap()

        def f(name):
            a, b = CONST_F32[name]
            return g.const[:, a:b]

        def h(name):
            a, b = CONST_BF[name]
            return g.const_bf[:, a:b]

        def col(name):
            return g.col[:, COLS[name]:COLS[name] + 1]

        c = g.c = Shared()
        c.ident, c.cos, c.sin = f("ident"), f("cos"), f("sin")
        c.ident_bf, c.band, c.first = h("ident"), h("band"), h("first")
        c.col, c.f, c.h = col, f, h
        c.row = lambda name: g.row[:, ROWS[name][0]:ROWS[name][1]]
        c.row_bv = c.row("bv")
        c.iota_t16, c.iota_s16 = iota16[:, 0:TILES], iota16[:, TILES:TILES + P]

        setup(nc, g, w, S)
        setup_attention(nc, g, w, S)
        for half, tag in enumerate(("f1", "f2")):
            if tag == "f2":
                with nc.Block() as block:
                    @block.gpsimd
                    def _(pool):
                        for name, sem in half_sems.items():
                            if not name.startswith(("e_gathered", "c_fetched")):
                                pool.sem_clear(sem)
            normalise(nc, g, S, tag, g.x, g.u, plus=c.row("proj_b"))
            sink_attention(nc, g, S, tag)
            route(nc, g, S, tag)
            experts(nc, g, S, tag, half)
            combine(nc, g, S, tag, half)
            if tag == "f1":
                normalise(nc, g, S, "l", g.x, g.u, plus=c.row("bo"))
                window_and_linear(nc, g, S)
                normalise(nc, g, S, "m", g.u, None)
                mlp(nc, g, S)
        stored = S("stored")
        with nc.Block() as block:
            @block.sync
            def _(sp):
                sp.dma_start(out.rearrange("b (n p) d -> p (b n) d", p=P), g.x[:, :, :]).then_inc(stored, 16)
                sp.wait_ge(stored, 16)


_INS = ["L0_attn_x", "L0_attn_g1", "L0_attn_b1", "L0_attn_Wqkv_a", "L0_attn_bqkv_a", "L0_attn_Wp_a", "L0_attn_bp_a",
        "L0_attn_Wqkv_s", "L0_attn_bqkv_s", "L0_attn_Wo_s", "L0_attn_bo_s", "L0_attn_Wo", "L0_attn_bo", "L0_attn_gm",
        "L0_attn_bm", "L0_attn_W1", "L0_attn_b1m", "L0_attn_W2", "L0_attn_b2m", "L0_ffn_attn_norm_w",
        "L0_ffn_ffn_norm_w", "L0_ffn_qkv_w", "L0_ffn_qkv_b", "L0_ffn_proj_w", "L0_ffn_proj_b", "L0_ffn_attn_sink",
        "L0_ffn_gate_w", "L0_ffn_gate_b", "L0_ffn_W_up", "L0_ffn_W_down"]


def _constants():
    import numpy as np
    c = np.zeros((P, NCONST), np.float32)

    def put(name, a):
        lo, hi = CONST_F32[name]
        c[:, lo:hi] = a

    p = np.arange(P)
    put("ident", np.eye(P))
    inv = (1.0 / np.float32(150000.0) ** (np.arange(0, DH, 2, dtype=np.float32) / np.float32(DH))).astype(np.float32)
    pos = (np.arange(SEQ, dtype=np.float32) / np.float32(32.0)).astype(np.float32)
    ang = (pos[None, :] * inv[(p % DH) // 2][:, None]).astype(np.float32)
    put("cos", np.cos(ang))
    put("sin", np.sin(ang))
    put("iota_e", np.arange(NE)[None, :])
    put("iota_s", np.arange(P)[None, :])
    put("iota_t", np.arange(TILES)[None, :])
    t = (p % 32) // AE
    put("cols", np.stack([p, -(t >= 2).astype(np.float32), -(t % 2 == 1).astype(np.float32)], 1))
    put("token", p[:, None] + P * np.arange(NBLK)[None, :])
    put("scan", np.tile((np.arange(NBLK) > 0).astype(np.float32), NE)[None, :])
    hd = p // AE
    put("blockdiag", np.repeat(hd[:, None] == np.arange(AH)[None, :], AW, axis=1))
    put("causal_t", (p[:, None] <= p[None, :]))
    h = np.zeros((P, NCONST_BF), np.float32)

    def puth(name, a):
        lo, hi = CONST_BF[name]
        h[:, lo:hi] = a

    big = np.float32(-1e30)
    r, s = p[:, None], p[None, :]
    own = np.where(s <= r, 0, big)
    prev = np.where(s >= r, 0, big)
    prev_x = np.where(s > r, 0, big)
    puth("ident", np.eye(P))
    puth("before", s > r)
    puth("ones", 1.0)
    puth("band", np.concatenate([prev, own, prev, own], 1))
    puth("band_x", np.concatenate([prev_x, own, prev_x, own], 1))
    puth("first", np.concatenate([own, own], 1))
    return c, h


def kernel(**inputs):
    import numpy as _np
    import concourse.bacc as _bacc
    from concourse import mybir as _mybir
    from concourse.bass_utils import run_bass_kernel_spmd as _run

    nc = _bacc.Bacc("TRN2", target_bir_lowering=False, num_devices=1)
    arrays, w = {}, {}
    for name in _INS:
        a = _np.ascontiguousarray(inputs[name])
        arrays[f"in_{name}"] = a
        w[name] = nc.dram_tensor(f"in_{name}", a.shape, _mybir.dt.from_np(a.dtype), kind="ExternalInput").ap()
    for name, a in zip(("const", "const_bf"), _constants()):
        arrays[f"in_{name}"] = a
        w[name] = nc.dram_tensor(f"in_{name}", a.shape, _mybir.dt.from_np(a.dtype), kind="ExternalInput").ap()
    out = nc.dram_tensor("out_0_dram", (NB, SEQ, D), _mybir.dt.float32, kind="ExternalOutput").ap()
    build(nc, w, out)
    r = _run(nc, [arrays], core_ids=[0])
    return r.results[0]["out_0_dram"]
```

```python
from contextlib import ExitStack

import concourse.bass as bass
from concourse import mybir

F32 = mybir.dt.float32
BF16 = mybir.dt.bfloat16
F16 = mybir.dt.float16
I32 = mybir.dt.int32
U32 = mybir.dt.uint32
ALU = mybir.AluOpType
ACT = mybir.ActivationFunctionType
AX = mybir.AxisListType

P = 128
D = 128
NB, SEQ = 4, 512
BPS = SEQ // P
NBLK = NB * BPS
EPS = 1e-5

HEADS, KVH, DH = 16, 4, 64
QCH = HEADS // 2
NCH = QCH + KVH // 2
VW = DH + 1
PAIRS = HEADS // 2
NE, TOPK, DFF = 32, 4, 128
TILES = NBLK * TOPK + NE
AH, AE = 16, 8
AW = AE + 1
DM = 4 * D
KDUP = 4
LIN_ONE = 1.0001

ROWS = {}
_at = 0
for _name, _n in (("bv", KVH * DH), ("proj_b", D), ("gate_b", NE), ("sink", HEADS),
                  ("bk_s", D), ("bv_a", D), ("bv_s", D), ("bo", D), ("b2m", D)):
    ROWS[_name] = (_at, _at + _n)
    _at += _n
NROW = _at
COLS = {n: k for k, n in enumerate(
    ["attn_w", "ffn_w", "g1", "b1", "gm", "bm", "bp_a", "bo_s", "b1m0", "b1m1", "b1m2", "b1m3",
     "q_lo", "k_lo", "part"])}
NCOL = len(COLS)
CONST_F32 = {}
_at = 0
for _name, _n in (("ident", P), ("cos", SEQ), ("sin", SEQ), ("iota_e", NE), ("iota_s", P),
                  ("iota_t", TILES), ("cols", 3), ("token", NBLK), ("scan", NE * NBLK),
                  ("blockdiag", AH * AW), ("causal_t", P)):
    CONST_F32[_name] = (_at, _at + _n)
    _at += _n
NCONST = _at
CONST_BF = {"ident": (0, P), "before": (P, 2 * P), "ones": (2 * P, 3 * P),
            "band": (3 * P, 7 * P), "first": (7 * P, 9 * P), "band_x": (9 * P, 13 * P)}
NCONST_BF = 13 * P


class Shared:
    pass


def chained(eng, sem, start=0):
    count = [start]

    def link(ins):
        count[0] += 1
        ins.then_inc(sem, 1)
        eng.wait_ge(sem, count[0])

    link.count = count
    return link


def setup(nc, g, w, S):
    with ExitStack() as ctx:
        row = ctx.enter_context(nc.sbuf_tensor("rows_1", [1, NROW], F32))
        qkb = ctx.enter_context(nc.sbuf_tensor("qk_bias_row", [1, 2, NCH, P], F32))
        sink = ctx.enter_context(nc.sbuf_tensor("sink_row", [1, HEADS], F32))
        one = ctx.enter_context(nc.sbuf_tensor("ones_row", [1, P], F32))
        masks = ctx.enter_context(nc.sbuf_tensor("masks_f32", [P, NCONST_BF], F32))
        loaded = S("setup_loaded")
        made = S("setup_made")
        turned = S("setup_turned")
        spread = S("setup_spread")
        kept = S("setup_kept")
        n_dma = [0]

        def halves(t):
            half = KVH * DH
            return [(t[:, 0:4, 0:DH], 0), (t[:, 0:4, DH:P], half), (t[:, 4:8, 0:DH], 2 * half),
                    (t[:, 4:8, DH:P], 3 * half)]

        loads = [(g.const[:, :], w["const"]), (masks[:, :], w["const_bf"]),
                 (g.x[:, :, :], w["L0_attn_x"].rearrange("b (n p) d -> p (b n) d", p=P)),
                 (g.w_qk[:, QCH:NCH, :], w["L0_ffn_qkv_w"][:, HEADS * DH:(HEADS + KVH) * DH].rearrange("d (c e) -> d c e", e=P)),
                 (g.w_v[:, :], w["L0_ffn_qkv_w"][:, (HEADS + KVH) * DH:]),
                 (g.gate[:, :], w["L0_ffn_gate_w"])]
        for dst, at in halves(g.w_qk):
            loads.append((dst, w["L0_ffn_qkv_w"][:, at:at + 4 * DH].rearrange("d (c e) -> d c e", e=DH)))
        qb = w["L0_ffn_qkv_b"].rearrange("(o n) -> o n", o=1)
        for dst, at in halves(qkb[:, 0]):
            loads.append((dst, qb[:, at:at + 4 * DH].rearrange("d (c e) -> d c e", e=DH)))
        loads.append((qkb[:, 0, QCH:NCH, :], qb[:, HEADS * DH:(HEADS + KVH) * DH].rearrange("d (c e) -> d c e", e=P)))
        pw = w["L0_ffn_proj_w"]
        for dst, at in ((g.w_proj[0:DH, 0:4, :], 0), (g.w_proj[DH:P, 0:4, :], 256),
                        (g.w_proj[0:DH, 4:8, :], 512), (g.w_proj[DH:P, 4:8, :], 768)):
            loads.append((dst, pw[at:at + 256, :].rearrange("(c e) d -> e c d", e=DH)))

        def rowload(name, src):
            a, b = ROWS[name]
            loads.append((row[:, a:b], src.rearrange("(o n) -> o n", o=1)))

        rowload("bv", w["L0_ffn_qkv_b"][(HEADS + KVH) * DH:])
        rowload("proj_b", w["L0_ffn_proj_b"])
        rowload("gate_b", w["L0_ffn_gate_b"])
        rowload("bk_s", w["L0_attn_bqkv_s"][D:2 * D])
        rowload("bv_a", w["L0_attn_bqkv_a"][2 * D:])
        rowload("bv_s", w["L0_attn_bqkv_s"][2 * D:])
        rowload("bo", w["L0_attn_bo"])
        rowload("b2m", w["L0_attn_b2m"])
        loads.append((sink[:, :], w["L0_ffn_attn_sink"].rearrange("(o n) -> o n", o=1)))
        for name, src in (("attn_w", "L0_ffn_attn_norm_w"), ("ffn_w", "L0_ffn_ffn_norm_w"), ("g1", "L0_attn_g1"),
                          ("b1", "L0_attn_b1"), ("gm", "L0_attn_gm"), ("bm", "L0_attn_bm"),
                          ("bp_a", "L0_attn_bp_a"), ("bo_s", "L0_attn_bo_s")):
            loads.append((g.col[:, COLS[name]:COLS[name] + 1], w[src].rearrange("(p o) -> p o", o=1)))
        k = COLS["b1m0"]
        for j in range(DM // P):
            loads.append((g.col[:, k + j:k + j + 1], w["L0_attn_b1m"][j * P:(j + 1) * P].rearrange("(p o) -> p o", o=1)))
        for half in range(2):
            e0, e1 = half * NE // 2, (half + 1) * NE // 2
            loads.append((g.w_up[:, e0:e1, :], w["L0_ffn_W_up"][e0:e1].rearrange("e d f -> d e f")))
            loads.append((g.w_down[:, e0:e1, :], w["L0_ffn_W_down"][e0:e1].rearrange("e f d -> f e d")))
        total = 16 * len(loads)
        banks = g.bank

        with nc.Block() as block:
            @block.sync
            def _(sp):
                for dst, src in loads[0::2]:
                    sp.dma_start(dst, src).then_inc(loaded, 16)

            @block.scalar
            def _(act):
                for dst, src in loads[1::2]:
                    act.dma_start(dst, src).then_inc(loaded, 16)

            @block.gpsimd
            def _(pool):
                pool.memset(one[:, :], 1.0).then_inc(made, 1)

            @block.vector
            def _(dve):
                dve.wait_ge(loaded, total)
                link = chained(dve, turned)
                link(dve.tensor_copy(g.const_bf[:, :], masks[:, :]))
                link(dve.tensor_scalar(g.w_qk[:, 0:QCH, :], g.w_qk[:, 0:QCH, :], DH ** -0.5, None, ALU.mult))
                link(dve.tensor_scalar(qkb[:, 0, 0:QCH, :], qkb[:, 0, 0:QCH, :], DH ** -0.5, None, ALU.mult))
                for dst, src in ((g.w_rot, g.w_qk[:, :, :]), (qkb[:, 1], qkb[:, 0])):
                    d = (dst[:, :, :] if dst is g.w_rot else dst).rearrange("p c (e t) -> p c e t", t=2)
                    s = src.rearrange("p c (e t) -> p c e t", t=2)
                    link(dve.tensor_scalar(d[:, :, :, 0], s[:, :, :, 1], -1.0, None, ALU.mult))
                    link(dve.tensor_copy(d[:, :, :, 1], s[:, :, :, 0]))
                link(dve.tensor_copy(g.iota16[:, 0:TILES], g.const[:, CONST_F32["iota_t"][0]:CONST_F32["iota_t"][1]]))
                link(dve.tensor_copy(g.iota16[:, TILES:TILES + P], g.const[:, CONST_F32["iota_s"][0]:CONST_F32["iota_s"][1]]))
                a = ROWS["sink"][0]
                for half in range(2):
                    for up in range(2):
                        link(dve.tensor_copy(row[:, a + 8 * up + half:a + 8 * up + 8:2],
                                             sink[:, 8 * up + 4 * half:8 * up + 4 * half + 4]))
                dve.wait_ge(spread, 1)
                dve.tensor_copy(g.qk_bias[:, :], banks[0][:, 0:2 * NCH]).then_inc(kept, 1)
                for j in range(0, NROW, 512):
                    n = min(512, NROW - j)
                    dve.tensor_copy(g.row[:, j:j + n], banks[1 + j // 512][:, 0:n]).then_inc(kept, 1)
                dve.wait_ge(kept, 1 + (NROW + 511) // 512)
                a, b = ROWS["sink"]
                dve.tensor_scalar(g.neg_sink[:, :], g.row[:, a:b], -1.0, None, ALU.mult).then_inc(kept, 1)

            @block.tensor
            def _(pe):
                pe.wait_ge(loaded, total)
                pe.wait_ge(made, 1)
                pe.wait_ge(turned, 13)
                for v in range(2):
                    for c in range(NCH):
                        pe.matmul(banks[0][:, v * NCH + c:v * NCH + c + 1], qkb[:, v, c, :], one[:, 0:1], start=True, stop=True)
                for j in range(0, NROW, 512):
                    n = min(512, NROW - j)
                    last = pe.matmul(banks[1 + j // 512][:, 0:n], one[:, :], row[:, j:j + n], start=True, stop=True)
                last.then_inc(spread, 1)


def normalise(nc, g, S, tag, src, out, plus=None):
    st = g.stat
    with ExitStack():
        roots, v_ready, rooted = S(f"{tag}_norm_chain"), S(f"{tag}_norm_var"), S(f"{tag}_norm_sqrt")
        with nc.Block() as block:
            @block.vector
            def _(dve):
                link = chained(dve, roots)
                for i in range(NBLK):
                    last = dve.bn_stats(st.six[:, i, :], src[:, i, :])
                link(last)
                for i in range(NBLK):
                    last = dve.bn_aggr(st.mv[:, i, :], st.six[:, i, :])
                link(last)
                link(dve.tensor_copy(st.mean[:, :], st.mv[:, :, 0]))
                link(dve.tensor_scalar(st.v[:, :], st.mv[:, :, 1], EPS, None, ALU.add))

                def rsqrt(y, v, n):
                    dve.wait_ge(rooted, n)
                    link(dve.reciprocal(y, st.s[:, :]))
                    link(dve.tensor_tensor(st.t[:, :], y, y, ALU.mult))
                    link(dve.tensor_tensor(st.t[:, :], st.t[:, :], v, ALU.mult))
                    link(dve.tensor_scalar(st.t[:, :], st.t[:, :], -0.5, 1.5, ALU.mult, ALU.add))
                    link(dve.tensor_tensor(y, y, st.t[:, :], ALU.mult))

                rsqrt(st.r[:, :], st.v[:, :], 1)
                link(dve.tensor_tensor(st.v2[:, :], st.r[:, :], st.r[:, :], ALU.mult))
                link(dve.tensor_tensor(st.v2[:, :], st.v2[:, :], st.mv[:, :, 1], ALU.mult))
                link(dve.tensor_scalar(st.v2[:, :], st.v2[:, :], EPS, None, ALU.add))
                rsqrt(st.rr[:, :], st.v2[:, :], 2)
                link(dve.tensor_tensor(st.rr[:, :], st.rr[:, :], st.r[:, :], ALU.mult))
                for i in range(NBLK if out is not None else 0):
                    last = dve.tensor_scalar(out[:, i, :], src[:, i, :], st.mean[:, i:i + 1], st.r[:, i:i + 1],
                                             ALU.subtract, ALU.mult)
                if out is not None:
                    link(last)
                if plus is not None:
                    link(dve.tensor_tensor(out[:, :, :], out[:, :, :],
                                           plus.unsqueeze(1).broadcast_to([P, NBLK, D]), ALU.add))

            @block.scalar
            def _(act):
                act.wait_ge(roots, 4)
                act.activation(st.s[:, :], st.v[:, :], ACT.Sqrt).then_inc(rooted, 1)
                act.wait_ge(roots, 12)
                act.activation(st.s[:, :], st.v2[:, :], ACT.Sqrt).then_inc(rooted, 1)


def sink_attention(nc, g, S, tag):
    with ExitStack() as ctx:
        def sb(name, shape, dt=F32):
            return ctx.enter_context(nc.sbuf_tensor(f"{tag}_{name}", shape, dt))

        hn = sb("hn", [P, BPS, D])
        hT = sb("hT", [P, SEQ])
        qT = sb("qT", [P, QCH, SEQ])
        kz = sb("kz", [P, KVH, SEQ])
        rope_a = sb("rope_a", [P, 2, SEQ])
        rope_b = sb("rope_b", [P, 2, SEQ])
        v = sb("v", [P, BPS, KVH, VW])
        probs = sb("probs", [P, 2, 2, 2 * P])
        v_high = sb("v_high", [P, BPS, KVH, VW], F16)
        v_low = sb("v_low", [P, BPS, KVH, VW], F16)
        p_high = sb("p_high", [P, 2, 4, P], F16)
        p_low = sb("p_low", [P, 2, 4, P], F16)
        neg = sb("neg_max", [P, BPS, HEADS])
        sinks = sb("sinks", [P, BPS, HEADS])
        den = sb("den", [P, 2, 4])
        y = sb("y", [P, 2, HEADS, DH])
        yT = sb("yT", [P, QCH, P])
        scores = g.bank[0:3]
        turned = g.bank[3:5]
        av = g.bank[5:7]
        misc = g.bank[7]
        c = g.c
        ident, ident_bf = c.ident, c.ident_bf
        NP = BPS * PAIRS
        KCH = NCH - QCH
        ORDER = list(range(QCH, NCH)) + list(range(QCH))
        NR = NCH + KCH

        def adds_through(k):
            return k + 1 + min(k + 1, KCH)

        normed, hT_turned, hT_ready = S(tag + "_normed"), S(tag + "_hT_turned"), S(tag + "_hT")
        qk_made, roped_parts, roped = S(tag + "_qk"), S(tag + "_rope_parts"), S(tag + "_roped")
        v_made, v_ready = S(tag + "_v_made"), S(tag + "_v")
        scored, maxed, probed = S(tag + "_scored"), S(tag + "_maxed"), S(tag + "_probs")
        v_rounded, v_parted = S(tag + "_v_rounded"), S(tag + "_v_parted")
        p_turned, p_rounded, p_parted = S(tag + "_p_turned"), S(tag + "_p_rounded"), S(tag + "_p_parted")
        mixed, sink_sum, sinks_exp, y_ready = S(tag + "_mixed"), S(tag + "_sink_sum"), S(tag + "_sinks"), S(tag + "_y")
        y_turned, yT_ready, projected, added = S(tag + "_y_turned"), S(tag + "_yT"), S(tag + "_proj"), S(tag + "_added")
        chain, ones, zeroed = S(tag + "_chain"), S(tag + "_ones"), S(tag + "_zeroed")
        centred = S(tag + "_centred")
        qk_banks = (scores[0:2], turned)
        v_banks = (scores[2], av[0])
        NEXT_NORM, NEXT_TURN, TAIL_TURN, TAIL_PROJECT = 1, 4, 2, 4
        CHAIN = 64

        def keys(blk):
            return P if blk == 0 else 2 * P

        with nc.Block() as block:
            @block.vector
            def _(dve):
                dve.memset(v[:, :, :, DH:VW], 1.0).then_inc(ones, 1)

                def rows_norm(b):
                    blks = bass.DynSlice(b * BPS, BPS)
                    dve.tensor_tensor(hn[:, :, :], g.x[:, blks, :],
                                      g.stat.mean[:, blks].unsqueeze(2).broadcast_to([P, BPS, D]), ALU.subtract).then_inc(centred, 1)
                    dve.wait_ge(centred, b + 1)
                    dve.tensor_tensor(hn[:, :, :], hn[:, :, :],
                                      g.stat.rr[:, blks].unsqueeze(2).broadcast_to([P, BPS, D]), ALU.mult).then_inc(normed, 1)

                def add_proj(b, blk):
                    dve.wait_ge(projected, b * BPS + blk + 1)
                    at = g.u[:, bass.DynSlice(b * BPS + blk, 1), :].rearrange("p o d -> p (o d)")
                    dve.tensor_tensor(at, misc[:, 0:D], at, ALU.add).then_inc(added, 1)

                def rope(b, tail):
                    for k, ch in enumerate(ORDER):
                        dve.wait_ge(qk_made, b * NCH + k + 1)
                        if k >= 2:
                            dve.wait_ge(roped, b * NR + adds_through(k - 2))
                        ba, bb = qk_banks[k % 2]
                        dve.scalar_tensor_tensor(rope_a[:, k % 2, :], ba[:, :], g.qk_bias[:, ch:ch + 1], c.cos,
                                                 ALU.add, ALU.mult)
                        dve.scalar_tensor_tensor(rope_b[:, k % 2, :], bb[:, :], g.qk_bias[:, NCH + ch:NCH + ch + 1], c.sin,
                                                 ALU.add, ALU.mult).then_inc(roped_parts, 1)
                        if k in (4, 6):
                            h = (k - 4) // 2
                            dve.wait_ge(v_made, b * 2 + h + 1)
                            for j in range(2):
                                last = dve.tensor_tensor(
                                    v[:, 2 * h + j, :, 0:DH],
                                    v_banks[h][:, j * KVH * DH:(j + 1) * KVH * DH].rearrange("p (h e) -> p h e", e=DH),
                                    c.row_bv.rearrange("p (h e) -> p h e", e=DH), ALU.add)
                            last.then_inc(v_ready, 1)
                        if k == TAIL_PROJECT + 1 and tail is not None:
                            add_proj(tail, BPS - 1)
                    dve.wait_ge(v_rounded, b + 1)
                    dve.tensor_tensor(v_low[:, :, :, :], v[:, :, :, :], v_high[:, :, :, :], ALU.subtract).then_inc(v_parted, 1)

                def pairs(b, last):
                    n_link = [0]

                    def link(ins):
                        n_link[0] += 1
                        ins.then_inc(chain, 1)
                        dve.wait_ge(chain, b * CHAIN + n_link[0])

                    def row_max(n):
                        blk, pr = divmod(n, PAIRS)
                        k, half = divmod(pr, 2)
                        dve.wait_ge(scored, b * NP + n + 1)
                        w = keys(blk)
                        at = neg[:, blk, 4 * k + half:4 * k + 4:2]
                        link(dve.tensor_reduce(at, scores[n % 3][:, 0:2 * w].rearrange("p (h k) -> p h k", h=2),
                                               AX.X, ALU.max, negate=True))
                        dve.tensor_tensor(at, at, g.neg_sink[:, 4 * k + half:4 * k + 4:2], ALU.min).then_inc(maxed, 1)
                        if half:
                            dve.wait_ge(maxed, b * NP + n + 1)
                            dve.tensor_tensor(sinks[:, blk, 4 * k:4 * k + 4], neg[:, blk, 4 * k:4 * k + 4],
                                              g.neg_sink[:, 4 * k:4 * k + 4], ALU.subtract).then_inc(sink_sum, 1)

                    def part_probs(n):
                        m = 2 * keys(n // PAIRS)
                        dve.wait_ge(p_rounded, b * NP + n + 1)
                        dve.tensor_tensor(p_low[:, n % 2, 0:m // P, :], turned[n % 2][:, 0:m].rearrange("p (j q) -> p j q", q=P),
                                          p_high[:, n % 2, 0:m // P, :], ALU.subtract).then_inc(p_parted, 1)

                    def heads_out(m):
                        blk, k = divmod(m, PAIRS // 2)
                        dve.wait_ge(mixed, b * NP + 2 * m + 2)
                        dve.wait_ge(sinks_exp, b * NP // 2 + m + 1)
                        if k == 0 and blk >= 2:
                            dve.wait_ge(y_turned, b * 2 * BPS + 2 * (blk - 2) + 2)
                        a4 = av[m % 2][:, 0:4 * VW].rearrange("p (h e) -> p h e", e=VW)
                        d = den[:, m % 2, :]
                        link(dve.tensor_tensor(d, a4[:, :, DH], sinks[:, blk, 4 * k:4 * k + 4], ALU.add))
                        link(dve.reciprocal(d, d))
                        dve.tensor_tensor(y[:, blk % 2, 4 * k:4 * k + 4, :], a4[:, :, 0:DH],
                                          d.unsqueeze(2).broadcast_to([P, 4, DH]), ALU.mult).then_inc(y_ready, 1)

                    row_max(0)
                    for n in range(NP + 2):
                        if n + 1 < NP:
                            row_max(n + 1)
                        if 0 <= n - 1 < NP:
                            part_probs(n - 1)
                        if n >= 3 and (n - 3) % 2 == 0 and (n - 3) // 2 < NP // 2:
                            heads_out((n - 3) // 2)
                        if n >= PAIRS + 6 and (n - PAIRS - 6) % PAIRS == 0:
                            add_proj(b, (n - PAIRS - 6) // PAIRS)
                        if n == NEXT_NORM and not last:
                            rows_norm(b + 1)
                    assert n_link[0] == CHAIN, n_link[0]

                rows_norm(0)
                rope(0, None)
                with dve.Fori(0, NB - 1) as b:
                    pairs(b, False)
                    rope(b + 1, b)
                pairs(NB - 1, True)
                add_proj(NB - 1, BPS - 1)

            @block.gpsimd
            def _(pool):
                pool.memset(kz[:, :, :], 0.0).then_inc(zeroed, 1)
                pool.wait_ge(zeroed, 1)

                def add_rotary(b):
                    for k in range(NCH):
                        pool.wait_ge(roped_parts, b * NCH + k + 1)
                        if k >= KCH:
                            pool.tensor_tensor(qT[:, k - KCH, :], rope_a[:, k % 2, :], rope_b[:, k % 2, :], ALU.add).then_inc(roped, 1)
                            if k == KCH:
                                pool.wait_ge(roped, b * NR + 2 * KCH + 1)
                            continue
                        for half in range(2):
                            lo = half * DH
                            pool.tensor_tensor(kz[lo:lo + DH, 2 * k + half, :], rope_a[lo:lo + DH, k % 2, :],
                                               rope_b[lo:lo + DH, k % 2, :], ALU.add).then_inc(roped, 1)
                            pool.wait_ge(roped, b * NR + 2 * k + half + 1)

                add_rotary(0)
                with pool.Fori(0, NB - 1) as b:
                    add_rotary(b + 1)

            @block.scalar
            def _(act):

                def scale_rows(b):
                    act.wait_ge(hT_turned, b + 1)
                    act.activation(hT[:, :], misc[:, :], ACT.Copy, scale=c.col("attn_w")).then_inc(hT_ready, 1)

                def copy_y(b, j):
                    act.wait_ge(y_turned, b * 2 * BPS + j + 1)
                    if j % 2 == 0 and j >= 2:
                        act.wait_ge(projected, b * BPS + j // 2)
                    act.activation(yT[:, 4 * (j % 2):4 * (j % 2) + 4, :], misc[:, :].rearrange("p (j q) -> p j q", q=P),
                                   ACT.Copy).then_inc(yT_ready, 1)

                def round_values(b):
                    act.wait_ge(v_ready, b * 2 + 2)
                    act.activation(v_high[:, :, :, :], v[:, :, :, :], ACT.Copy).then_inc(v_rounded, 1)

                def pairs(b, last):
                    def exps(n):
                        blk, pr = divmod(n, PAIRS)
                        k, half = divmod(pr, 2)
                        act.wait_ge(maxed, b * NP + n + 1)
                        if n >= 2:
                            act.wait_ge(p_turned, b * NP + n - 1)
                        w = keys(blk)
                        for h in range(2):
                            col = 4 * k + half + 2 * h
                            last = act.activation(probs[:, n % 2, h, 0:w], scores[n % 3][:, h * w:(h + 1) * w], ACT.Exp,
                                                  bias=neg[:, blk, col:col + 1])
                        last.then_inc(probed, 1)
                        if half:
                            act.wait_ge(sink_sum, b * NP // 2 + n // 2 + 1)
                            at = sinks[:, blk, 4 * k:4 * k + 4]
                            act.activation(at, at, ACT.Exp).then_inc(sinks_exp, 1)

                    def round_probs(n):
                        blk = n // PAIRS
                        act.wait_ge(p_turned, b * NP + n + 1)
                        if n >= 2:
                            act.wait_ge(mixed, b * NP + n - 1)
                        m = 2 * keys(blk)
                        act.activation(p_high[:, n % 2, 0:m // P, :], turned[n % 2][:, 0:m].rearrange("p (j q) -> p j q", q=P),
                                       ACT.Copy).then_inc(p_rounded, 1)

                    for n in range(NP + 1):
                        if n < NP:
                            exps(n)
                        if 0 <= n - 1 < NP:
                            round_probs(n - 1)
                        m = n - PAIRS - 4
                        if n < NP and m >= 0 and m % PAIRS < 2:
                            copy_y(b, 2 * (m // PAIRS) + m % PAIRS)
                        if n == NEXT_TURN + 1 and not last:
                            scale_rows(b + 1)

                def tail(b):
                    for j in (2 * BPS - 2, 2 * BPS - 1):
                        copy_y(b, j)

                scale_rows(0)
                round_values(0)
                with act.Fori(0, NB - 1) as b:
                    pairs(b, False)
                    tail(b)
                    round_values(b + 1)
                pairs(NB - 1, True)
                tail(NB - 1)

            @block.tensor
            def _(pe):
                pe.wait_ge(ones, 1)

                def turn_rows(b):
                    pe.wait_ge(normed, b + 1)
                    for j in range(BPS):
                        last = pe.transpose(misc[:, j * P:(j + 1) * P], hn[:, j, :], ident)
                    last.then_inc(hT_turned, 1)

                def turn_y(b, j):
                    blk = j // 2
                    if j % 2 == 0:
                        pe.wait_ge(y_ready, b * NP // 2 + (blk + 1) * PAIRS // 2)
                        if blk:
                            pe.wait_ge(added, b * BPS + blk)
                    else:
                        pe.wait_ge(yT_ready, b * 2 * BPS + j)
                    for q in range(4):
                        ch = 4 * (j % 2) + q
                        last = pe.transpose(misc[:, q * P:(q + 1) * P], y[:, blk % 2, 2 * ch:2 * ch + 2, :].rearrange("p h e -> p (h e)"), ident)
                    last.then_inc(y_turned, 1)

                def project(b, blk):
                    pe.wait_ge(yT_ready, b * 2 * BPS + 2 * blk + 2)
                    for ch in range(QCH):
                        last = pe.matmul(misc[:, 0:D], yT[:, ch, :], g.w_proj[:, ch, :], start=ch == 0, stop=ch == QCH - 1)
                    last.then_inc(projected, 1)

                def products(b, tail):
                    pe.wait_ge(hT_ready, b + 1)
                    for k in range(NCH):
                        if k >= 2:
                            pe.wait_ge(roped_parts, b * NCH + k - 1)
                        elif k == 1 and tail is not None:
                            pe.wait_ge(p_parted, tail * NP + NP)
                        ba, bb = qk_banks[k % 2]
                        ch = ORDER[k]
                        pe.matmul(ba[:, :], g.w_qk[:, ch, :], hT[:, :], start=True, stop=True)
                        pe.matmul(bb[:, :], g.w_rot[:, ch, :], hT[:, :], start=True, stop=True).then_inc(qk_made, 1)
                        if k == 1 and tail is not None:
                            pe.wait_ge(y_ready, tail * NP // 2 + NP // 2)
                        if k in (1, 2):
                            for j in range(2):
                                blk = 2 * (k - 1) + j
                                last = pe.matmul(v_banks[k - 1][:, j * KVH * DH:(j + 1) * KVH * DH], hT[:, blk * P:(blk + 1) * P],
                                                 g.w_v[:, :], start=True, stop=True)
                            last.then_inc(v_made, 1)
                        if tail is not None:
                            if k in (TAIL_TURN, TAIL_TURN + 1):
                                turn_y(tail, 2 * BPS - 2 + k - TAIL_TURN)
                            if k == TAIL_PROJECT:
                                project(tail, BPS - 1)

                def pairs(b, is_last):
                    def score(n):
                        blk, pr = divmod(n, PAIRS)
                        k, half = divmod(pr, 2)
                        if blk == 0 and half == 0:
                            pe.wait_ge(roped, b * NR + adds_through(KCH + 2 * k + 1))
                        if n == 0:
                            pe.wait_ge(roped_parts, b * NCH + NCH - 1)
                        w = keys(blk)
                        bank = scores[n % 3]
                        mask = c.first if blk == 0 else c.band
                        pe.matmul(bank[:, 0:2 * w], ident_bf, mask, start=True, stop=False)
                        kv = 2 * (k >= 2) + half
                        for h in range(2):
                            last = pe.matmul(bank[:, h * w:(h + 1) * w], qT[:, 2 * k + h, blk * P:(blk + 1) * P],
                                             kz[:, kv, (blk + 1) * P - w:(blk + 1) * P], start=False, stop=h == 1)
                        last.then_inc(scored, 1)

                    def turn(n):
                        blk = n // PAIRS
                        pe.wait_ge(probed, b * NP + n + 1)
                        if n >= 2:
                            pe.wait_ge(p_parted, b * NP + n - 1)
                        nk = keys(blk) // P
                        for h in range(2):
                            for j in range(nk):
                                at = (h * nk + j) * P
                                last = pe.transpose(turned[n % 2][:, at:at + P], probs[:, n % 2, h, j * P:(j + 1) * P], ident)
                        last.then_inc(p_turned, 1)

                    def mix(n):
                        blk, pr = divmod(n, PAIRS)
                        k, half = divmod(pr, 2)
                        m = n // 2
                        pe.wait_ge(p_parted, b * NP + n + 1)
                        if n == 0:
                            pe.wait_ge(v_parted, b + 1)
                        if half == 0 and m >= 2:
                            pe.wait_ge(y_ready, b * NP // 2 + m - 1)
                        nk = keys(blk) // P
                        kv = 2 * (k >= 2) + half
                        for h in range(2):
                            q = 2 * h + half
                            for j in range(nk):
                                at = (slice(None), blk - nk + 1 + j, kv, slice(None))
                                for i, (p, vv) in enumerate(((p_high, v_low), (p_low, v_high), (p_high, v_high))):
                                    last = pe.matmul(av[m % 2][:, q * VW:(q + 1) * VW], p[:, n % 2, h * nk + j, :], vv[at],
                                                     start=j == 0 and i == 0, stop=j == nk - 1 and i == 2)
                        last.then_inc(mixed, 1)

                    for n in range(3):
                        score(n)
                    for n in range(NP + 1):
                        if n < NP:
                            turn(n)
                        if n + 3 < NP:
                            score(n + 3)
                        if n >= 1:
                            mix(n - 1)
                        if n == NEXT_TURN and not is_last:
                            turn_rows(b + 1)
                        m = n - PAIRS - 3
                        if m >= 0 and n < NP:
                            if m % PAIRS < 2:
                                if m == 0 and not is_last:
                                    pe.wait_ge(hT_ready, b + 2)
                                turn_y(b, 2 * (m // PAIRS) + m % PAIRS)
                            if m % PAIRS == 2:
                                project(b, m // PAIRS)

                turn_rows(0)
                products(0, None)
                with pe.Fori(0, NB - 1) as b:
                    pairs(b, False)
                    products(b + 1, b)
                pairs(NB - 1, True)
                for j in (2 * BPS - 2, 2 * BPS - 1):
                    turn_y(NB - 1, j)
                project(NB - 1, BPS - 1)


def route(nc, g, S, tag):
    c, r = g.c, g.routing
    with ExitStack() as ctx:
        def sb(name, shape, dt=F32):
            return ctx.enter_context(nc.sbuf_tensor(f"{tag}_{name}", shape, dt))

        hn = sb("rms_rows", [P, NBLK, D])
        hT = sb("rms_T", [P, NBLK * P])
        logit = sb("logits", [P, NBLK, NE])
        top = sb("top", [P, NBLK, 8])
        at8 = sb("top_at", [P, NBLK, 8], U32)
        at = sb("top_at_f", [P, NBLK, 8])
        picked = sb("picked", [P, TOPK, NBLK, NE])
        any16 = sb("picked_any", [P, NBLK, NE], BF16)
        any_a = sb("picked_a", [P, NBLK, NE])
        any_b = sb("picked_b", [P, NBLK, NE])
        e4 = sb("top_exp", [P, NBLK, TOPK])
        esum = sb("top_sum", [P, NBLK])
        count = sb("count", [P, NE, NBLK])
        upto = sb("count_upto", [P, NE, NBLK])
        slot_of = sb("slot_of", [P, NBLK, NE])
        work = sb("work", [P, NBLK, NE])
        ntile_i = sb("ntile_i", [P, NE], I32)
        ntile = sb("ntile", [P, NE])
        tile_end = sb("tile_end", [P, NE])
        base = sb("base", [P, NE])
        slot_f = sb("slot_f", [P, NBLK, TOPK])
        hi_i, lo_i = sb("slot_hi_i", [P, NBLK * TOPK], I32), sb("slot_lo_i", [P, NBLK * TOPK], I32)
        hi, lo = sb("slot_hi", [P, NBLK * TOPK]), sb("slot_lo", [P, NBLK * TOPK])
        RING = 8
        in_tile = sb("in_tile", [P, RING, P], F16)
        of_tile = sb("of_tile", [P, RING, TILES], F16)
        le = sb("ended", [P, NE])
        owner = sb("owner", [P, 1])
        square = sb("square", [P, D])

        chain, squared, rooted = S(tag + "_r_chain"), S(tag + "_r_squared"), S(tag + "_r_sqrt")
        rows_ready, rows_out, turned, hT_ready = (S(tag + "_r_" + n) for n in ("rows", "rows_out", "turned", "hT"))
        gated, chosen, counted, exped = (S(tag + "_r_" + n) for n in ("gated", "chosen", "counted", "exp"))
        hot, mapped, owned, owner_row = (S(tag + "_r_" + n) for n in ("hot", "mapped", "owned", "owner"))
        marks = {}

        with nc.Block() as block:
            @block.scalar
            def _(act):
                for i in range(NBLK):
                    if i:
                        act.wait_ge(squared, i)
                    act.activation(square[:, :], g.u[:, i, :], ACT.Square, accum_out=g.stat.v2[:, i:i + 1]).then_inc(squared, 1)
                act.wait_ge(chain, 1)
                act.activation(g.stat.s[:, :], g.stat.v[:, :], ACT.Sqrt).then_inc(rooted, 1)
                for q in range(4):
                    act.wait_ge(turned, q + 1)
                    act.activation(hT[:, q * 512:(q + 1) * 512], g.bank[q][:, :], ACT.Copy, scale=c.col("ffn_w")).then_inc(hT_ready, 1)
                act.wait_ge(exped, 1)
                act.activation(e4[:, :, :], e4[:, :, :], ACT.Exp).then_inc(exped, 1)

            @block.sync
            def _(sp):
                for q in range(4):
                    sp.wait_ge(rows_ready, q + 1)
                    sp.dma_start(g.rows_dram.rearrange("(i p) d -> p i d", p=P)[:, 4 * q:4 * q + 4, :],
                                 hn[:, 4 * q:4 * q + 4, :]).then_inc(rows_out, 16)
                sp.wait_ge(rows_out, 64)

            @block.tensor
            def _(pe):
                for q in range(4):
                    pe.wait_ge(rows_ready, q + 1)
                    for j in range(4):
                        last = pe.transpose(g.bank[q][:, j * P:(j + 1) * P], hn[:, 4 * q + j, :], c.ident)
                    last.then_inc(turned, 1)
                for i in range(NBLK):
                    if i % 4 == 0:
                        pe.wait_ge(hT_ready, i // 4 + 1)
                    last = pe.matmul(g.bank[4][:, i * NE:(i + 1) * NE], hT[:, i * P:(i + 1) * P], g.gate[:, :], start=True, stop=True)
                last.then_inc(gated, 1)
                pe.wait_ge(chosen, 1)
                flat = any16[:, :, :].rearrange("p i e -> p (i e)")
                pe.matmul(g.bank[5][:, :], c.h("ones"), flat, start=True, stop=True).then_inc(counted, 1)
                pe.matmul(g.bank[6][:, :], c.h("before"), flat, start=True, stop=True).then_inc(counted, 1)
                for m in range(NBLK * TOPK):
                    pe.wait_ge(hot, m + 1)
                    pe.matmul(g.bank[7][:, 0:TILES], in_tile[:, m % RING, :], of_tile[:, m % RING, :],
                              start=m == 0, stop=m == NBLK * TOPK - 1).then_inc(mapped, 1)
                pe.wait_ge(owned, 1)
                pe.matmul(g.bank[0][0:1, 0:P], owner[:, :], c.ident, start=True, stop=True).then_inc(owner_row, 1)

            @block.vector
            def _(dve):
                link = chained(dve, chain)
                st = g.stat
                dve.wait_ge(squared, NBLK)
                link(dve.tensor_scalar(st.v[:, :], st.v2[:, :], 1.0 / D, EPS, ALU.mult, ALU.add))
                dve.wait_ge(rooted, 1)
                y = st.r[:, :]
                link(dve.reciprocal(y, st.s[:, :]))
                link(dve.tensor_tensor(st.t[:, :], y, y, ALU.mult))
                link(dve.tensor_tensor(st.t[:, :], st.t[:, :], st.v[:, :], ALU.mult))
                link(dve.tensor_scalar(st.t[:, :], st.t[:, :], -0.5, 1.5, ALU.mult, ALU.add))
                link(dve.tensor_tensor(y, y, st.t[:, :], ALU.mult))
                for i in range(NBLK):
                    last = dve.tensor_scalar(hn[:, i, :], g.u[:, i, :], st.r[:, i:i + 1], None, ALU.mult)
                    if i % 4 == 3:
                        last.then_inc(rows_ready, 1)
                dve.wait_ge(gated, 1)
                link(dve.tensor_tensor(logit[:, :, :], g.bank[4][:, :].rearrange("p (i e) -> p i e", e=NE),
                                       c.row("gate_b").unsqueeze(1).broadcast_to([P, NBLK, NE]), ALU.add))
                for i in range(NBLK):
                    last = dve.max(top[:, i, :], logit[:, i, :])
                link(last)
                for i in range(NBLK):
                    last = dve.max_index(at8[:, i, :], top[:, i, :], logit[:, i, :])
                link(last)
                dve.tensor_tensor(e4[:, :, :], top[:, :, 0:TOPK], top[:, :, 0:1].broadcast_to([P, NBLK, TOPK]), ALU.subtract).then_inc(exped, 1)
                link(dve.tensor_copy(at[:, :, :], at8[:, :, :]))
                iota = c.f("iota_e").unsqueeze(1).broadcast_to([P, NBLK, NE])
                for k in range(TOPK):
                    last = dve.tensor_tensor(picked[:, k], iota, at[:, :, k:k + 1].broadcast_to([P, NBLK, NE]), ALU.is_equal)
                link(last)
                dve.tensor_tensor(any_a[:, :, :], picked[:, 0], picked[:, 1], ALU.add)
                link(dve.tensor_tensor(any_b[:, :, :], picked[:, 2], picked[:, 3], ALU.add))
                dve.tensor_tensor(any16[:, :, :], any_a[:, :, :], any_b[:, :, :], ALU.add).then_inc(chosen, 1)
                dve.wait_ge(exped, 2)
                link(dve.tensor_reduce(esum[:, :], e4[:, :, :], AX.X, ALU.add))
                link(dve.reciprocal(esum[:, :], esum[:, :]))
                link(dve.tensor_scalar(esum[:, :], esum[:, :], 0.5, None, ALU.mult))
                link(dve.tensor_tensor(r.weight[:, :].rearrange("p (i k) -> p i k", k=TOPK), e4[:, :, :],
                                       esum[:, :].unsqueeze(2).broadcast_to([P, NBLK, TOPK]), ALU.mult))
                dve.wait_ge(counted, 1)
                link(dve.tensor_copy(count[:, :, :].rearrange("p e i -> p i e"), g.bank[5][:, :].rearrange("p (i e) -> p i e", e=NE)))
                flat = lambda t: t[:, :, :].rearrange("p e i -> p (e i)")
                link(dve.tensor_tensor_scan(flat(upto), c.f("scan"), flat(count), 0.0, ALU.mult, ALU.add))
                link(dve.tensor_scalar(ntile_i[:, :], upto[:, :, NBLK - 1], float(P - 1), None, ALU.add))
                link(dve.tensor_scalar(ntile_i[:, :], ntile_i[:, :], 7, None, ALU.arith_shift_right))
                link(dve.tensor_copy(ntile[:, :], ntile_i[:, :]))
                link(dve.tensor_tensor_scan(tile_end[:, :], c.f("iota_t")[:, 1:2].broadcast_to([P, NE]), ntile[:, :], 0.0, ALU.mult, ALU.add))
                link(dve.tensor_tensor(base[:, :], tile_end[:, :], ntile[:, :], ALU.subtract))
                link(dve.tensor_scalar(base[:, :], base[:, :], float(P), None, ALU.mult))
                link(dve.tensor_tensor(flat(upto), flat(upto), flat(count), ALU.subtract))
                dve.wait_ge(counted, 2)
                link(dve.tensor_tensor(slot_of[:, :, :], g.bank[6][:, :].rearrange("p (i e) -> p i e", e=NE),
                                       upto[:, :, :].rearrange("p e i -> p i e"), ALU.add))
                link(dve.tensor_tensor(slot_of[:, :, :], slot_of[:, :, :], base[:, :].unsqueeze(1).broadcast_to([P, NBLK, NE]), ALU.add))
                for k in range(TOPK):
                    link(dve.tensor_tensor(work[:, :, :], picked[:, k], slot_of[:, :, :], ALU.mult))
                    link(dve.tensor_reduce(slot_f[:, :, k:k + 1].rearrange("p i o -> p (i o)"), work[:, :, :], AX.X, ALU.add))
                link(dve.tensor_scalar(le[:, :], tile_end[:, :], c.f("cols")[:, 0:1], None, ALU.is_le))
                link(dve.tensor_reduce(owner[:, :], le[:, :], AX.X, ALU.add))
                dve.tensor_scalar(owner[:, :], owner[:, :], float(NE - 1), None, ALU.min).then_inc(owned, 1)
                link(dve.tensor_copy(r.slot[:, :], slot_f[:, :, :].rearrange("p i k -> p (i k)")))
                si = r.slot[:, :].bitcast(I32)
                dve.tensor_scalar(hi_i[:, :], si, 7, None, ALU.arith_shift_right)
                link(dve.tensor_scalar(lo_i[:, :], si, P - 1, None, ALU.bitwise_and))
                dve.tensor_copy(hi[:, :], hi_i[:, :])
                link(dve.tensor_copy(lo[:, :], lo_i[:, :]))
                for m in range(NBLK * TOPK):
                    i = m // TOPK
                    if m >= RING:
                        dve.wait_ge(mapped, m - RING + 1)
                    dve.tensor_scalar(of_tile[:, m % RING, :], c.iota_t16, hi[:, m:m + 1], c.f("token")[:, i:i + 1], ALU.is_equal, ALU.mult)
                    dve.tensor_scalar(in_tile[:, m % RING, :], c.iota_s16, lo[:, m:m + 1], None, ALU.is_equal).then_inc(hot, 1)
                dve.wait_ge(owner_row, 1)
                dve.tensor_copy(r.owner[:, :], g.bank[0][0:1, 0:P])
                dve.wait_ge(mapped, NBLK * TOPK)
                dve.tensor_copy(r.token[:, :], g.bank[7][:, 0:TILES])


def experts(nc, g, S, tag, before):
    c, r = g.c, g.routing
    U = 8
    DEPTH = 3
    TURNS = TILES // U - 1
    gathered_before = before * TILES // U * 16
    with ExitStack() as ctx:
        def sb(name, shape, dt=F32):
            return ctx.enter_context(nc.sbuf_tensor(f"{tag}_{name}", shape, dt))

        idx = sb("tile_tokens", [P, U], U32)
        fence = sb("tile_fence", [1, 1])
        rows = sb("tile_rows", [P, U, D])
        rowsT = sb("tile_rowsT", [P, 2, P])
        silu = sb("tile_silu", [P, 2, DFF])
        act_rows = sb("tile_act", [P, 2, DFF])
        actT = sb("tile_actT", [P, 2, P])
        y = sb("tile_y", [P, U, D])
        b_rows, b_up, b_act, b_y = g.bank[0:2], g.bank[2:4], g.bank[4:6], g.bank[6:8]
        idx_ready = S(tag + "_e_idx")
        gathered = [S(f"{tag}_e_gathered{j}") for j in range(U)]
        stored = [S(f"{tag}_e_stored{j}") for j in range(U)]
        x_turned, x_ready, upped, silued = (S(tag + "_e_" + n) for n in ("x_turned", "x", "upped", "silu"))
        acted, a_turned, a_ready, downed, y_ready = (S(tag + "_e_" + n) for n in ("acted", "a_turned", "a", "downed", "y"))

        def over_steps(eng, step):
            for s in range(DEPTH + U):
                step(s, s % U, s // U, lambda k, s=s: s - k >= 0)
            with eng.Fori(1, TURNS) as t:
                for j in range(U):
                    step(t * U + (DEPTH + j), (DEPTH + j) % U, t + (DEPTH + j) // U, lambda k: True)
            for s in range(DEPTH + TURNS * U, TILES + DEPTH):
                step(s, s % U, s // U, lambda k, s=s: s - k < TILES)

        with nc.Block() as block:
            @block.gpsimd
            def _(pool):
                def gathers(t, first):
                    for q in range(2):
                        for j in range(4 * q, 4 * q + 4):
                            if not first:
                                pool.wait_ge(gathered[j], t * 16 + gathered_before)
                        pool.tensor_copy(idx[:, 4 * q:4 * q + 4], r.token[:, bass.DynSlice(t * U + 4 * q, 4)]).then_inc(idx_ready, 1)
                        if not first:
                            pool.wait_ge(x_turned, t * U - U + 4 * q + 4)
                        pool.wait_ge(idx_ready, t * 4 + 2 * q + 2)
                        pool.tensor_tensor(fence[:, :], fence[:, :], fence[:, :], ALU.add).then_inc(idx_ready, 1)
                        for j in range(4 * q, 4 * q + 4):
                            pool.indirect_dma_start(out=rows[:, j, :], out_offset=None, in_=g.rows_dram,
                                                    in_offset=bass.IndirectOffsetOnAxis(ap=idx[:, j:j + 1], axis=0)).then_inc(gathered[j], 16)

                pool.memset(fence[:, :], 0.0).then_inc(idx_ready, 1)
                gathers(0, True)
                with pool.Fori(1, TILES // U) as t:
                    gathers(t, False)

            @block.tensor
            def _(pe):
                def step(s, r8, q, on):
                    if on(1):
                        e_up = pe.value_load(r.owner[0:1, bass.DynSlice(s - 1, 1)], min_val=0, max_val=NE - 1)
                    if on(3):
                        e_down = pe.value_load(r.owner[0:1, bass.DynSlice(s - 3, 1)], min_val=0, max_val=NE - 1)
                    if on(0):
                        pe.wait_ge(gathered[r8], q * 16 + 16 + gathered_before)
                        if not (isinstance(s, int) and s < 2):
                            pe.wait_ge(x_ready, s - 1)
                        pe.transpose(b_rows[r8 % 2][:, 0:P], rows[:, r8, :], c.ident).then_inc(x_turned, 1)
                    if on(1):
                        pe.wait_ge(x_ready, s)
                        if not (isinstance(s, int) and s < 3):
                            pe.wait_ge(acted, s - 2)
                        up = g.w_up[:, bass.DynSlice(e_up, 1), :].rearrange("p o f -> p (o f)")
                        pe.matmul(b_up[(r8 - 1) % 2][:, 0:2 * DFF], rowsT[:, (r8 - 1) % 2, :], up, start=True, stop=True).then_inc(upped, 1)
                    if on(2):
                        pe.wait_ge(acted, s - 1)
                        if not (isinstance(s, int) and s < 4):
                            pe.wait_ge(a_ready, s - 3)
                        pe.transpose(b_act[r8 % 2][:, 0:P], act_rows[:, r8 % 2, :], c.ident).then_inc(a_turned, 1)
                    if on(3):
                        pe.wait_ge(a_ready, s - 2)
                        if not (isinstance(s, int) and s < 5):
                            pe.wait_ge(y_ready, s - 4)
                        down = g.w_down[:, bass.DynSlice(e_down, 1), :].rearrange("p o f -> p (o f)")
                        pe.matmul(b_y[(r8 - 3) % 2][:, 0:D], actT[:, (r8 - 3) % 2, :], down, start=True, stop=True).then_inc(downed, 1)

                over_steps(pe, step)

            @block.scalar
            def _(act):
                def step(s, r8, q, on):
                    if on(0):
                        act.wait_ge(x_turned, s + 1)
                        if not (isinstance(s, int) and s < 2):
                            act.wait_ge(upped, s - 1)
                        act.activation(rowsT[:, r8 % 2, :], b_rows[r8 % 2][:, 0:P], ACT.Copy, scale=c.col("ffn_w")).then_inc(x_ready, 1)
                    if on(1):
                        act.wait_ge(upped, s)
                        if not (isinstance(s, int) and s < 3):
                            act.wait_ge(acted, s - 2)
                        act.activation(silu[:, (r8 - 1) % 2, :], b_up[(r8 - 1) % 2][:, DFF:2 * DFF], ACT.Silu).then_inc(silued, 1)

                over_steps(act, step)

            @block.vector
            def _(dve):
                def step(s, r8, q, on):
                    if on(1):
                        dve.wait_ge(silued, s)
                        if not (isinstance(s, int) and s < 3):
                            dve.wait_ge(a_turned, s - 2)
                        k = (r8 - 1) % 2
                        dve.tensor_tensor(act_rows[:, k, :], b_up[k][:, 0:DFF], silu[:, k, :], ALU.mult).then_inc(acted, 1)
                    if on(2):
                        dve.wait_ge(a_turned, s - 1)
                        if not (isinstance(s, int) and s < 4):
                            dve.wait_ge(downed, s - 3)
                        dve.tensor_copy(actT[:, r8 % 2, :], b_act[r8 % 2][:, 0:P]).then_inc(a_ready, 1)
                    if on(3):
                        dve.wait_ge(downed, s - 2)
                        if not (isinstance(s, int) and s - 3 < U):
                            dve.wait_ge(stored[(r8 - 3) % U], (q if r8 >= 3 else q - 1) * 16)
                        dve.tensor_copy(y[:, (r8 - 3) % U, :], b_y[(r8 - 3) % 2][:, 0:D]).then_inc(y_ready, 1)

                over_steps(dve, step)

            @block.sync
            def _(sp):
                with sp.Fori(0, TILES // U) as t:
                    for j in range(U):
                        sp.wait_ge(y_ready, t * U + j + 1)
                        sp.dma_start(g.y_dram[bass.DynSlice((t * U + j) * P, P), :], y[:, j, :]).then_inc(stored[j], 16)
                for j in range(U):
                    sp.wait_ge(stored[j], TILES // U * 16)


def combine(nc, g, S, tag, before):
    r = g.routing
    with ExitStack() as ctx:
        def sb(name, shape, dt=F32):
            return ctx.enter_context(nc.sbuf_tensor(f"{tag}_{name}", shape, dt))

        BLKS = 2
        N = BLKS * TOPK
        fetched_before = before * NBLK // BLKS * 16
        idx = sb("c_slots", [P, N], U32)
        fence = sb("c_fence", [1, 1])
        rows = sb("c_rows", [P, N, D])
        weight = sb("c_weight", [P, N])
        idx_ready, added, started = (S(tag + "_c_" + n) for n in ("idx", "added", "started"))
        fetched = [S(f"{tag}_c_fetched{j}") for j in range(N)]

        with nc.Block() as block:
            @block.gpsimd
            def _(pool):
                def turn(t, first):
                    for q in range(BLKS):
                        if not first:
                            pool.wait_ge(added, t * N - N + TOPK * (q + 1))
                        pool.tensor_copy(idx[:, TOPK * q:TOPK * (q + 1)], r.slot[:, bass.DynSlice(t * N + TOPK * q, TOPK)]).then_inc(idx_ready, 1)
                        pool.wait_ge(idx_ready, t * 2 * BLKS + 2 * q + 2)
                        pool.tensor_tensor(fence[:, :], fence[:, :], fence[:, :], ALU.add).then_inc(idx_ready, 1)
                        for j in range(TOPK * q, TOPK * (q + 1)):
                            pool.indirect_dma_start(out=rows[:, j, :], out_offset=None, in_=g.y_dram,
                                                    in_offset=bass.IndirectOffsetOnAxis(ap=idx[:, j:j + 1], axis=0)).then_inc(fetched[j], 16)

                pool.memset(fence[:, :], 0.0).then_inc(idx_ready, 1)
                turn(0, True)
                with pool.Fori(1, NBLK // BLKS) as t:
                    turn(t, False)

            @block.vector
            def _(dve):
                dve.scalar_tensor_tensor(g.x[:, :, :].rearrange("p i d -> p (i d)"), g.u[:, :, :].rearrange("p i d -> p (i d)"), 0.5,
                                         g.x[:, :, :].rearrange("p i d -> p (i d)"), ALU.mult, ALU.add).then_inc(started, 1)
                dve.wait_ge(started, 1)
                with dve.Fori(0, NBLK // BLKS) as t:
                    for j in range(N):
                        dve.wait_ge(fetched[j], t * 16 + 16 + fetched_before)
                        at = g.x[:, bass.DynSlice(t * BLKS + j // TOPK, 1), :].rearrange("p o d -> p (o d)")
                        dve.scalar_tensor_tensor(at, rows[:, j, :], r.weight[:, bass.DynSlice(t * N + j, 1)], at, ALU.mult, ALU.add).then_inc(added, 1)
                        dve.wait_ge(added, t * N + j + 1)


def setup_attention(nc, g, w, S):
    with ExitStack() as ctx:
        wa = ctx.enter_context(nc.sbuf_tensor("l_wqkv_a", [P, 3 * D], F32))
        ws = ctx.enter_context(nc.sbuf_tensor("l_wqkv_s", [P, 3 * D], F32))
        rows = ctx.enter_context(nc.sbuf_tensor("l_bias_rows", [1, 4, D], F32))
        wide = ctx.enter_context(nc.sbuf_tensor("l_bias_wide", [1, 17, P], F32))
        one = ctx.enter_context(nc.sbuf_tensor("l_one", [1, 1], F32))
        loaded, chain, made, spread, kept = (S("l_setup_" + n) for n in ("loaded", "chain", "made", "spread", "kept"))
        loads = [(wa[:, :], w["L0_attn_Wqkv_a"]), (ws[:, :], w["L0_attn_Wqkv_s"]), (g.w_p[:, :], w["L0_attn_Wp_a"]),
                 (g.w_os[:, :], w["L0_attn_Wo_s"]), (g.w_o[:, :], w["L0_attn_Wo"]), (g.w1[:, :], w["L0_attn_W1"]),
                 (g.w2[:, :, :], w["L0_attn_W2"].rearrange("(c f) d -> f c d", f=P))]
        for k, (name, at) in enumerate((("L0_attn_bqkv_a", 0), ("L0_attn_bqkv_a", D), ("L0_attn_bqkv_s", 0), ("L0_attn_bqkv_s", D))):
            loads.append((rows[:, k, :], w[name][at:at + D].rearrange("(o n) -> o n", o=1)))

        with nc.Block() as block:
            @block.sync
            def _(sp):
                for dst, src in loads:
                    sp.dma_start(dst, src).then_inc(loaded, 16)

            @block.vector
            def _(dve):
                dve.wait_ge(loaded, 16 * len(loads))
                link = chained(dve, chain)
                link(dve.memset(one[:, :], 1.0))
                link(dve.tensor_scalar(wa[:, 0:D], wa[:, 0:D], AE ** -0.5, None, ALU.mult))
                link(dve.tensor_scalar(ws[:, 0:D], ws[:, 0:D], AE ** -0.5, None, ALU.mult))
                link(dve.tensor_scalar(rows[:, 0:3:2, :], rows[:, 0:3:2, :], AE ** -0.5, None, ALU.mult))
                for k, (src, at) in enumerate(((wa, 0), (wa, D), (ws, 0), (ws, D))):
                    for t in range(KDUP):
                        dst = g.w_dup[:, k, :].rearrange("p (h t e) -> p h t e", t=KDUP, e=AE)
                        last = dve.tensor_copy(dst[:, :, t, :], src[:, at:at + D].rearrange("p (h e) -> p h e", e=AE))
                        dst = wide[:, 4 * k:4 * k + 4, :].rearrange("p c (h t e) -> p (c h) t e", t=KDUP, e=AE)
                        last = dve.tensor_copy(dst[:, :, t, :], rows[:, k, :].rearrange("p (h e) -> p h e", e=AE))
                dve.tensor_copy(wide[:, 16, :], rows[:, 2, :])
                dve.tensor_copy(g.w_qs[:, :], ws[:, 0:D])
                dve.tensor_copy(g.w_tok[:, 0:D], ws[:, D:2 * D])
                dve.tensor_copy(g.w_tok[:, D:2 * D], wa[:, 2 * D:])
                link(dve.tensor_copy(g.w_tok[:, 2 * D:], ws[:, 2 * D:]))
                link(dve.tensor_tensor(g.col[:, COLS["bp_a"]:COLS["bp_a"] + 1], g.c.col("bp_a"), g.c.col("bo_s"), ALU.add))
                dve.sem_inc(made, 1)
                dve.wait_ge(spread, 1)
                link(dve.tensor_copy(g.dup_bias[:, 0:17], g.bank[0][:, 0:17]))
                for at, sign in ((0, 1), (4, 2)):
                    dve.tensor_scalar(g.dup_bias[:, 17 + at:21 + at], g.dup_bias[:, at:at + 4], g.c.f("cols")[:, sign:sign + 1],
                                      None, ALU.mult).then_inc(kept, 1)
                dve.tensor_scalar(g.dup_bias[:, 25:34], g.dup_bias[:, 8:17], LIN_ONE - 1.0, None, ALU.add).then_inc(kept, 1)

            @block.tensor
            def _(pe):
                pe.wait_ge(made, 1)
                for k in range(17):
                    last = pe.matmul(g.bank[0][:, k:k + 1], wide[:, k, :], one[:, :], start=True, stop=True)
                last.then_inc(spread, 1)


def window_and_linear(nc, g, S):
    with ExitStack() as ctx:
        def sb(name, shape, dt=F32):
            return ctx.enter_context(nc.sbuf_tensor("l_" + name, shape, dt))

        QA, KA, QS, KS = range(4)
        NCK = 4
        hn = sb("hn", [P, BPS, D])
        xT = sb("xT", [P, SEQ])
        dup = sb("dup", [P, 4, NCK, SEQ], F16)
        own_a = sb("own_a", [P, 4, NCK, SEQ], F16)
        R = 4
        whole = sb("whole", [P, R, SEQ])
        high = sb("high", [P, R, SEQ], F16)
        raised = sb("raised", [P, 2, SEQ])
        floor = sb("floor", [P, 2, SEQ])
        qcT = sb("qcT", [P, SEQ])
        ktok = sb("ktok", [P, BPS, D])
        kz = sb("kz", [P, BPS, D])
        ke = sb("ke", [P, BPS, D])
        kf = sb("kf", [P, 2, D])
        va = sb("va", [P, BPS, AH, AW])
        vs = sb("vs", [P, BPS, AH, AW])
        state = sb("state", [P, BPS - 1, AH * AW])
        probs = sb("probs", [P, 2, 2, 2 * P])
        va_high = sb("va_high", [P, BPS, AH, AW], F16)
        va_low = sb("va_low", [P, BPS, AH, AW], F16)
        p_high = sb("p_high", [P, 2, 4, P], F16)
        p_low = sb("p_low", [P, 2, 4, P], F16)
        fence = sb("fence", [P, 2])
        linT = sb("linT", [P, 2, 4, P])
        neg = sb("neg_max", [P, BPS, PAIRS, 2])
        den = sb("den", [P, 2, AH])
        yy = sb("yy", [P, 2, 2, D])
        yT = sb("yT", [P, 2, P])
        mT = sb("mT", [P, P])
        scores, turned = g.bank[0:2], g.bank[2:4]
        lin_bank, win_out, lin_out, misc = g.bank[4:8]
        zbank = (turned[0], turned[1], lin_bank, win_out)
        tbank = (scores[0], scores[1], lin_out, misc)
        c = g.c
        NP, NQ, NZ, NS = BPS * PAIRS, BPS * 4, 17, 16
        ones, normed, x_turned, x_ready = (S("l_" + n) for n in ("ones", "normed", "x_turned", "x"))
        z_made, z_copied, z_used, q_made = (S("l_" + n) for n in ("z_made", "z_copied", "z_used", "q_made"))
        high_made, dup_v, dup_p, fenced = (S("l_" + n) for n in ("high", "dup_v", "dup_p", "fenced"))
        va_rounded, va_parted, centred = (S("l_" + n) for n in ("va_rounded", "va_parted", "centred"))
        t_made, t_biased, k_exped, t_ready = (S("l_" + n) for n in ("t_made", "t_biased", "k_exped", "t_ready"))
        st_made, st_ready = S("l_st_made"), S("l_st")
        scored, maxed, probed, p_turned = (S("l_" + n) for n in ("scored", "maxed", "probs", "p_turned"))
        p_rounded, p_parted, mixed = (S("l_" + n) for n in ("p_rounded", "p_parted", "mixed"))
        l_scored, l_masked, l_mixed, l_out, w_out = (S("l_" + n) for n in ("l_scored", "l_masked", "l_mixed", "l_out", "w_out"))
        y_turned, yT_ready, m_made, m_ready, projected, added = (
            S("l_" + n) for n in ("y_turned", "yT", "m_made", "m", "projected", "added"))
        chain = S("l_chain")
        zeroed, placed = S("l_zeroed"), S("l_placed")
        CHAIN, NLINK = 12, BPS
        keyed = S("l_keyed")
        NEXT_NORM, NEXT_TURN = 1, 4
        BY_DVE = (1, 3, 5, 7)

        def wait_split(eng, b, k):
            n = sum(i <= k for i in BY_DVE)
            if k in BY_DVE:
                eng.wait_ge(dup_v, b * len(BY_DVE) + n)
            else:
                eng.wait_ge(dup_p, b * (NS - len(BY_DVE)) + k + 1 - n)

        def low_rows(kind):
            return c.f("cols")[:, 1:2] if kind in (QA, QS) else c.f("cols")[:, 2:3]

        def split(eng, k):
            kind, ck = divmod(k, NCK)
            return eng.tensor_tensor(dup[:, kind, ck, :], high[:, k % R, :], whole[:, k % R, :], ALU.add)

        def keys(blk):
            return P if blk == 0 else 2 * P

        def pair_heads(pr):
            j, up = pr % 4, pr // 4
            return j, 2 * up, (8 * up + j, 8 * up + 4 + j)

        with nc.Block() as block:
            @block.vector
            def _(dve):
                dve.memset(va[:, :, :, AE:AW], 1.0).then_inc(ones, 1)
                dve.memset(vs[:, :, :, AE:AW], 1.0).then_inc(ones, 1)

                def rows_norm(b):
                    blks = bass.DynSlice(b * BPS, BPS)
                    dve.tensor_tensor(hn[:, :, :], g.x[:, blks, :],
                                      g.stat.mean[:, blks].unsqueeze(2).broadcast_to([P, BPS, D]), ALU.subtract).then_inc(centred, 1)
                    dve.wait_ge(centred, b + 1)
                    dve.tensor_tensor(hn[:, :, :], hn[:, :, :],
                                      g.stat.rr[:, blks].unsqueeze(2).broadcast_to([P, BPS, D]), ALU.mult).then_inc(normed, 1)

                def token_rows(b, blk):
                    dve.wait_ge(t_made, b * BPS + blk + 1)
                    a = ROWS["bk_s"][0]
                    bank = tbank[blk]
                    for k, dst in ((1, va), (2, vs)):
                        dve.tensor_tensor(dst[:, blk, :, 0:AE], bank[:, k * D:(k + 1) * D].rearrange("p (h e) -> p h e", e=AE),
                                          g.row[:, a + k * D:a + (k + 1) * D].rearrange("p (h e) -> p h e", e=AE), ALU.add)
                    dve.tensor_tensor(kz[:, blk, :], bank[:, 0:D], g.row[:, a:a + D], ALU.add).then_inc(t_biased, 1)

                def token_keys(b, blk):
                    dve.wait_ge(k_exped, b * BPS + blk + 1)
                    i = blk % 2
                    dve.tensor_scalar(kf[:, i, :], kz[:, blk, :], LIN_ONE - 1.0, LIN_ONE - 1.0, ALU.add, ALU.max).then_inc(keyed, 1)
                    dve.wait_ge(keyed, b * NLINK + blk + 1)
                    dve.scalar_tensor_tensor(ktok[:, blk, :], ke[:, blk, :], 1.0, kf[:, i, :], ALU.min, ALU.add).then_inc(t_ready, 1)

                def add_proj(b, blk):
                    dve.wait_ge(projected, b * BPS + blk + 1)
                    at = g.u[:, bass.DynSlice(b * BPS + blk, 1), :].rearrange("p o d -> p (o d)")
                    dve.tensor_tensor(at, misc[:, 0:D], at, ALU.add).then_inc(added, 1)

                def products(b, tail):
                    for k in range(NZ):
                        if k >= 2 * NCK:
                            dve.wait_ge(z_copied, b * NZ + k + 1)
                            i = k % 2
                            dve.tensor_scalar(floor[:, i, :], zbank[k % 4][:, :], g.dup_bias[:, 17 + k:18 + k], LIN_ONE - 1.0,
                                              ALU.add, ALU.max).then_inc(z_used, 1)
                            dve.wait_ge(z_used, b * 9 + k - 8 + 1)
                            if k < NS:
                                wait_split(dve, b, k - R)
                            dst = whole[:, k % R, :] if k < NS else qcT[:, :]
                            dve.scalar_tensor_tensor(dst, raised[:, i, :], 1.0, floor[:, i, :], ALU.min, ALU.add).then_inc(q_made, 1)
                        if k - 1 in BY_DVE:
                            dve.wait_ge(high_made, b * NS + k)
                            dve.wait_ge(z_copied, b * NZ + k)
                            split(dve, k - 1).then_inc(dup_v, 1)
                        if k == 5 and tail is not None:
                            add_proj(tail, BPS - 1)
                        if 5 <= k < 5 + BPS:
                            token_rows(b, k - 5)
                        if 7 <= k < 7 + BPS:
                            token_keys(b, k - 7)
                        if k == 13:
                            dve.wait_ge(va_rounded, b + 1)
                            dve.tensor_tensor(va_low[:, :, :, :], va[:, :, :, :], va_high[:, :, :, :], ALU.subtract).then_inc(va_parted, 1)
                    dve.wait_ge(st_made, b + 1)
                    dve.tensor_tensor(state[:, :, :], misc[:, 0:(BPS - 1) * AH * AW].rearrange("p (m n) -> p m n", n=AH * AW),
                                      c.f("blockdiag").unsqueeze(1).broadcast_to([P, BPS - 1, AH * AW]), ALU.mult).then_inc(st_ready, 1)

                def pairs(b, last):
                    n_link = [0]

                    def link(ins):
                        n_link[0] += 1
                        ins.then_inc(chain, 1)
                        dve.wait_ge(chain, b * CHAIN + n_link[0])

                    def row_max(n):
                        blk, pr = divmod(n, PAIRS)
                        dve.wait_ge(scored, b * NP + n + 1)
                        w = keys(blk)
                        dve.tensor_reduce(neg[:, blk, pr, :], scores[n % 2][:, 0:2 * w].rearrange("p (h k) -> p h k", h=2),
                                          AX.X, ALU.max, negate=True).then_inc(maxed, 1)

                    def part_probs(n):
                        m = 2 * keys(n // PAIRS)
                        dve.wait_ge(p_rounded, b * NP + n + 1)
                        dve.tensor_tensor(p_low[:, n % 2, 0:m // P, :], turned[n % 2][:, 0:m].rearrange("p (j q) -> p j q", q=P),
                                          p_high[:, n % 2, 0:m // P, :], ALU.subtract).then_inc(p_parted, 1)

                    def causal(m):
                        dve.wait_ge(l_scored, b * NQ + m + 1)
                        if m >= 2:
                            dve.wait_ge(l_mixed, b * NQ + m - 1)
                        dve.tensor_tensor(linT[:, m % 2], lin_bank[:, :].rearrange("p (h q) -> p h q", q=P),
                                          c.f("causal_t").unsqueeze(1).broadcast_to([P, 4, P]), ALU.mult).then_inc(l_masked, 1)

                    def outs(blk):
                        i = blk % 2
                        dve.wait_ge(mixed, b * NP + (blk + 1) * PAIRS)
                        if blk >= 2:
                            dve.wait_ge(y_turned, b * BPS + blk - 1)
                        a = win_out[:, 0:AH * AW].rearrange("p (h e) -> p h e", e=AW)
                        link(dve.reciprocal(den[:, 0, :], a[:, :, AE]))
                        dve.tensor_tensor(yy[:, i, 0, :].rearrange("p (h e) -> p h e", e=AE), a[:, :, 0:AE],
                                          den[:, 0, :].unsqueeze(2).broadcast_to([P, AH, AE]), ALU.mult).then_inc(w_out, 1)
                        dve.wait_ge(l_mixed, b * NQ + 4 * blk + 4)
                        a = lin_out[:, 0:AH * AW].rearrange("p (h e) -> p h e", e=AW)
                        link(dve.tensor_scalar(den[:, 1, :], a[:, :, AE], 1e-6, None, ALU.add))
                        link(dve.reciprocal(den[:, 1, :], den[:, 1, :]))
                        dve.tensor_tensor(yy[:, i, 1, :].rearrange("p (h e) -> p h e", e=AE), a[:, :, 0:AE],
                                          den[:, 1, :].unsqueeze(2).broadcast_to([P, AH, AE]), ALU.mult).then_inc(l_out, 1)

                    row_max(0)
                    for n in range(NP + 2):
                        if n + 1 < NP:
                            row_max(n + 1)
                        if 0 <= n - 1 < NP:
                            part_probs(n - 1)
                        if n < NP and n % 2 == 0:
                            causal(n // 2)
                        if n >= PAIRS + 1 and (n - PAIRS - 1) % PAIRS == 0:
                            outs((n - PAIRS - 1) // PAIRS)
                        if n >= PAIRS + 5 and (n - PAIRS - 5) % PAIRS == 0:
                            add_proj(b, (n - PAIRS - 5) // PAIRS)
                        if n == NEXT_NORM and not last:
                            rows_norm(b + 1)
                    assert n_link[0] == CHAIN, n_link[0]

                rows_norm(0)
                products(0, None)
                with dve.Fori(0, NB - 1) as b:
                    pairs(b, False)
                    products(b + 1, b)
                pairs(NB - 1, True)
                add_proj(NB - 1, BPS - 1)

            @block.sync
            def _(sp):
                sp.wait_ge(zeroed, 1)

                def place(b):
                    for k in (2 * NCK - 2, 2 * NCK - 1):
                        wait_split(sp, b, k)
                    for j in range(4):
                        rows = slice(32 * j, 32 * j + 32)
                        sp.dma_start(own_a[rows, j, :, :], dup[rows, KA, :, :]).then_inc(placed, 16)

                place(0)
                with sp.Fori(0, NB - 1) as b:
                    place(b + 1)

            @block.gpsimd
            def _(pool):
                pool.memset(own_a[:, :, :, :], 0.0).then_inc(zeroed, 1)
                pool.memset(fence[:, :], 0.0).then_inc(fenced, 1)
                pool.wait_ge(fenced, 1)

                def splits(b, before):
                    mine = [k for k in range(NS) if k not in BY_DVE]
                    for i, k in enumerate(mine):
                        if i:
                            pool.wait_ge(dup_p, b * len(mine) + i)
                        elif before:
                            pool.wait_ge(dup_p, b * len(mine))
                        if k < 2 * NCK:
                            pool.wait_ge(z_copied, b * NZ + k + 1)
                        else:
                            pool.wait_ge(high_made, b * NS + k + 1)
                        pool.tensor_tensor(fence[:, 0:1], fence[:, 1:2], fence[:, 1:2], ALU.add).then_inc(fenced, 1)
                        split(pool, k).then_inc(dup_p, 1)

                splits(0, False)
                with pool.Fori(0, NB - 1) as b:
                    splits(b + 1, True)

            @block.scalar
            def _(act):

                def scale_rows(b):
                    act.wait_ge(x_turned, b + 1)
                    act.activation(xT[:, :], misc[:, :], ACT.Identity, scale=c.col("g1"), bias=c.col("b1")).then_inc(x_ready, 1)

                def copy_y(b, blk):
                    act.wait_ge(y_turned, b * BPS + blk + 1)
                    act.activation(yT[:, :, :], misc[:, 0:2 * P].rearrange("p (j q) -> p j q", q=P), ACT.Copy).then_inc(yT_ready, 1)

                def copy_m(b, blk):
                    act.wait_ge(m_made, b * BPS + blk + 1)
                    act.activation(mT[:, :], misc[:, 0:P], ACT.Identity, bias=c.col("bp_a")).then_inc(m_ready, 1)

                def products(b, tail):
                    for k in range(NZ):
                        act.wait_ge(z_made, b * NZ + k + 1)
                        bias = g.dup_bias[:, k:k + 1]
                        if k < 2 * NCK:
                            if k >= R:
                                wait_split(act, b, k - R)
                            act.activation(high[:, k % R, :], zbank[k % 4][:, :], ACT.Identity, scale=low_rows(k // NCK),
                                           bias=g.dup_bias[:, 17 + k:18 + k]).then_inc(high_made, 1)
                            act.activation(whole[:, k % R, :], zbank[k % 4][:, :], ACT.Identity, bias=bias).then_inc(z_copied, 1)
                        else:
                            if k >= 10:
                                act.wait_ge(q_made, b * 9 + k - 10 + 1)
                            act.activation(raised[:, k % 2, :], zbank[k % 4][:, :], ACT.Exp, bias=bias).then_inc(z_copied, 1)
                        if k > 2 * NCK:
                            act.wait_ge(q_made, b * 9 + k - 8)
                            wait_split(act, b, k - 1 - R)
                            act.activation(high[:, (k - 1) % R, :], whole[:, (k - 1) % R, :], ACT.Copy,
                                           scale=low_rows((k - 1) // NCK)).then_inc(high_made, 1)
                        if k == 1 and tail is not None:
                            copy_y(tail, BPS - 1)
                        if k == 3 and tail is not None:
                            copy_m(tail, BPS - 1)
                        if 6 <= k < 6 + BPS:
                            blk = k - 6
                            act.wait_ge(t_biased, b * BPS + blk + 1)
                            if blk >= 2:
                                act.wait_ge(t_ready, b * BPS + blk - 1)
                            act.activation(ke[:, blk, :], kz[:, blk, :], ACT.Exp).then_inc(k_exped, 1)
                        if k == 11:
                            act.activation(va_high[:, :, :, :], va[:, :, :, :], ACT.Copy).then_inc(va_rounded, 1)

                def pairs(b, last):
                    def exps(n):
                        blk, pr = divmod(n, PAIRS)
                        act.wait_ge(maxed, b * NP + n + 1)
                        if n >= 2:
                            act.wait_ge(p_turned, b * NP + n - 1)
                        w = keys(blk)
                        for h in range(2):
                            last = act.activation(probs[:, n % 2, h, 0:w], scores[n % 2][:, h * w:(h + 1) * w], ACT.Exp,
                                                  bias=neg[:, blk, pr, h:h + 1])
                        last.then_inc(probed, 1)

                    def round_probs(n):
                        blk = n // PAIRS
                        act.wait_ge(p_turned, b * NP + n + 1)
                        if n >= 2:
                            act.wait_ge(mixed, b * NP + n - 1)
                        m = 2 * keys(blk)
                        act.activation(p_high[:, n % 2, 0:m // P, :], turned[n % 2][:, 0:m].rearrange("p (j q) -> p j q", q=P),
                                       ACT.Copy).then_inc(p_rounded, 1)

                    for n in range(NP + 1):
                        if n < NP:
                            exps(n)
                        if n >= 1:
                            round_probs(n - 1)
                        m = n - PAIRS - 2
                        if n < NP and m >= 0 and m % PAIRS == 0:
                            copy_y(b, m // PAIRS)
                        if n < NP and m >= 0 and m % PAIRS == 1:
                            copy_m(b, m // PAIRS)
                        if n == NEXT_TURN + 1 and not last:
                            scale_rows(b + 1)

                scale_rows(0)
                products(0, None)
                with act.Fori(0, NB - 1) as b:
                    pairs(b, False)
                    products(b + 1, b)
                pairs(NB - 1, True)
                copy_y(NB - 1, BPS - 1)
                copy_m(NB - 1, BPS - 1)

            @block.tensor
            def _(pe):
                pe.wait_ge(ones, 2)

                def turn_rows(b):
                    pe.wait_ge(normed, b + 1)
                    for j in range(BPS):
                        last = pe.transpose(misc[:, j * P:(j + 1) * P], hn[:, j, :], c.ident)
                    last.then_inc(x_turned, 1)

                def turn_y(b, blk):
                    pe.wait_ge(l_out, b * BPS + blk + 1)
                    if blk:
                        pe.wait_ge(added, b * BPS + blk)
                    for q in range(2):
                        last = pe.transpose(misc[:, q * P:(q + 1) * P], yy[:, blk % 2, q, :], c.ident)
                    last.then_inc(y_turned, 1)

                def merge(b, blk):
                    pe.wait_ge(yT_ready, b * BPS + blk + 1)
                    pe.matmul(misc[:, 0:P], g.w_p[:, :], yT[:, 0, :], start=True, stop=False)
                    pe.matmul(misc[:, 0:P], g.w_os[:, :], yT[:, 1, :], start=False, stop=True).then_inc(m_made, 1)

                def project(b, blk):
                    pe.wait_ge(m_ready, b * BPS + blk + 1)
                    pe.matmul(misc[:, 0:D], mT[:, :], g.w_o[:, :], start=True, stop=True).then_inc(projected, 1)

                def products(b, tail):
                    pe.wait_ge(x_ready, b + 1)
                    for k in range(NZ):
                        if tail is not None and k == 0:
                            pe.wait_ge(p_parted, tail * NP + NP)
                        if tail is not None and k == 2:
                            pe.wait_ge(l_masked, tail * NQ + NQ)
                        if 4 <= k < 12:
                            pe.wait_ge(z_copied, b * NZ + k - 3)
                        elif k >= 12:
                            pe.wait_ge(z_used, b * 9 + k - 12 + 1)
                        kind, ck = divmod(k, NCK)
                        lhs = g.w_dup[:, kind, ck * P:(ck + 1) * P] if k < NS else g.w_qs[:, :]
                        pe.matmul(zbank[k % 4][:, :], lhs, xT[:, :], start=True, stop=True).then_inc(z_made, 1)
                        if tail is not None:
                            if k == 1:
                                turn_y(tail, BPS - 1)
                            if k == 3:
                                merge(tail, BPS - 1)
                            if k == 4:
                                project(tail, BPS - 1)
                            if k == 6:
                                pe.wait_ge(added, tail * BPS + BPS)
                        if 3 <= k < 3 + BPS:
                            blk = k - 3
                            pe.matmul(tbank[blk][:, 0:3 * D], xT[:, blk * P:(blk + 1) * P], g.w_tok[:, :], start=True, stop=True).then_inc(t_made, 1)
                    pe.wait_ge(t_ready, b * BPS + BPS)
                    for m in range(BPS - 1):
                        for j in range(m + 1):
                            last = pe.matmul(misc[:, m * AH * AW:(m + 1) * AH * AW], ktok[:, j, :],
                                             vs[:, j].rearrange("p h e -> p (h e)"), start=j == 0, stop=j == m)
                    last.then_inc(st_made, 1)

                def pairs(b, is_last):
                    def score(n):
                        blk, pr = divmod(n, PAIRS)
                        j, ck, _ = pair_heads(pr)
                        if n == 0:
                            pe.wait_ge(placed, b * 64 + 64)
                        w = keys(blk)
                        bank = scores[n % 2]
                        pe.matmul(bank[:, 0:2 * w], c.ident_bf, c.first if blk == 0 else c.h("band_x"), start=True, stop=False)
                        for h in range(2):
                            last = pe.matmul(bank[:, h * w:(h + 1) * w], dup[:, QA, ck + h, blk * P:(blk + 1) * P],
                                             own_a[:, j, ck + h, (blk + 1) * P - w:(blk + 1) * P], start=False, stop=h == 1)
                        last.then_inc(scored, 1)

                    def turn(n):
                        blk = n // PAIRS
                        pe.wait_ge(probed, b * NP + n + 1)
                        if n >= 2:
                            pe.wait_ge(p_parted, b * NP + n - 1)
                        nk = keys(blk) // P
                        for h in range(2):
                            for j in range(nk):
                                at = (h * nk + j) * P
                                last = pe.transpose(turned[n % 2][:, at:at + P], probs[:, n % 2, h, j * P:(j + 1) * P], c.ident)
                        last.then_inc(p_turned, 1)

                    def mix(n):
                        blk, pr = divmod(n, PAIRS)
                        pe.wait_ge(p_parted, b * NP + n + 1)
                        if n == 0:
                            pe.wait_ge(va_parted, b + 1)
                        if pr == 0 and blk:
                            pe.wait_ge(w_out, b * BPS + blk)
                        nk = keys(blk) // P
                        for h, head in enumerate(pair_heads(pr)[2]):
                            for j in range(nk):
                                at = (slice(None), blk - nk + 1 + j, head, slice(None))
                                for i, (p, vv) in enumerate(((p_high, va_low), (p_low, va_high), (p_high, va_high))):
                                    last = pe.matmul(win_out[:, head * AW:(head + 1) * AW], p[:, n % 2, h * nk + j, :], vv[at],
                                                     start=j == 0 and i == 0, stop=j == nk - 1 and i == 2)
                        last.then_inc(mixed, 1)

                    def lin_score(m):
                        blk, j = divmod(m, 4)
                        if m >= 1:
                            pe.wait_ge(l_masked, b * NQ + m)
                        else:
                            wait_split(pe, b, NS - 1)
                        rows = slice(32 * j, 32 * j + 32)
                        cols = slice(blk * P, (blk + 1) * P)
                        for ck in range(4):
                            last = pe.matmul(lin_bank[:, ck * P:(ck + 1) * P], dup[rows, KS, ck, cols], dup[rows, QS, ck, cols],
                                             start=True, stop=True)
                        last.then_inc(l_scored, 1)

                    def lin_mix(m):
                        blk, j = divmod(m, 4)
                        pe.wait_ge(l_masked, b * NQ + m + 1)
                        if j == 0 and blk:
                            pe.wait_ge(l_out, b * BPS + blk)
                            pe.matmul(lin_out[:, 0:AH * AW], qcT[:, blk * P:(blk + 1) * P], state[:, blk - 1, :], start=True, stop=False)
                        for ck in range(4):
                            head = 4 * ck + j
                            last = pe.matmul(lin_out[:, head * AW:(head + 1) * AW], linT[:, m % 2, ck, :], vs[:, blk, head, :],
                                             start=blk == 0, stop=blk == 0 or (ck == 3 and j == 3))
                        last.then_inc(l_mixed, 1)

                    score(0)
                    score(1)
                    pe.wait_ge(st_ready, b + 1)
                    pe.wait_ge(q_made, b * 9 + 9)
                    for n in range(NP + 1):
                        if n < NP:
                            turn(n)
                        if n + 2 < NP:
                            score(n + 2)
                        if n < NP and n % 2 == 0:
                            lin_score(n // 2)
                        if n >= 1:
                            mix(n - 1)
                        if n >= 1 and n % 2 == 1:
                            lin_mix(n // 2)
                        if n == NEXT_TURN and not is_last:
                            turn_rows(b + 1)
                        m = n - PAIRS - 1
                        if m >= 0 and n < NP:
                            if m == 0 and not is_last:
                                pe.wait_ge(x_ready, b + 2)
                            if m % PAIRS == 0:
                                turn_y(b, m // PAIRS)
                            if m % PAIRS == 1:
                                merge(b, m // PAIRS)
                            if m % PAIRS == 2:
                                project(b, m // PAIRS)

                turn_rows(0)
                products(0, None)
                with pe.Fori(0, NB - 1) as b:
                    pairs(b, False)
                    products(b + 1, b)
                pairs(NB - 1, True)
                turn_y(NB - 1, BPS - 1)
                merge(NB - 1, BPS - 1)
                project(NB - 1, BPS - 1)


def mlp(nc, g, S):
    with ExitStack() as ctx:
        def sb(name, shape, dt=F32):
            return ctx.enter_context(nc.sbuf_tensor("m_" + name, shape, dt))

        NCK = DM // P
        hn = sb("hn", [P, BPS, D])
        hT = sb("hT", [P, SEQ])
        mid = sb("mid", [P, NCK, SEQ])
        c = g.c
        start, normed, turned, hT_ready, upped, gelued, downed, added, chain = (
            S("m_" + n) for n in ("start", "normed", "turned", "hT", "upped", "gelu", "downed", "added", "chain"))
        rows, ups, downs = g.bank[0], g.bank[1:5], g.bank[5:7]

        with nc.Block() as block:
            @block.vector
            def _(dve):
                dve.tensor_tensor(g.x[:, :, :], g.x[:, :, :], g.u[:, :, :], ALU.add).then_inc(start, 1)
                dve.wait_ge(start, 1)
                dve.tensor_tensor(g.x[:, :, :], g.x[:, :, :], c.row("b2m").unsqueeze(1).broadcast_to([P, NBLK, D]), ALU.add).then_inc(start, 1)
                dve.wait_ge(start, 2)
                with dve.Fori(0, NB) as b:
                    blks = bass.DynSlice(b * BPS, BPS)
                    dve.tensor_tensor(hn[:, :, :], g.u[:, blks, :],
                                      g.stat.mean[:, blks].unsqueeze(2).broadcast_to([P, BPS, D]), ALU.subtract).then_inc(chain, 1)
                    dve.wait_ge(chain, b + 1)
                    dve.tensor_tensor(hn[:, :, :], hn[:, :, :],
                                      g.stat.r[:, blks].unsqueeze(2).broadcast_to([P, BPS, D]), ALU.mult).then_inc(normed, 1)
                    dve.wait_ge(turned, b + 1)
                    dve.tensor_scalar(hT[:, :], rows[:, :], c.col("gm"), c.col("bm"), ALU.mult, ALU.add).then_inc(hT_ready, 1)
                    for blk in range(BPS):
                        dve.wait_ge(downed, b * BPS + blk + 1)
                        at = g.x[:, bass.DynSlice(b * BPS + blk, 1), :].rearrange("p o d -> p (o d)")
                        dve.tensor_tensor(at, downs[blk % 2][:, 0:D], at, ALU.add).then_inc(added, 1)

            @block.scalar
            def _(act):
                with act.Fori(0, NB) as b:
                    for k in range(NCK):
                        act.wait_ge(upped, b * NCK + k + 1)
                        act.activation(mid[:, k, :], ups[k][:, :], ACT.Gelu, bias=c.col(f"b1m{k}")).then_inc(gelued, 1)

            @block.tensor
            def _(pe):
                with pe.Fori(0, NB) as b:
                    pe.wait_ge(normed, b + 1)
                    for j in range(BPS):
                        last = pe.transpose(rows[:, j * P:(j + 1) * P], hn[:, j, :], c.ident)
                    last.then_inc(turned, 1)
                    pe.wait_ge(hT_ready, b + 1)
                    for k in range(NCK):
                        pe.matmul(ups[k][:, :], g.w1[:, k * P:(k + 1) * P], hT[:, :], start=True, stop=True).then_inc(upped, 1)
                    pe.wait_ge(gelued, b * NCK + NCK)
                    for blk in range(BPS):
                        if blk >= 2:
                            pe.wait_ge(added, b * BPS + blk - 1)
                        for k in range(NCK):
                            last = pe.matmul(downs[blk % 2][:, 0:D], mid[:, k, blk * P:(blk + 1) * P], g.w2[:, k, :],
                                             start=k == 0, stop=k == NCK - 1)
                        last.then_inc(downed, 1)
                    pe.wait_ge(added, b * BPS + BPS)


def build(nc, w, out):
    with ExitStack() as ctx:
        g = Shared()

        def sb(name, shape, dt=F32):
            return ctx.enter_context(nc.sbuf_tensor(name, shape, dt))

        half_sems = {}

        def S(name):
            if name[:3] not in ("f1_", "f2_"):
                return ctx.enter_context(nc.semaphore(name))
            if name[3:] not in half_sems:
                half_sems[name[3:]] = ctx.enter_context(nc.semaphore("ffn_" + name[3:]))
            return half_sems[name[3:]]

        g.x = sb("x", [P, NBLK, D])
        g.u = sb("u", [P, NBLK, D])
        g.w_qk = sb("w_qk", [P, NCH, P])
        g.w_rot = sb("w_rot", [P, NCH, P])
        g.w_v = sb("w_v", [P, KVH * DH])
        g.w_proj = sb("w_proj", [P, QCH, D])
        g.gate = sb("gate", [P, NE])
        g.w_up = sb("w_up", [P, NE, 2 * DFF])
        g.w_down = sb("w_down", [P, NE, D])
        g.w_dup = sb("w_dup", [P, 4, 4 * P])
        g.dup_bias = sb("dup_bias", [P, 34])
        g.w_qs = sb("w_qs", [P, D])
        g.w_tok = sb("w_tok", [P, 3 * D])
        g.w_p = sb("w_p", [P, D])
        g.w_os = sb("w_os", [P, D])
        g.w_o = sb("w_o", [P, D])
        g.w1 = sb("w1", [P, DM])
        g.w2 = sb("w2", [P, DM // P, D])
        g.const = sb("const", [P, NCONST])
        g.const_bf = sb("const_bf", [P, NCONST_BF], BF16)
        g.col = sb("col", [P, NCOL])
        g.row = sb("row", [P, NROW])
        g.neg_sink = sb("neg_sink", [P, HEADS])
        g.qk_bias = sb("qk_bias", [P, 2 * NCH])
        g.bank = [ctx.enter_context(nc.psum_tensor(f"bank{i}", [P, 512], F32)) for i in range(8)]
        st = g.stat = Shared()
        st.six = sb("st_six", [P, NBLK, 6])
        st.mv = sb("st_mv", [P, NBLK, 2])
        st.mean, st.v, st.v2, st.s, st.t, st.r, st.rr = (
            sb("st_" + n, [P, NBLK]) for n in ("mean", "var", "var2", "root", "work", "r", "rr"))

        r = g.routing = Shared()
        r.weight = ctx.enter_context(nc.sbuf_tensor("route_weight", [P, NBLK * TOPK], F32))
        r.slot = ctx.enter_context(nc.sbuf_tensor("route_slot", [P, NBLK * TOPK], U32))
        r.token = ctx.enter_context(nc.sbuf_tensor("route_token", [P, TILES], U32))
        r.owner = ctx.enter_context(nc.sbuf_tensor("route_owner", [1, P], I32))
        iota16 = g.iota16 = sb("iota16", [P, TILES + P], F16)
        g.rows_dram = nc.dram_tensor("rows", (NBLK * P, D), F32, kind="Internal").ap()
        g.y_dram = nc.dram_tensor("expert_rows", (TILES * P, D), F32, kind="Internal").ap()

        def f(name):
            a, b = CONST_F32[name]
            return g.const[:, a:b]

        def h(name):
            a, b = CONST_BF[name]
            return g.const_bf[:, a:b]

        def col(name):
            return g.col[:, COLS[name]:COLS[name] + 1]

        c = g.c = Shared()
        c.ident, c.cos, c.sin = f("ident"), f("cos"), f("sin")
        c.ident_bf, c.band, c.first = h("ident"), h("band"), h("first")
        c.col, c.f, c.h = col, f, h
        c.row = lambda name: g.row[:, ROWS[name][0]:ROWS[name][1]]
        c.row_bv = c.row("bv")
        c.iota_t16, c.iota_s16 = iota16[:, 0:TILES], iota16[:, TILES:TILES + P]

        setup(nc, g, w, S)
        setup_attention(nc, g, w, S)
        for half, tag in enumerate(("f1", "f2")):
            if tag == "f2":
                with nc.Block() as block:
                    @block.gpsimd
                    def _(pool):
                        for name, sem in half_sems.items():
                            if not name.startswith(("e_gathered", "c_fetched")):
                                pool.sem_clear(sem)
            normalise(nc, g, S, tag, g.x, g.u, plus=c.row("proj_b"))
            sink_attention(nc, g, S, tag)
            route(nc, g, S, tag)
            experts(nc, g, S, tag, half)
            combine(nc, g, S, tag, half)
            if tag == "f1":
                normalise(nc, g, S, "l", g.x, g.u, plus=c.row("bo"))
                window_and_linear(nc, g, S)
                normalise(nc, g, S, "m", g.u, None)
                mlp(nc, g, S)
        stored = S("stored")
        with nc.Block() as block:
            @block.sync
            def _(sp):
                sp.dma_start(out.rearrange("b (n p) d -> p (b n) d", p=P), g.x[:, :, :]).then_inc(stored, 16)
                sp.wait_ge(stored, 16)


_INS = ["L0_attn_x", "L0_attn_g1", "L0_attn_b1", "L0_attn_Wqkv_a", "L0_attn_bqkv_a", "L0_attn_Wp_a", "L0_attn_bp_a",
        "L0_attn_Wqkv_s", "L0_attn_bqkv_s", "L0_attn_Wo_s", "L0_attn_bo_s", "L0_attn_Wo", "L0_attn_bo", "L0_attn_gm",
        "L0_attn_bm", "L0_attn_W1", "L0_attn_b1m", "L0_attn_W2", "L0_attn_b2m", "L0_ffn_attn_norm_w",
        "L0_ffn_ffn_norm_w", "L0_ffn_qkv_w", "L0_ffn_qkv_b", "L0_ffn_proj_w", "L0_ffn_proj_b", "L0_ffn_attn_sink",
        "L0_ffn_gate_w", "L0_ffn_gate_b", "L0_ffn_W_up", "L0_ffn_W_down"]


def _constants():
    import numpy as np
    c = np.zeros((P, NCONST), np.float32)

    def put(name, a):
        lo, hi = CONST_F32[name]
        c[:, lo:hi] = a

    p = np.arange(P)
    put("ident", np.eye(P))
    inv = (1.0 / np.float32(150000.0) ** (np.arange(0, DH, 2, dtype=np.float32) / np.float32(DH))).astype(np.float32)
    pos = (np.arange(SEQ, dtype=np.float32) / np.float32(32.0)).astype(np.float32)
    ang = (pos[None, :] * inv[(p % DH) // 2][:, None]).astype(np.float32)
    put("cos", np.cos(ang))
    put("sin", np.sin(ang))
    put("iota_e", np.arange(NE)[None, :])
    put("iota_s", np.arange(P)[None, :])
    put("iota_t", np.arange(TILES)[None, :])
    t = (p % 32) // AE
    put("cols", np.stack([p, -(t >= 2).astype(np.float32), -(t % 2 == 1).astype(np.float32)], 1))
    put("token", p[:, None] + P * np.arange(NBLK)[None, :])
    put("scan", np.tile((np.arange(NBLK) > 0).astype(np.float32), NE)[None, :])
    hd = p // AE
    put("blockdiag", np.repeat(hd[:, None] == np.arange(AH)[None, :], AW, axis=1))
    put("causal_t", (p[:, None] <= p[None, :]))
    h = np.zeros((P, NCONST_BF), np.float32)

    def puth(name, a):
        lo, hi = CONST_BF[name]
        h[:, lo:hi] = a

    big = np.float32(-1e30)
    r, s = p[:, None], p[None, :]
    own = np.where(s <= r, 0, big)
    prev = np.where(s >= r, 0, big)
    prev_x = np.where(s > r, 0, big)
    puth("ident", np.eye(P))
    puth("before", s > r)
    puth("ones", 1.0)
    puth("band", np.concatenate([prev, own, prev, own], 1))
    puth("band_x", np.concatenate([prev_x, own, prev_x, own], 1))
    puth("first", np.concatenate([own, own], 1))
    return c, h


def kernel(**inputs):
    import numpy as _np
    import concourse.bacc as _bacc
    from concourse import mybir as _mybir
    from concourse.bass_utils import run_bass_kernel_spmd as _run

    nc = _bacc.Bacc("TRN2", target_bir_lowering=False, num_devices=1)
    arrays, w = {}, {}
    for name in _INS:
        a = _np.ascontiguousarray(inputs[name])
        arrays[f"in_{name}"] = a
        w[name] = nc.dram_tensor(f"in_{name}", a.shape, _mybir.dt.from_np(a.dtype), kind="ExternalInput").ap()
    for name, a in zip(("const", "const_bf"), _constants()):
        arrays[f"in_{name}"] = a
        w[name] = nc.dram_tensor(f"in_{name}", a.shape, _mybir.dt.from_np(a.dtype), kind="ExternalInput").ap()
    out = nc.dram_tensor("out_0_dram", (NB, SEQ, D), _mybir.dt.float32, kind="ExternalOutput").ap()
    build(nc, w, out)
    r = _run(nc, [arrays], core_ids=[0])
    return r.results[0]["out_0_dram"]
```

```python
from contextlib import ExitStack

import concourse.bass as bass
from concourse import mybir

F32 = mybir.dt.float32
BF16 = mybir.dt.bfloat16
F16 = mybir.dt.float16
I32 = mybir.dt.int32
U32 = mybir.dt.uint32
ALU = mybir.AluOpType
ACT = mybir.ActivationFunctionType
AX = mybir.AxisListType

P = 128
D = 128
NB, SEQ = 4, 512
BPS = SEQ // P
NBLK = NB * BPS
EPS = 1e-5

HEADS, KVH, DH = 16, 4, 64
QCH = HEADS // 2
NCH = QCH + KVH // 2
VW = DH + 1
PAIRS = HEADS // 2
NE, TOPK, DFF = 32, 4, 128
TILES = NBLK * TOPK + NE
AH, AE = 16, 8
AW = AE + 1
GATHERS = 16
COMBINED = 2
DM = 4 * D
KDUP = 4
LIN_ONE = 1.0001

ROWS = {}
_at = 0
for _name, _n in (("bv", KVH * DH), ("proj_b", D), ("gate_b", NE), ("sink", HEADS),
                  ("bk_s", D), ("bv_a", D), ("bv_s", D), ("bo", D), ("b2m", D)):
    ROWS[_name] = (_at, _at + _n)
    _at += _n
NROW = _at
COLS = {n: k for k, n in enumerate(
    ["attn_w", "ffn_w", "g1", "b1", "gm", "bm", "bp_a", "bo_s", "b1m0", "b1m1", "b1m2", "b1m3",
     "q_lo", "k_lo", "part"])}
NCOL = len(COLS)
CONST_F32 = {}
_at = 0
for _name, _n in (("ident", P), ("cos", SEQ), ("sin", SEQ), ("iota_e", NE), ("iota_s", P),
                  ("iota_t", TILES), ("cols", 3), ("token", NBLK), ("scan", NE * NBLK),
                  ("blockdiag", AH * AW), ("causal_t", P)):
    CONST_F32[_name] = (_at, _at + _n)
    _at += _n
NCONST = _at
CONST_BF = {"ident": (0, P), "before": (P, 2 * P), "ones": (2 * P, 3 * P),
            "band": (3 * P, 7 * P), "first": (7 * P, 9 * P), "band_x": (9 * P, 13 * P)}
NCONST_BF = 13 * P


class Shared:
    pass


def chained(eng, sem, start=0):
    count = [start]

    def link(ins):
        count[0] += 1
        ins.then_inc(sem, 1)
        eng.wait_ge(sem, count[0])

    link.count = count
    return link


def setup(nc, g, w, S, stage):
    def sb(name, shape, dt=F32):
        return stage.enter_context(nc.sbuf_tensor("setup_" + name, shape, dt))

    qkb = sb("qk_bias", [NCH, 2, P])
    narrow = sb("bias_narrow", [16, 4, AE])
    wide = sb("bias_wide", [16, P])
    single = sb("bias_single", [1, P])
    masks = sb("masks_f32", [P, NCONST_BF])
    sink = sb("sink", [P, HEADS])
    wa = sb("wqkv_a", [P, 3 * D])
    ws = sb("wqkv_s", [P, 3 * D])
    loaded, loaded_late, chain = (S("setup_" + n) for n in ("loaded", "loaded_late", "chain"))
    ready, spread, kept = (S("setup_" + n) for n in ("ready", "spread", "kept"))
    g.experts_loaded = S("experts_loaded")

    def halves(t):
        half = KVH * DH
        return [(t[:, 0:4, 0:DH], 0), (t[:, 0:4, DH:P], half), (t[:, 4:8, 0:DH], 2 * half),
                (t[:, 4:8, DH:P], 3 * half)]

    def as_row(src):
        return src.rearrange("(o n) -> o n", o=1)

    first = CONST_F32["sin"][1]
    mask_parts = ((CONST_BF["ident"][0], CONST_BF["ident"][1]), (CONST_BF["band"][0], CONST_BF["first"][1]))
    later_parts = ((CONST_BF["before"][0], CONST_BF["ones"][1]), CONST_BF["band_x"])
    loads = [(masks[:, a:b], w["const_bf"][:, a:b]) for a, b in mask_parts]
    loads += [(g.const[:, 0:first], w["const"][:, 0:first]),
             (g.w_qk[:, QCH:NCH, :], w["L0_ffn_qkv_w"][:, HEADS * DH:(HEADS + KVH) * DH].rearrange("d (c e) -> d c e", e=P)),
             (g.x[:, :, :], w["L0_attn_x"].rearrange("b (n p) d -> p (b n) d", p=P))]
    for dst, at in halves(g.w_qk):
        loads.append((dst, w["L0_ffn_qkv_w"][:, at:at + 4 * DH].rearrange("d (c e) -> d c e", e=DH)))
    loads.append((g.w_v[:, :], w["L0_ffn_qkv_w"][:, (HEADS + KVH) * DH:]))
    qb = w["L0_ffn_qkv_b"]
    for k, (c0, lo) in enumerate(((0, 0), (0, DH), (4, 0), (4, DH))):
        loads.append((qkb[c0:c0 + 4, 0, lo:lo + DH], qb[4 * DH * k:4 * DH * (k + 1)].rearrange("(c e) -> c e", e=DH)))
    loads.append((qkb[QCH:NCH, 0, :], qb[HEADS * DH:(HEADS + KVH) * DH].rearrange("(c e) -> c e", e=P)))
    for name, src in (("bv", qb[(HEADS + KVH) * DH:]), ("proj_b", w["L0_ffn_proj_b"]), ("gate_b", w["L0_ffn_gate_b"])):
        a, b = ROWS[name]
        loads.append((g.row[:, a:b], as_row(src).broadcast_to([P, b - a])))
    loads.append((sink[:, :], as_row(w["L0_ffn_attn_sink"]).broadcast_to([P, HEADS])))
    for name, src in (("attn_w", "L0_ffn_attn_norm_w"),):
        loads.append((g.col[:, COLS[name]:COLS[name] + 1], w[src].rearrange("(p o) -> p o", o=1)))

    late = []
    pw = w["L0_ffn_proj_w"]
    for dst, at in ((g.w_proj[0:DH, 0:4, :], 0), (g.w_proj[DH:P, 0:4, :], 256),
                    (g.w_proj[0:DH, 4:8, :], 512), (g.w_proj[DH:P, 4:8, :], 768)):
        late.append((dst, pw[at:at + 256, :].rearrange("(c e) d -> e c d", e=DH)))
    late += [(wa[:, :], w["L0_attn_Wqkv_a"]), (ws[:, :], w["L0_attn_Wqkv_s"])]
    for kind, (name, at) in enumerate((("L0_attn_bqkv_a", 0), ("L0_attn_bqkv_a", D), ("L0_attn_bqkv_s", 0), ("L0_attn_bqkv_s", D))):
        late.append((narrow[4 * kind:4 * kind + 4, :, :], w[name][at:at + D].rearrange("(c h e) -> c h e", h=4, e=AE)))
    late.append((single[:, :], as_row(w["L0_attn_bqkv_s"][0:D])))
    for name, src in (("ffn_w", "L0_ffn_ffn_norm_w"), ("g1", "L0_attn_g1"), ("b1", "L0_attn_b1"), ("gm", "L0_attn_gm"),
                      ("bm", "L0_attn_bm"), ("bp_a", "L0_attn_bp_a"), ("bo_s", "L0_attn_bo_s")):
        late.append((g.col[:, COLS[name]:COLS[name] + 1], w[src].rearrange("(p o) -> p o", o=1)))
    k = COLS["b1m0"]
    for j in range(DM // P):
        late.append((g.col[:, k + j:k + j + 1], w["L0_attn_b1m"][j * P:(j + 1) * P].rearrange("(p o) -> p o", o=1)))
    for name, src in (("bk_s", w["L0_attn_bqkv_s"][D:2 * D]), ("bv_a", w["L0_attn_bqkv_a"][2 * D:]),
                      ("bv_s", w["L0_attn_bqkv_s"][2 * D:]), ("bo", w["L0_attn_bo"]), ("b2m", w["L0_attn_b2m"])):
        a, b = ROWS[name]
        late.append((g.row[:, a:b], as_row(src).broadcast_to([P, b - a])))
    late += [(masks[:, a:b], w["const_bf"][:, a:b]) for a, b in later_parts]
    late += [(g.const[:, first:], w["const"][:, first:])]
    late += [(g.gate[:, :], w["L0_ffn_gate_w"]), (g.w_p[:, :], w["L0_attn_Wp_a"]),
             (g.w_os[:, :], w["L0_attn_Wo_s"]), (g.w_o[:, :], w["L0_attn_Wo"]), (g.w1[:, :], w["L0_attn_W1"]),
             (g.w2[:, :, :], w["L0_attn_W2"].rearrange("(c f) d -> f c d", f=P))]
    last = []
    for half in range(2):
        e0, e1 = half * NE // 2, (half + 1) * NE // 2
        last.append((g.w_up[:, e0:e1, :], w["L0_ffn_W_up"][e0:e1].rearrange("e d f -> d e f")))
        last.append((g.w_down[:, e0:e1, :], w["L0_ffn_W_down"][e0:e1].rearrange("e f d -> f e d")))
    g.experts_loads = 16 * len(last)
    g.loaded_late, g.late_loads = loaded_late, 16 * len(late)
    banks = g.bank
    ident = g.c.ident

    with nc.Block() as block:
        @block.sync
        def _(sp):
            for dst, src in loads[0::2]:
                sp.dma_start(dst, src).then_inc(loaded, 16)

        @block.scalar
        def _(act):
            for dst, src in loads[1::2]:
                act.dma_start(dst, src).then_inc(loaded, 16)

        @block.vector
        def _(dve):
            dve.wait_ge(loaded, 16 * len(loads))
            link = chained(dve, chain)
            for a, b in mask_parts:
                dve.tensor_copy(g.const_bf[:, a:b], masks[:, a:b])
            dve.tensor_scalar(g.w_qk[:, 0:QCH, :], g.w_qk[:, 0:QCH, :], DH ** -0.5, None, ALU.mult)
            a, b = ROWS["sink"]
            for half in range(2):
                for up in range(2):
                    dve.tensor_copy(g.row[:, a + 8 * up + half:a + 8 * up + 8:2],
                                    sink[:, 8 * up + 4 * half:8 * up + 4 * half + 4])
            link(dve.tensor_scalar(qkb[0:QCH, 0, :], qkb[0:QCH, 0, :], DH ** -0.5, None, ALU.mult))
            s = qkb[:, 0, :].rearrange("c (e t) -> c e t", t=2)
            d = qkb[:, 1, :].rearrange("c (e t) -> c e t", t=2)
            dve.tensor_scalar(d[:, :, 0], s[:, :, 1], -1.0, None, ALU.mult)
            dve.tensor_copy(d[:, :, 1], s[:, :, 0]).then_inc(ready, 1)
            s = g.w_qk[:, :, :].rearrange("p c (e t) -> p c e t", t=2)
            d = g.w_rot[:, :, :].rearrange("p c (e t) -> p c e t", t=2)
            dve.tensor_scalar(d[:, :, :, 0], s[:, :, :, 1], -1.0, None, ALU.mult)
            dve.tensor_copy(d[:, :, :, 1], s[:, :, :, 0])
            link(dve.tensor_scalar(g.neg_sink[:, :], g.row[:, a:b], -1.0, None, ALU.mult))
            dve.wait_ge(spread, 1)
            dve.tensor_copy(g.qk_bias[:, :], banks[0][:, 0:2 * NCH]).then_inc(kept, 1)

        @block.tensor
        def _(pe):
            pe.wait_ge(loaded, 16 * len(loads))
            pe.wait_ge(ready, 1)
            for v in range(2):
                last_turn = pe.transpose(banks[0][:, v * NCH:(v + 1) * NCH], qkb[:, v, :], ident[0:NCH, 0:NCH])
            last_turn.then_inc(spread, 1)

    def later():
        chain_before = 2
        with nc.Block() as block:
            @block.vector
            def _(dve):
                dve.wait_ge(loaded_late, 16 * len(late))
                link = chained(dve, chain, chain_before)
                for a, b in later_parts:
                    dve.tensor_copy(g.const_bf[:, a:b], masks[:, a:b])
                dve.tensor_copy(g.iota16[:, 0:TILES], g.const[:, CONST_F32["iota_t"][0]:CONST_F32["iota_t"][1]])
                dve.tensor_copy(g.iota16[:, TILES:TILES + P], g.const[:, CONST_F32["iota_s"][0]:CONST_F32["iota_s"][1]])
                dve.tensor_copy(wide[:, :].rearrange("c (h t e) -> c h t e", t=KDUP, e=AE),
                                narrow[:, :, :].unsqueeze(2).broadcast_to([16, 4, KDUP, AE])).then_inc(ready, 1)
                dve.tensor_scalar(wa[:, 0:D], wa[:, 0:D], AE ** -0.5, None, ALU.mult)
                link(dve.tensor_scalar(ws[:, 0:D], ws[:, 0:D], AE ** -0.5, None, ALU.mult))
                for k, (src, at) in enumerate(((wa, 0), (wa, D), (ws, 0), (ws, D))):
                    dve.tensor_copy(g.w_dup[:, k, :].rearrange("p (h t e) -> p h t e", t=KDUP, e=AE),
                                    src[:, at:at + D].rearrange("p (h e) -> p h e", e=AE).unsqueeze(2).broadcast_to([P, AH, KDUP, AE]))
                dve.tensor_copy(g.w_qs[:, :], ws[:, 0:D])
                dve.tensor_copy(g.w_tok[:, 0:D], ws[:, D:2 * D])
                dve.tensor_copy(g.w_tok[:, D:2 * D], wa[:, 2 * D:])
                dve.tensor_copy(g.w_tok[:, 2 * D:], ws[:, 2 * D:])
                dve.tensor_tensor(g.col[:, COLS["bp_a"]:COLS["bp_a"] + 1], g.c.col("bp_a"), g.c.col("bo_s"), ALU.add)
                dve.wait_ge(spread, 2)
                for a, b in ((0, 4), (8, 12), (16, 17)):
                    dve.tensor_scalar(g.dup_bias[:, a:b], banks[1][:, a:b], AE ** -0.5, None, ALU.mult)
                dve.tensor_copy(g.dup_bias[:, 4:8], banks[1][:, 4:8])
                link(dve.tensor_copy(g.dup_bias[:, 12:16], banks[1][:, 12:16]))
                for at, sign in ((0, 1), (4, 2)):
                    dve.tensor_scalar(g.dup_bias[:, 17 + at:21 + at], g.dup_bias[:, at:at + 4], g.c.f("cols")[:, sign:sign + 1],
                                      None, ALU.mult)
                dve.tensor_scalar(g.dup_bias[:, 25:34], g.dup_bias[:, 8:17], LIN_ONE - 1.0, None, ALU.add).then_inc(kept, 1)

            @block.tensor
            def _(pe):
                pe.wait_ge(loaded_late, 16 * len(late))
                pe.wait_ge(ready, 2)
                pe.transpose(banks[1][:, 0:16], wide[:, :], ident[0:16, 0:16])
                pe.transpose(banks[1][:, 16:17], single[:, :], ident[0:1, 0:1]).then_inc(spread, 1)

    def load_rest(sp):
        for dst, src in late:
            sp.dma_start(dst, src).then_inc(loaded_late, 16)
        for dst, src in last:
            sp.dma_start(dst, src).then_inc(g.experts_loaded, 16)

    return load_rest, later


def residual(pool, g, plus, sem):
    u, wide = g.u[:, :, :], [P, NBLK, D]
    pool.tensor_tensor(u, g.x[:, :, :], g.stat.mean[:, :].unsqueeze(2).broadcast_to(wide), ALU.subtract).then_inc(sem, 1)
    pool.wait_ge(sem, 1)
    pool.tensor_tensor(u, u, g.stat.r[:, :].unsqueeze(2).broadcast_to(wide), ALU.mult).then_inc(sem, 1)
    pool.wait_ge(sem, 2)
    pool.tensor_tensor(u, u, plus.unsqueeze(1).broadcast_to(wide), ALU.add).then_inc(sem, 1)


def normalise(nc, g, S, tag, src):
    st = g.stat
    with ExitStack():
        roots, v_ready, rooted = S(f"{tag}_norm_chain"), S(f"{tag}_norm_var"), S(f"{tag}_norm_sqrt")
        with nc.Block() as block:
            @block.vector
            def _(dve):
                link = chained(dve, roots)
                for i in range(NBLK):
                    last = dve.bn_stats(st.six[:, i, :], src[:, i, :])
                link(last)
                for i in range(NBLK):
                    last = dve.bn_aggr(st.mv[:, i, :], st.six[:, i, :])
                link(last)
                link(dve.tensor_copy(st.mean[:, :], st.mv[:, :, 0]))
                link(dve.tensor_scalar(st.v[:, :], st.mv[:, :, 1], EPS, None, ALU.add))

                def rsqrt(y, v, n):
                    dve.wait_ge(rooted, n)
                    link(dve.reciprocal(y, st.s[:, :]))
                    link(dve.tensor_tensor(st.t[:, :], y, y, ALU.mult))
                    link(dve.tensor_tensor(st.t[:, :], st.t[:, :], v, ALU.mult))
                    link(dve.tensor_scalar(st.t[:, :], st.t[:, :], -0.5, 1.5, ALU.mult, ALU.add))
                    link(dve.tensor_tensor(y, y, st.t[:, :], ALU.mult))

                rsqrt(st.r[:, :], st.v[:, :], 1)
                link(dve.tensor_tensor(st.v2[:, :], st.r[:, :], st.r[:, :], ALU.mult))
                link(dve.tensor_tensor(st.v2[:, :], st.v2[:, :], st.mv[:, :, 1], ALU.mult))
                link(dve.tensor_scalar(st.v2[:, :], st.v2[:, :], EPS, None, ALU.add))
                rsqrt(st.rr[:, :], st.v2[:, :], 2)
                link(dve.tensor_tensor(st.rr[:, :], st.rr[:, :], st.r[:, :], ALU.mult))

            @block.scalar
            def _(act):
                act.wait_ge(roots, 4)
                act.activation(st.s[:, :], st.v[:, :], ACT.Sqrt).then_inc(rooted, 1)
                act.wait_ge(roots, 12)
                act.activation(st.s[:, :], st.v2[:, :], ACT.Sqrt).then_inc(rooted, 1)


def sink_attention(nc, g, S, tag, beside):
    with ExitStack() as ctx:
        def sb(name, shape, dt=F32):
            return ctx.enter_context(nc.sbuf_tensor(f"{tag}_{name}", shape, dt))

        hn = sb("hn", [P, BPS, D])
        hT = sb("hT", [P, SEQ])
        qT = sb("qT", [P, QCH, SEQ])
        kz = sb("kz", [P, KVH, SEQ])
        rope_a = sb("rope_a", [P, 2, SEQ])
        rope_b = sb("rope_b", [P, 2, SEQ])
        v = sb("v", [P, BPS, KVH, VW])
        probs = sb("probs", [P, 2, 2, 2 * P])
        v_high = sb("v_high", [P, BPS, KVH, VW], F16)
        v_low = sb("v_low", [P, BPS, KVH, VW], F16)
        p_high = sb("p_high", [P, 2, 4, P], F16)
        p_low = sb("p_low", [P, 2, 4, P], F16)
        neg = sb("neg_max", [P, BPS, HEADS])
        sinks = sb("sinks", [P, BPS, HEADS])
        den = sb("den", [P, 2, 4])
        y = sb("y", [P, 2, HEADS, DH])
        yT = sb("yT", [P, QCH, P])
        scores = g.bank[0:3]
        turned = g.bank[3:5]
        av = g.bank[5:7]
        misc = g.bank[7]
        c = g.c
        ident, ident_bf = c.ident, c.ident_bf
        NP = BPS * PAIRS
        KCH = NCH - QCH
        ORDER = list(range(QCH, NCH)) + list(range(QCH))
        NR = NCH + KCH

        def adds_through(k):
            return k + 1 + min(k + 1, KCH)

        normed, hT_turned, hT_ready = S(tag + "_normed"), S(tag + "_hT_turned"), S(tag + "_hT")
        qk_made, roped_parts, roped = S(tag + "_qk"), S(tag + "_rope_parts"), S(tag + "_roped")
        v_made, v_ready = S(tag + "_v_made"), S(tag + "_v")
        scored, maxed, probed = S(tag + "_scored"), S(tag + "_maxed"), S(tag + "_probs")
        v_rounded, v_parted = S(tag + "_v_rounded"), S(tag + "_v_parted")
        p_turned, p_rounded, p_parted = S(tag + "_p_turned"), S(tag + "_p_rounded"), S(tag + "_p_parted")
        mixed, sink_sum, sinks_exp, y_ready = S(tag + "_mixed"), S(tag + "_sink_sum"), S(tag + "_sinks"), S(tag + "_y")
        y_turned, yT_ready, projected, added = S(tag + "_y_turned"), S(tag + "_yT"), S(tag + "_proj"), S(tag + "_added")
        chain, ones, zeroed = S(tag + "_chain"), S(tag + "_ones"), S(tag + "_zeroed")
        centred, u_made = S(tag + "_centred"), S(tag + "_u_made")
        qk_banks = (scores[0:2], turned)
        v_banks = (scores[2], av[0])
        NEXT_NORM, NEXT_TURN, TAIL_TURN, TAIL_PROJECT = 1, 4, 2, 4
        CHAIN = 64

        def keys(blk):
            return P if blk == 0 else 2 * P

        with nc.Block() as block:
            @block.vector
            def _(dve):
                dve.memset(v[:, :, :, DH:VW], 1.0).then_inc(ones, 1)

                def rows_norm(b):
                    blks = bass.DynSlice(b * BPS, BPS)
                    dve.tensor_tensor(hn[:, :, :], g.x[:, blks, :],
                                      g.stat.mean[:, blks].unsqueeze(2).broadcast_to([P, BPS, D]), ALU.subtract).then_inc(centred, 1)
                    dve.wait_ge(centred, b + 1)
                    dve.tensor_tensor(hn[:, :, :], hn[:, :, :],
                                      g.stat.rr[:, blks].unsqueeze(2).broadcast_to([P, BPS, D]), ALU.mult).then_inc(normed, 1)

                def add_proj(b, blk):
                    if blk == 0:
                        dve.wait_ge(u_made, 3)
                    dve.wait_ge(projected, b * BPS + blk + 1)
                    at = g.u[:, bass.DynSlice(b * BPS + blk, 1), :].rearrange("p o d -> p (o d)")
                    dve.tensor_tensor(at, misc[:, 0:D], at, ALU.add).then_inc(added, 1)

                def rope(b, tail):
                    for k, ch in enumerate(ORDER):
                        dve.wait_ge(qk_made, b * NCH + k + 1)
                        if k >= 2:
                            dve.wait_ge(roped, b * NR + adds_through(k - 2))
                        ba, bb = qk_banks[k % 2]
                        dve.scalar_tensor_tensor(rope_a[:, k % 2, :], ba[:, :], g.qk_bias[:, ch:ch + 1], c.cos,
                                                 ALU.add, ALU.mult)
                        dve.scalar_tensor_tensor(rope_b[:, k % 2, :], bb[:, :], g.qk_bias[:, NCH + ch:NCH + ch + 1], c.sin,
                                                 ALU.add, ALU.mult).then_inc(roped_parts, 1)
                        if k in (4, 6):
                            h = (k - 4) // 2
                            dve.wait_ge(v_made, b * 2 + h + 1)
                            for j in range(2):
                                last = dve.tensor_tensor(
                                    v[:, 2 * h + j, :, 0:DH],
                                    v_banks[h][:, j * KVH * DH:(j + 1) * KVH * DH].rearrange("p (h e) -> p h e", e=DH),
                                    c.row_bv.rearrange("p (h e) -> p h e", e=DH), ALU.add)
                            last.then_inc(v_ready, 1)
                        if k == TAIL_PROJECT + 1 and tail is not None:
                            add_proj(tail, BPS - 1)
                    dve.wait_ge(v_rounded, b + 1)
                    dve.tensor_tensor(v_low[:, :, :, :], v[:, :, :, :], v_high[:, :, :, :], ALU.subtract).then_inc(v_parted, 1)

                def pairs(b, last):
                    n_link = [0]

                    def link(ins):
                        n_link[0] += 1
                        ins.then_inc(chain, 1)
                        dve.wait_ge(chain, b * CHAIN + n_link[0])

                    def row_max(n):
                        blk, pr = divmod(n, PAIRS)
                        k, half = divmod(pr, 2)
                        dve.wait_ge(scored, b * NP + n + 1)
                        w = keys(blk)
                        at = neg[:, blk, 4 * k + half:4 * k + 4:2]
                        link(dve.tensor_reduce(at, scores[n % 3][:, 0:2 * w].rearrange("p (h k) -> p h k", h=2),
                                               AX.X, ALU.max, negate=True))
                        dve.tensor_tensor(at, at, g.neg_sink[:, 4 * k + half:4 * k + 4:2], ALU.min).then_inc(maxed, 1)
                        if half:
                            dve.wait_ge(maxed, b * NP + n + 1)
                            dve.tensor_tensor(sinks[:, blk, 4 * k:4 * k + 4], neg[:, blk, 4 * k:4 * k + 4],
                                              g.neg_sink[:, 4 * k:4 * k + 4], ALU.subtract).then_inc(sink_sum, 1)

                    def part_probs(n):
                        m = 2 * keys(n // PAIRS)
                        dve.wait_ge(p_rounded, b * NP + n + 1)
                        dve.tensor_tensor(p_low[:, n % 2, 0:m // P, :], turned[n % 2][:, 0:m].rearrange("p (j q) -> p j q", q=P),
                                          p_high[:, n % 2, 0:m // P, :], ALU.subtract).then_inc(p_parted, 1)

                    def heads_out(m):
                        blk, k = divmod(m, PAIRS // 2)
                        dve.wait_ge(mixed, b * NP + 2 * m + 2)
                        dve.wait_ge(sinks_exp, b * NP // 2 + m + 1)
                        if k == 0 and blk >= 2:
                            dve.wait_ge(y_turned, b * 2 * BPS + 2 * (blk - 2) + 2)
                        a4 = av[m % 2][:, 0:4 * VW].rearrange("p (h e) -> p h e", e=VW)
                        d = den[:, m % 2, :]
                        link(dve.tensor_tensor(d, a4[:, :, DH], sinks[:, blk, 4 * k:4 * k + 4], ALU.add))
                        link(dve.reciprocal(d, d))
                        dve.tensor_tensor(y[:, blk % 2, 4 * k:4 * k + 4, :], a4[:, :, 0:DH],
                                          d.unsqueeze(2).broadcast_to([P, 4, DH]), ALU.mult).then_inc(y_ready, 1)

                    row_max(0)
                    for n in range(NP + 2):
                        if n + 1 < NP:
                            row_max(n + 1)
                        if 0 <= n - 1 < NP:
                            part_probs(n - 1)
                        if n >= 3 and (n - 3) % 2 == 0 and (n - 3) // 2 < NP // 2:
                            heads_out((n - 3) // 2)
                        if n >= PAIRS + 6 and (n - PAIRS - 6) % PAIRS == 0:
                            add_proj(b, (n - PAIRS - 6) // PAIRS)
                        if n == NEXT_NORM and not last:
                            rows_norm(b + 1)
                    assert n_link[0] == CHAIN, n_link[0]

                rows_norm(0)
                rope(0, None)
                with dve.Fori(0, NB - 1) as b:
                    pairs(b, False)
                    rope(b + 1, b)
                pairs(NB - 1, True)
                add_proj(NB - 1, BPS - 1)

            @block.sync
            def _(sp):
                if beside is not None:
                    beside(sp)

            @block.gpsimd
            def _(pool):
                pool.memset(kz[:, :, :], 0.0).then_inc(zeroed, 1)
                pool.wait_ge(zeroed, 1)

                def add_rotary(b):
                    for k in range(NCH):
                        pool.wait_ge(roped_parts, b * NCH + k + 1)
                        if k >= KCH:
                            pool.tensor_tensor(qT[:, k - KCH, :], rope_a[:, k % 2, :], rope_b[:, k % 2, :], ALU.add).then_inc(roped, 1)
                            if k == KCH:
                                pool.wait_ge(roped, b * NR + 2 * KCH + 1)
                            continue
                        for half in range(2):
                            lo = half * DH
                            pool.tensor_tensor(kz[lo:lo + DH, 2 * k + half, :], rope_a[lo:lo + DH, k % 2, :],
                                               rope_b[lo:lo + DH, k % 2, :], ALU.add).then_inc(roped, 1)
                            pool.wait_ge(roped, b * NR + 2 * k + half + 1)

                add_rotary(0)
                residual(pool, g, c.row("proj_b"), u_made)
                with pool.Fori(0, NB - 1) as b:
                    add_rotary(b + 1)

            @block.scalar
            def _(act):

                def scale_rows(b):
                    act.wait_ge(hT_turned, b + 1)
                    act.activation(hT[:, :], misc[:, :], ACT.Copy, scale=c.col("attn_w")).then_inc(hT_ready, 1)

                def copy_y(b, j):
                    act.wait_ge(y_turned, b * 2 * BPS + j + 1)
                    if j % 2 == 0 and j >= 2:
                        act.wait_ge(projected, b * BPS + j // 2)
                    act.activation(yT[:, 4 * (j % 2):4 * (j % 2) + 4, :], misc[:, :].rearrange("p (j q) -> p j q", q=P),
                                   ACT.Copy).then_inc(yT_ready, 1)

                def round_values(b):
                    act.wait_ge(v_ready, b * 2 + 2)
                    act.activation(v_high[:, :, :, :], v[:, :, :, :], ACT.Copy).then_inc(v_rounded, 1)

                def pairs(b, last):
                    def exps(n):
                        blk, pr = divmod(n, PAIRS)
                        k, half = divmod(pr, 2)
                        act.wait_ge(maxed, b * NP + n + 1)
                        if n >= 2:
                            act.wait_ge(p_turned, b * NP + n - 1)
                        w = keys(blk)
                        for h in range(2):
                            col = 4 * k + half + 2 * h
                            last = act.activation(probs[:, n % 2, h, 0:w], scores[n % 3][:, h * w:(h + 1) * w], ACT.Exp,
                                                  bias=neg[:, blk, col:col + 1])
                        last.then_inc(probed, 1)
                        if half:
                            act.wait_ge(sink_sum, b * NP // 2 + n // 2 + 1)
                            at = sinks[:, blk, 4 * k:4 * k + 4]
                            act.activation(at, at, ACT.Exp).then_inc(sinks_exp, 1)

                    def round_probs(n):
                        blk = n // PAIRS
                        act.wait_ge(p_turned, b * NP + n + 1)
                        if n >= 2:
                            act.wait_ge(mixed, b * NP + n - 1)
                        m = 2 * keys(blk)
                        act.activation(p_high[:, n % 2, 0:m // P, :], turned[n % 2][:, 0:m].rearrange("p (j q) -> p j q", q=P),
                                       ACT.Copy).then_inc(p_rounded, 1)

                    for n in range(NP + 1):
                        if n < NP:
                            exps(n)
                        if 0 <= n - 1 < NP:
                            round_probs(n - 1)
                        m = n - PAIRS - 4
                        if n < NP and m >= 0 and m % PAIRS < 2:
                            copy_y(b, 2 * (m // PAIRS) + m % PAIRS)
                        if n == NEXT_TURN + 1 and not last:
                            scale_rows(b + 1)

                def tail(b):
                    for j in (2 * BPS - 2, 2 * BPS - 1):
                        copy_y(b, j)

                scale_rows(0)
                round_values(0)
                with act.Fori(0, NB - 1) as b:
                    pairs(b, False)
                    tail(b)
                    round_values(b + 1)
                pairs(NB - 1, True)
                tail(NB - 1)

            @block.tensor
            def _(pe):
                pe.wait_ge(ones, 1)

                def turn_rows(b):
                    pe.wait_ge(normed, b + 1)
                    for j in range(BPS):
                        last = pe.transpose(misc[:, j * P:(j + 1) * P], hn[:, j, :], ident)
                    last.then_inc(hT_turned, 1)

                def turn_y(b, j):
                    blk = j // 2
                    if j % 2 == 0:
                        pe.wait_ge(y_ready, b * NP // 2 + (blk + 1) * PAIRS // 2)
                        if blk:
                            pe.wait_ge(added, b * BPS + blk)
                    else:
                        pe.wait_ge(yT_ready, b * 2 * BPS + j)
                    for q in range(4):
                        ch = 4 * (j % 2) + q
                        last = pe.transpose(misc[:, q * P:(q + 1) * P], y[:, blk % 2, 2 * ch:2 * ch + 2, :].rearrange("p h e -> p (h e)"), ident)
                    last.then_inc(y_turned, 1)

                def project(b, blk):
                    pe.wait_ge(yT_ready, b * 2 * BPS + 2 * blk + 2)
                    for ch in range(QCH):
                        last = pe.matmul(misc[:, 0:D], yT[:, ch, :], g.w_proj[:, ch, :], start=ch == 0, stop=ch == QCH - 1)
                    last.then_inc(projected, 1)

                def products(b, tail):
                    pe.wait_ge(hT_ready, b + 1)
                    for k in range(NCH):
                        if k >= 2:
                            pe.wait_ge(roped_parts, b * NCH + k - 1)
                        elif k == 1 and tail is not None:
                            pe.wait_ge(p_parted, tail * NP + NP)
                        ba, bb = qk_banks[k % 2]
                        ch = ORDER[k]
                        pe.matmul(ba[:, :], g.w_qk[:, ch, :], hT[:, :], start=True, stop=True)
                        pe.matmul(bb[:, :], g.w_rot[:, ch, :], hT[:, :], start=True, stop=True).then_inc(qk_made, 1)
                        if k == 1 and tail is not None:
                            pe.wait_ge(y_ready, tail * NP // 2 + NP // 2)
                        if k in (1, 2):
                            for j in range(2):
                                blk = 2 * (k - 1) + j
                                last = pe.matmul(v_banks[k - 1][:, j * KVH * DH:(j + 1) * KVH * DH], hT[:, blk * P:(blk + 1) * P],
                                                 g.w_v[:, :], start=True, stop=True)
                            last.then_inc(v_made, 1)
                        if tail is not None:
                            if k in (TAIL_TURN, TAIL_TURN + 1):
                                turn_y(tail, 2 * BPS - 2 + k - TAIL_TURN)
                            if k == TAIL_PROJECT:
                                project(tail, BPS - 1)

                def pairs(b, is_last):
                    def score(n):
                        blk, pr = divmod(n, PAIRS)
                        k, half = divmod(pr, 2)
                        if blk == 0 and half == 0:
                            pe.wait_ge(roped, b * NR + adds_through(KCH + 2 * k + 1))
                        if n == 0:
                            pe.wait_ge(roped_parts, b * NCH + NCH - 1)
                        w = keys(blk)
                        bank = scores[n % 3]
                        mask = c.first if blk == 0 else c.band
                        pe.matmul(bank[:, 0:2 * w], ident_bf, mask, start=True, stop=False)
                        kv = 2 * (k >= 2) + half
                        for h in range(2):
                            last = pe.matmul(bank[:, h * w:(h + 1) * w], qT[:, 2 * k + h, blk * P:(blk + 1) * P],
                                             kz[:, kv, (blk + 1) * P - w:(blk + 1) * P], start=False, stop=h == 1)
                        last.then_inc(scored, 1)

                    def turn(n):
                        blk = n // PAIRS
                        pe.wait_ge(probed, b * NP + n + 1)
                        if n >= 2:
                            pe.wait_ge(p_parted, b * NP + n - 1)
                        nk = keys(blk) // P
                        for h in range(2):
                            for j in range(nk):
                                at = (h * nk + j) * P
                                last = pe.transpose(turned[n % 2][:, at:at + P], probs[:, n % 2, h, j * P:(j + 1) * P], ident)
                        last.then_inc(p_turned, 1)

                    def mix(n):
                        blk, pr = divmod(n, PAIRS)
                        k, half = divmod(pr, 2)
                        m = n // 2
                        pe.wait_ge(p_parted, b * NP + n + 1)
                        if n == 0:
                            pe.wait_ge(v_parted, b + 1)
                        if half == 0 and m >= 2:
                            pe.wait_ge(y_ready, b * NP // 2 + m - 1)
                        nk = keys(blk) // P
                        kv = 2 * (k >= 2) + half
                        for h in range(2):
                            q = 2 * h + half
                            for j in range(nk):
                                at = (slice(None), blk - nk + 1 + j, kv, slice(None))
                                for i, (p, vv) in enumerate(((p_high, v_low), (p_low, v_high), (p_high, v_high))):
                                    last = pe.matmul(av[m % 2][:, q * VW:(q + 1) * VW], p[:, n % 2, h * nk + j, :], vv[at],
                                                     start=j == 0 and i == 0, stop=j == nk - 1 and i == 2)
                        last.then_inc(mixed, 1)

                    for n in range(3):
                        score(n)
                    for n in range(NP + 1):
                        if n < NP:
                            turn(n)
                        if n + 3 < NP:
                            score(n + 3)
                        if n >= 1:
                            mix(n - 1)
                        if n == NEXT_TURN and not is_last:
                            turn_rows(b + 1)
                        m = n - PAIRS - 3
                        if m >= 0 and n < NP:
                            if m % PAIRS < 2:
                                if m == 0 and not is_last:
                                    pe.wait_ge(hT_ready, b + 2)
                                turn_y(b, 2 * (m // PAIRS) + m % PAIRS)
                            if m % PAIRS == 2:
                                project(b, m // PAIRS)

                turn_rows(0)
                products(0, None)
                pe.wait_ge(g.loaded_late, g.late_loads)
                with pe.Fori(0, NB - 1) as b:
                    pairs(b, False)
                    products(b + 1, b)
                pairs(NB - 1, True)
                for j in (2 * BPS - 2, 2 * BPS - 1):
                    turn_y(NB - 1, j)
                project(NB - 1, BPS - 1)


def route(nc, g, S, tag):
    c, r = g.c, g.routing
    with ExitStack() as ctx:
        def sb(name, shape, dt=F32):
            return ctx.enter_context(nc.sbuf_tensor(f"{tag}_{name}", shape, dt))

        hn = sb("rms_rows", [P, NBLK, D])
        hT = sb("rms_T", [P, NBLK * P])
        logit = sb("logits", [P, NBLK, NE])
        top = sb("top", [P, NBLK, 8])
        at8 = sb("top_at", [P, NBLK, 8], U32)
        at = sb("top_at_f", [P, NBLK, 8])
        picked = sb("picked", [P, TOPK, NBLK, NE])
        any16 = sb("picked_any", [P, NBLK, NE], BF16)
        any_a = sb("picked_a", [P, NBLK, NE])
        any_b = sb("picked_b", [P, NBLK, NE])
        e4 = sb("top_exp", [P, NBLK, TOPK])
        esum = sb("top_sum", [P, NBLK])
        count = sb("count", [P, NE, NBLK])
        upto = sb("count_upto", [P, NE, NBLK])
        slot_of = sb("slot_of", [P, NBLK, NE])
        work = sb("work", [P, NBLK, NE])
        ntile_i = sb("ntile_i", [P, NE], I32)
        ntile = sb("ntile", [P, NE])
        tile_end = sb("tile_end", [P, NE])
        base = sb("base", [P, NE])
        slot_f = sb("slot_f", [P, NBLK, TOPK])
        hi_i, lo_i = sb("slot_hi_i", [P, NBLK * TOPK], I32), sb("slot_lo_i", [P, NBLK * TOPK], I32)
        hi = sb("slot_hi", [P, NBLK * TOPK])
        RING = 8
        in_tile = sb("in_tile", [P, 2, RING, P], F16)
        away = sb("tiles_away", [P, 2, TILES], F16)
        neg_token = sb("neg_token", [P, NBLK])
        lo16 = sb("slot_lo16", [P, NBLK * TOPK], F16)
        of_tile = sb("of_tile", [P, RING, TILES], F16)
        le = sb("ended", [P, NE])
        owner = sb("owner", [P, 1])
        square = sb("square", [P, 2, D])

        chain, squared, rooted = S(tag + "_r_chain"), S(tag + "_r_squared"), S(tag + "_r_sqrt")
        rows_ready, rows_out, turned, hT_ready = (S(tag + "_r_" + n) for n in ("rows", "rows_out", "turned", "hT"))
        gated, chosen, counted, exped = (S(tag + "_r_" + n) for n in ("gated", "chosen", "counted", "exp"))
        hot, mapped, owned, owner_row = (S(tag + "_r_" + n) for n in ("hot", "mapped", "owned", "owner"))
        located, apart, hot_a = S(tag + "_r_located"), S(tag + "_r_apart"), S(tag + "_r_hot_a")
        squares = S(tag + "_r_squares")

        with nc.Block() as block:
            @block.scalar
            def _(act):
                for i in range(NBLK // 2):
                    if i:
                        act.wait_ge(squared, i)
                    act.activation(square[:, 0, :], g.u[:, i, :], ACT.Square, accum_out=g.stat.v2[:, i:i + 1]).then_inc(squared, 1)
                act.wait_ge(chain, 1)
                act.activation(g.stat.s[:, :], g.stat.v[:, :], ACT.Sqrt).then_inc(rooted, 1)
                for q in range(4):
                    act.wait_ge(turned, q + 1)
                    act.activation(hT[:, q * 512:(q + 1) * 512], g.bank[q][:, :], ACT.Copy, scale=c.col("ffn_w")).then_inc(hT_ready, 1)
                act.wait_ge(exped, 1)
                act.activation(e4[:, :, :], e4[:, :, :], ACT.Exp).then_inc(exped, 1)
                act.wait_ge(located, 1)
                for m in range(3, NBLK * TOPK, 4):
                    i, n = m // TOPK, m // 4
                    if m >= RING:
                        act.wait_ge(mapped, m - RING + 1)
                    act.activation(away[:, n % 2, :], c.iota_t16, ACT.Abs, scale=-1.0, bias=hi[:, m:m + 1]).then_inc(apart, 1)
                    act.wait_ge(apart, n + 1)
                    act.activation(of_tile[:, m % RING, :], away[:, n % 2, :], ACT.Relu, scale=neg_token[:, i:i + 1],
                                   bias=c.f("token")[:, i:i + 1]).then_inc(hot_a, 1)

            @block.sync
            def _(sp):
                for q in range(4):
                    sp.wait_ge(rows_ready, q + 1)
                    sp.dma_start(g.rows_dram.rearrange("(i p) d -> p i d", p=P)[:, 4 * q:4 * q + 4, :],
                                 hn[:, 4 * q:4 * q + 4, :]).then_inc(rows_out, 16)
                sp.wait_ge(rows_out, 64)

            @block.tensor
            def _(pe):
                for q in range(5):
                    if q < 4:
                        pe.wait_ge(rows_ready, q + 1)
                        for j in range(4):
                            last = pe.transpose(g.bank[q][:, j * P:(j + 1) * P], hn[:, 4 * q + j, :], c.ident)
                        last.then_inc(turned, 1)
                    if q >= 1:
                        pe.wait_ge(hT_ready, q)
                        for i in range(4 * q - 4, 4 * q):
                            last = pe.matmul(g.bank[4][:, i * NE:(i + 1) * NE], hT[:, i * P:(i + 1) * P], g.gate[:, :], start=True, stop=True)
                last.then_inc(gated, 1)
                pe.wait_ge(chosen, 1)
                flat = any16[:, :, :].rearrange("p i e -> p (i e)")
                pe.matmul(g.bank[5][:, :], c.h("ones"), flat, start=True, stop=True).then_inc(counted, 1)
                pe.matmul(g.bank[6][:, :], c.h("before"), flat, start=True, stop=True).then_inc(counted, 1)
                for m in range(NBLK * TOPK):
                    if m % 4 == 3:
                        pe.wait_ge(hot_a, m // 4 + 1)
                    else:
                        pe.wait_ge(hot, m - m // 4 + 1)
                    pe.matmul(g.bank[7][:, 0:TILES], in_tile[:, m // RING % 2, m % RING, :], of_tile[:, m % RING, :],
                              start=m == 0, stop=m == NBLK * TOPK - 1).then_inc(mapped, 1)
                pe.wait_ge(owned, 1)
                pe.matmul(g.bank[0][0:1, 0:P], owner[:, :], c.ident, start=True, stop=True).then_inc(owner_row, 1)

            @block.vector
            def _(dve):
                link = chained(dve, chain)
                st = g.stat
                for i in range(NBLK // 2, NBLK):
                    if i > NBLK // 2:
                        dve.wait_ge(squares, i - NBLK // 2)
                    dve.scalar_tensor_tensor(square[:, 1, :], g.u[:, i, :], 1.0, g.u[:, i, :], ALU.mult, ALU.mult,
                                             accum_out=g.stat.v2[:, i:i + 1]).then_inc(squares, 1)
                dve.wait_ge(squared, NBLK // 2)
                dve.wait_ge(squares, NBLK // 2)
                link(dve.tensor_scalar(st.v[:, :], st.v2[:, :], 1.0 / D, EPS, ALU.mult, ALU.add))
                dve.wait_ge(rooted, 1)
                y = st.r[:, :]
                link(dve.reciprocal(y, st.s[:, :]))
                link(dve.tensor_tensor(st.t[:, :], y, y, ALU.mult))
                link(dve.tensor_tensor(st.t[:, :], st.t[:, :], st.v[:, :], ALU.mult))
                link(dve.tensor_scalar(st.t[:, :], st.t[:, :], -0.5, 1.5, ALU.mult, ALU.add))
                link(dve.tensor_tensor(y, y, st.t[:, :], ALU.mult))
                for i in range(NBLK):
                    last = dve.tensor_scalar(hn[:, i, :], g.u[:, i, :], st.r[:, i:i + 1], None, ALU.mult)
                    if i % 4 == 3:
                        last.then_inc(rows_ready, 1)
                dve.wait_ge(gated, 1)
                link(dve.tensor_tensor(logit[:, :, :], g.bank[4][:, :].rearrange("p (i e) -> p i e", e=NE),
                                       c.row("gate_b").unsqueeze(1).broadcast_to([P, NBLK, NE]), ALU.add))
                for i in range(NBLK):
                    last = dve.max(top[:, i, :], logit[:, i, :])
                link(last)
                for i in range(NBLK):
                    last = dve.max_index(at8[:, i, :], top[:, i, :], logit[:, i, :])
                link(last)
                dve.tensor_tensor(e4[:, :, :], top[:, :, 0:TOPK], top[:, :, 0:1].broadcast_to([P, NBLK, TOPK]), ALU.subtract).then_inc(exped, 1)
                link(dve.tensor_copy(at[:, :, :], at8[:, :, :]))
                iota = c.f("iota_e").unsqueeze(1).broadcast_to([P, NBLK, NE])
                for k in range(TOPK):
                    last = dve.tensor_tensor(picked[:, k], iota, at[:, :, k:k + 1].broadcast_to([P, NBLK, NE]), ALU.is_equal)
                link(last)
                dve.tensor_tensor(any_a[:, :, :], picked[:, 0], picked[:, 1], ALU.add)
                link(dve.tensor_tensor(any_b[:, :, :], picked[:, 2], picked[:, 3], ALU.add))
                dve.tensor_tensor(any16[:, :, :], any_a[:, :, :], any_b[:, :, :], ALU.add).then_inc(chosen, 1)
                dve.wait_ge(exped, 2)
                link(dve.tensor_reduce(esum[:, :], e4[:, :, :], AX.X, ALU.add))
                link(dve.reciprocal(esum[:, :], esum[:, :]))
                link(dve.tensor_scalar(esum[:, :], esum[:, :], 0.5, None, ALU.mult))
                link(dve.tensor_tensor(r.weight[:, :].rearrange("p (i k) -> p i k", k=TOPK), e4[:, :, :],
                                       esum[:, :].unsqueeze(2).broadcast_to([P, NBLK, TOPK]), ALU.mult))
                dve.wait_ge(counted, 1)
                link(dve.tensor_copy(count[:, :, :].rearrange("p e i -> p i e"), g.bank[5][:, :].rearrange("p (i e) -> p i e", e=NE)))
                flat = lambda t: t[:, :, :].rearrange("p e i -> p (e i)")
                link(dve.tensor_tensor_scan(flat(upto), c.f("scan"), flat(count), 0.0, ALU.mult, ALU.add))
                link(dve.tensor_scalar(ntile_i[:, :], upto[:, :, NBLK - 1], float(P - 1), None, ALU.add))
                link(dve.tensor_scalar(ntile_i[:, :], ntile_i[:, :], 7, None, ALU.arith_shift_right))
                link(dve.tensor_copy(ntile[:, :], ntile_i[:, :]))
                link(dve.tensor_tensor_scan(tile_end[:, :], c.f("iota_t")[:, 1:2].broadcast_to([P, NE]), ntile[:, :], 0.0, ALU.mult, ALU.add))
                link(dve.tensor_tensor(base[:, :], tile_end[:, :], ntile[:, :], ALU.subtract))
                link(dve.tensor_scalar(base[:, :], base[:, :], float(P), None, ALU.mult))
                link(dve.tensor_tensor(flat(upto), flat(upto), flat(count), ALU.subtract))
                dve.wait_ge(counted, 2)
                link(dve.tensor_tensor(slot_of[:, :, :], g.bank[6][:, :].rearrange("p (i e) -> p i e", e=NE),
                                       upto[:, :, :].rearrange("p e i -> p i e"), ALU.add))
                link(dve.tensor_tensor(slot_of[:, :, :], slot_of[:, :, :], base[:, :].unsqueeze(1).broadcast_to([P, NBLK, NE]), ALU.add))
                for k in range(TOPK):
                    link(dve.tensor_tensor(work[:, :, :], picked[:, k], slot_of[:, :, :], ALU.mult))
                    link(dve.tensor_reduce(slot_f[:, :, k:k + 1].rearrange("p i o -> p (i o)"), work[:, :, :], AX.X, ALU.add))
                link(dve.tensor_scalar(le[:, :], tile_end[:, :], c.f("cols")[:, 0:1], None, ALU.is_le))
                link(dve.tensor_reduce(owner[:, :], le[:, :], AX.X, ALU.add))
                dve.tensor_scalar(owner[:, :], owner[:, :], float(NE - 1), None, ALU.min).then_inc(owned, 1)
                link(dve.tensor_copy(r.slot[:, :], slot_f[:, :, :].rearrange("p i k -> p (i k)")))
                si = r.slot[:, :].bitcast(I32)
                dve.tensor_scalar(hi_i[:, :], si, 7, None, ALU.arith_shift_right)
                link(dve.tensor_scalar(lo_i[:, :], si, P - 1, None, ALU.bitwise_and))
                dve.tensor_copy(hi[:, :], hi_i[:, :])
                dve.tensor_scalar(neg_token[:, :], c.f("token"), -1.0, None, ALU.mult)
                link(dve.tensor_copy(lo16[:, :], lo_i[:, :]))
                dve.sem_inc(located, 1)
                for m in range(NBLK * TOPK):
                    i = m // TOPK
                    if m >= RING and m % 4 != 3:
                        dve.wait_ge(mapped, m - RING + 1)
                    if m % RING == 0:
                        dve.tensor_tensor(in_tile[:, m // RING % 2], c.iota_s16.unsqueeze(1).broadcast_to([P, RING, P]),
                                          lo16[:, m:m + RING].unsqueeze(2).broadcast_to([P, RING, P]), ALU.is_equal)
                    if m % 4 == 3:
                        continue
                    dve.tensor_scalar(of_tile[:, m % RING, :], c.iota_t16, hi[:, m:m + 1], c.f("token")[:, i:i + 1],
                                      ALU.is_equal, ALU.mult).then_inc(hot, 1)
                dve.wait_ge(owner_row, 1)
                dve.tensor_copy(r.owner[:, :], g.bank[0][0:1, 0:P])
                dve.wait_ge(mapped, NBLK * TOPK)
                dve.tensor_copy(r.token[:, :], g.bank[7][:, 0:TILES])


def experts(nc, g, S, tag, before):
    c, r = g.c, g.routing
    U = GATHERS
    YR = 8
    DEPTH = 4
    TURNS = TILES // U - 1
    gathered_before = [before * (TILES // U + (NBLK // COMBINED if j < COMBINED * TOPK else 0)) * 16 for j in range(U)]
    with ExitStack() as ctx:
        def sb(name, shape, dt=F32):
            return ctx.enter_context(nc.sbuf_tensor(f"{tag}_{name}", shape, dt))

        idx = sb("tile_tokens", [P, U], U32)
        fence = sb("tile_fence", [1, 1])
        rows = sb("tile_rows", [P, U, D])
        rowsT = sb("tile_rowsT", [P, 2, P])
        silu = sb("tile_silu", [P, 2, DFF])
        act_rows = sb("tile_act", [P, 4, DFF])
        actT = sb("tile_actT", [P, 2, P])
        y = sb("tile_y", [P, YR, D])
        b_rows, b_up, b_act, b_y = g.bank[0:2], g.bank[2:4], g.bank[4:6], g.bank[6:8]
        idx_ready = S(tag + "_e_idx")
        gathered = [S(f"{tag}_e_gathered{j}") for j in range(U)]
        stored = [S(f"{tag}_e_stored{j}") for j in range(YR)]
        x_turned, x_ready, upped, silued = (S(tag + "_e_" + n) for n in ("x_turned", "x", "upped", "silu"))
        acted, a_turned, a_ready, downed, y_ready = (S(tag + "_e_" + n) for n in ("acted", "a_turned", "a", "downed", "y"))

        def over_steps(eng, step):
            for s in range(DEPTH + U):
                step(s, s % U, s // U, lambda k, s=s: s - k >= 0, s)
            with eng.Fori(1, TURNS) as t:
                for j in range(U):
                    step(t * U + (DEPTH + j), (DEPTH + j) % U, t + (DEPTH + j) // U, lambda k: True, j)
            for s in range(DEPTH + TURNS * U, TILES + DEPTH):
                step(s, s % U, s // U, lambda k, s=s: s - k < TILES, s - DEPTH - TURNS * U)

        with nc.Block() as block:
            @block.gpsimd
            def _(pool):
                def gathers(t, first):
                    for q in range(U // 4):
                        for j in range(4 * q, 4 * q + 4):
                            if not first:
                                pool.wait_ge(gathered[j], t * 16 + gathered_before[j])
                        pool.tensor_copy(idx[:, 4 * q:4 * q + 4], r.token[:, bass.DynSlice(t * U + 4 * q, 4)]).then_inc(idx_ready, 1)
                        if not first:
                            pool.wait_ge(x_turned, t * U - U + 4 * q + 4)
                        pool.wait_ge(idx_ready, t * (U // 2) + 2 * q + 2)
                        pool.tensor_tensor(fence[:, :], fence[:, :], fence[:, :], ALU.add).then_inc(idx_ready, 1)
                        for j in range(4 * q, 4 * q + 4):
                            pool.indirect_dma_start(out=rows[:, j, :], out_offset=None, in_=g.rows_dram,
                                                    in_offset=bass.IndirectOffsetOnAxis(ap=idx[:, j:j + 1], axis=0)).then_inc(gathered[j], 16)

                pool.memset(fence[:, :], 0.0).then_inc(idx_ready, 1)
                gathers(0, True)
                with pool.Fori(1, TILES // U) as t:
                    gathers(t, False)

            @block.tensor
            def _(pe):
                owner = {}

                def read_owners(first, at, n):
                    owner.clear()
                    _, values = nc.values_load_multi_w_load_instructions(
                        r.owner[0:1, bass.DynSlice(at, n)], engines=[mybir.EngineType.PE], min_val=0, max_val=NE - 1,
                        skip_runtime_bounds_check_because="route() leaves a count of at most NE experts, cut to NE - 1")
                    for i, v in enumerate(values):
                        owner[first + i] = v

                def step(s, r8, q, on, n):
                    if n == 0:
                        if isinstance(s, int):
                            read_owners(0, 0, U + DEPTH) if s == 0 else read_owners(-DEPTH, s - DEPTH, TILES + DEPTH - s)
                        else:
                            read_owners(-DEPTH, s - DEPTH, U + DEPTH)
                    if on(1):
                        e_up = owner[n - 1]
                    if on(4):
                        e_down = owner[n - 4]
                    if on(0):
                        pe.wait_ge(gathered[r8], q * 16 + 16 + gathered_before[r8])
                        if not (isinstance(s, int) and s < 2):
                            pe.wait_ge(x_ready, s - 1)
                        pe.transpose(b_rows[r8 % 2][:, 0:P], rows[:, r8, :], c.ident).then_inc(x_turned, 1)
                    if on(1):
                        pe.wait_ge(x_ready, s)
                        if not (isinstance(s, int) and s < 3):
                            pe.wait_ge(acted, s - 2)
                        up = g.w_up[:, bass.DynSlice(e_up, 1), :].rearrange("p o f -> p (o f)")
                        pe.matmul(b_up[(r8 - 1) % 2][:, 0:2 * DFF], rowsT[:, (r8 - 1) % 2, :], up, start=True, stop=True).then_inc(upped, 1)
                    if on(3):
                        pe.wait_ge(acted, s - 2)
                        if not (isinstance(s, int) and s < 5):
                            pe.wait_ge(a_ready, s - 4)
                        pe.transpose(b_act[(r8 - 3) % 2][:, 0:P], act_rows[:, (r8 - 3) % 4, :], c.ident).then_inc(a_turned, 1)
                    if on(4):
                        pe.wait_ge(a_ready, s - 3)
                        if not (isinstance(s, int) and s < 6):
                            pe.wait_ge(y_ready, s - 5)
                        down = g.w_down[:, bass.DynSlice(e_down, 1), :].rearrange("p o f -> p (o f)")
                        pe.matmul(b_y[r8 % 2][:, 0:D], actT[:, r8 % 2, :], down, start=True, stop=True).then_inc(downed, 1)

                if before == 0:
                    pe.wait_ge(g.experts_loaded, g.experts_loads)
                over_steps(pe, step)

            @block.scalar
            def _(act):
                def step(s, r8, q, on, *_):
                    if on(0):
                        act.wait_ge(x_turned, s + 1)
                        if not (isinstance(s, int) and s < 2):
                            act.wait_ge(upped, s - 1)
                        act.activation(rowsT[:, r8 % 2, :], b_rows[r8 % 2][:, 0:P], ACT.Copy, scale=c.col("ffn_w")).then_inc(x_ready, 1)
                    if on(1):
                        act.wait_ge(upped, s)
                        if not (isinstance(s, int) and s < 3):
                            act.wait_ge(acted, s - 2)
                        act.activation(silu[:, (r8 - 1) % 2, :], b_up[(r8 - 1) % 2][:, DFF:2 * DFF], ACT.Silu).then_inc(silued, 1)

                over_steps(act, step)

            @block.vector
            def _(dve):
                def step(s, r8, q, on, *_):
                    if on(3):
                        dve.wait_ge(a_turned, s - 2)
                        if not (isinstance(s, int) and s < 5):
                            dve.wait_ge(downed, s - 4)
                        dve.tensor_copy(actT[:, (r8 - 3) % 2, :], b_act[(r8 - 3) % 2][:, 0:P]).then_inc(a_ready, 1)
                    if on(1):
                        dve.wait_ge(silued, s)
                        if not (isinstance(s, int) and s < 5):
                            dve.wait_ge(a_turned, s - 4)
                        k = (r8 - 1) % 2
                        dve.tensor_tensor(act_rows[:, (r8 - 1) % 4, :], b_up[k][:, 0:DFF], silu[:, k, :], ALU.mult).then_inc(acted, 1)
                    if on(4):
                        dve.wait_ge(downed, s - 3)
                        if not (isinstance(s, int) and s - 4 < YR):
                            dve.wait_ge(stored[(r8 - 4) % YR], (q * (U // YR) + (r8 - 4) // YR) * 16)
                        dve.tensor_copy(y[:, (r8 - 4) % YR, :], b_y[r8 % 2][:, 0:D]).then_inc(y_ready, 1)

                over_steps(dve, step)

            @block.sync
            def _(sp):
                with sp.Fori(0, TILES // YR) as t:
                    for j in range(YR):
                        sp.wait_ge(y_ready, t * YR + j + 1)
                        sp.dma_start(g.y_dram[bass.DynSlice((t * YR + j) * P, P), :], y[:, j, :]).then_inc(stored[j], 16)
                for j in range(YR):
                    sp.wait_ge(stored[j], TILES // YR * 16)


def combine(nc, g, S, tag, before):
    r = g.routing
    with ExitStack() as ctx:
        def sb(name, shape, dt=F32):
            return ctx.enter_context(nc.sbuf_tensor(f"{tag}_{name}", shape, dt))

        BLKS = COMBINED
        N = BLKS * TOPK
        gathers = TILES // GATHERS
        fetched_before = (gathers + before * (gathers + NBLK // BLKS)) * 16
        idx = sb("c_slots", [P, N], U32)
        fence = sb("c_fence", [1, 1])
        rows = sb("c_rows", [P, N, D])
        weight = sb("c_weight", [P, N])
        idx_ready, added, started = (S(tag + "_c_" + n) for n in ("idx", "added", "started"))
        fetched = [S(f"{tag}_e_gathered{j}") for j in range(N)]

        with nc.Block() as block:
            @block.gpsimd
            def _(pool):
                def turn(t, first):
                    for q in range(BLKS):
                        if not first:
                            pool.wait_ge(added, t * N - N + TOPK * (q + 1))
                        pool.tensor_copy(idx[:, TOPK * q:TOPK * (q + 1)], r.slot[:, bass.DynSlice(t * N + TOPK * q, TOPK)]).then_inc(idx_ready, 1)
                        pool.wait_ge(idx_ready, t * 2 * BLKS + 2 * q + 2)
                        pool.tensor_tensor(fence[:, :], fence[:, :], fence[:, :], ALU.add).then_inc(idx_ready, 1)
                        for j in range(TOPK * q, TOPK * (q + 1)):
                            pool.indirect_dma_start(out=rows[:, j, :], out_offset=None, in_=g.y_dram,
                                                    in_offset=bass.IndirectOffsetOnAxis(ap=idx[:, j:j + 1], axis=0)).then_inc(fetched[j], 16)

                pool.memset(fence[:, :], 0.0).then_inc(idx_ready, 1)
                turn(0, True)
                with pool.Fori(1, NBLK // BLKS) as t:
                    turn(t, False)

            @block.vector
            def _(dve):
                dve.scalar_tensor_tensor(g.x[:, :, :].rearrange("p i d -> p (i d)"), g.u[:, :, :].rearrange("p i d -> p (i d)"), 0.5,
                                         g.x[:, :, :].rearrange("p i d -> p (i d)"), ALU.mult, ALU.add).then_inc(started, 1)
                dve.wait_ge(started, 1)
                with dve.Fori(0, NBLK // BLKS) as t:
                    for j in range(N):
                        dve.wait_ge(fetched[j], t * 16 + 16 + fetched_before)
                        at = g.x[:, bass.DynSlice(t * BLKS + j // TOPK, 1), :].rearrange("p o d -> p (o d)")
                        dve.scalar_tensor_tensor(at, rows[:, j, :], r.weight[:, bass.DynSlice(t * N + j, 1)], at, ALU.mult, ALU.add).then_inc(added, 1)
                        dve.wait_ge(added, t * N + j + 1)


def window_and_linear(nc, g, S):
    with ExitStack() as ctx:
        def sb(name, shape, dt=F32):
            return ctx.enter_context(nc.sbuf_tensor("l_" + name, shape, dt))

        r = g.routing
        slots = sb("slots", [P, 2 * TOPK], U32)
        weights = sb("weights", [P, 2 * TOPK])
        fetched_rows = sb("fetched_rows", [P, 2 * TOPK, D])
        six = sb("six", [P, BPS, 6])
        mv = sb("mv", [P, BPS, 2])
        mean = sb("mean", [P, BPS])
        both, roots, inv, work = (sb(n, [P, 2 * BPS]) for n in ("vars", "roots", "inverses", "newton"))
        r1, r2 = sb("r1", [P, BPS]), sb("r2", [P, BPS])
        u_rows = sb("u_rows", [P, BPS, D])
        idx_ready, summed, started = (S("f1_c_" + n) for n in ("idx", "added", "started"))
        fetched = [S(f"f1_e_gathered{j}") for j in range(2 * TOPK)]
        fetched_before = TILES // GATHERS * 16
        FETCH, SUMS, STATS, RES = 3, 5, 13, 5
        stat_chain, var_ready, rooted = S("l_stat_chain"), S("l_vars"), S("l_rooted")
        QA, KA, QS, KS = range(4)
        NCK = 4
        hn = sb("hn", [P, BPS, D])
        xT = sb("xT", [P, SEQ])
        dup = sb("dup", [P, 4, NCK, SEQ], F16)
        own_a = sb("own_a", [P, 4, NCK, SEQ], F16)
        R = 3
        whole = sb("whole", [P, R, SEQ])
        high = sb("high", [P, R, SEQ], F16)
        raised = sb("raised", [P, 2, SEQ])
        floor = sb("floor", [P, 2, SEQ])
        qcT = sb("qcT", [P, SEQ])
        kz = sb("kz", [P, BPS, D])
        ktok = sb("ktok", [P, BPS, D])
        kf = sb("kf", [P, 2, D])
        va = sb("va", [P, BPS, AH, AW])
        vs = sb("vs", [P, BPS, AH, AW])
        state = sb("state", [P, BPS - 1, AH * AW])
        probs = sb("probs", [P, 2, 2, 2 * P])
        va_high = sb("va_high", [P, BPS, AH, AW], F16)
        va_low = sb("va_low", [P, BPS, AH, AW], F16)
        p_high = sb("p_high", [P, 3, 4, P], F16)
        p_low = sb("p_low", [P, 3, 4, P], F16)
        fence = sb("fence", [P, 2])
        linT = sb("linT", [P, 2, 4, P])
        neg = sb("neg_max", [P, BPS, PAIRS, 2])
        den = sb("den", [P, 2, AH])
        yy = sb("yy", [P, 2, 2, D])
        yT = sb("yT", [P, 2, P])
        mT = sb("mT", [P, P])
        scores, turned = g.bank[0:2], g.bank[2:4]
        lin_bank, win_out, lin_out, misc = g.bank[4:8]
        zbank = (turned[0], turned[1], lin_bank, win_out)
        tbank = (scores[0], scores[1], lin_out, misc)
        c = g.c
        NP, NQ, NZ, NS = BPS * PAIRS, BPS * 4, 17, 16
        ones, normed, x_turned, x_ready = (S("l_" + n) for n in ("ones", "normed", "x_turned", "x"))
        z_made, z_copied, z_used, q_made = (S("l_" + n) for n in ("z_made", "z_copied", "z_used", "q_made"))
        high_made, dup_v, dup_p, fenced = (S("l_" + n) for n in ("high", "dup_v", "dup_p", "fenced"))
        va_rounded, va_parted, centred = (S("l_" + n) for n in ("va_rounded", "va_parted", "centred"))
        t_made, t_biased, k_exped, t_ready = (S("l_" + n) for n in ("t_made", "t_biased", "k_exped", "t_ready"))
        st_made, st_ready = S("l_st_made"), S("l_st")
        scored, maxed, probed, p_turned = (S("l_" + n) for n in ("scored", "maxed", "probs", "p_turned"))
        p_rounded, p_parted, mixed = (S("l_" + n) for n in ("p_rounded", "p_parted", "mixed"))
        l_scored, l_masked, l_mixed, l_out, w_out = (S("l_" + n) for n in ("l_scored", "l_masked", "l_mixed", "l_out", "w_out"))
        y_turned, yT_ready, m_made, m_ready, projected, added = (
            S("l_" + n) for n in ("y_turned", "yT", "m_made", "m", "projected", "added"))
        chain = S("l_chain")
        zeroed, placed = S("l_zeroed"), S("l_placed")
        CHAIN, NLINK = 12, BPS
        keyed, u_made = S("l_keyed"), S("l_u_made")
        NEXT_STATS, NEXT_NORM, NEXT_TURN = 29, 31, 32
        BY_DVE = (1, 3, 5, 7)

        def wait_split(eng, b, k):
            n = sum(i <= k for i in BY_DVE)
            if k in BY_DVE:
                eng.wait_ge(dup_v, b * len(BY_DVE) + n)
            else:
                eng.wait_ge(dup_p, b * (NS - len(BY_DVE)) + k + 1 - n)

        def low_rows(kind):
            return c.f("cols")[:, 1:2] if kind in (QA, QS) else c.f("cols")[:, 2:3]

        def split(eng, k):
            kind, ck = divmod(k, NCK)
            return eng.tensor_tensor(dup[:, kind, ck, :], high[:, k % R, :], whole[:, k % R, :], ALU.add)

        def keys(blk):
            return P if blk == 0 else 2 * P

        def pair_heads(pr):
            j, up = pr % 4, pr // 4
            return j, 2 * up, (8 * up + j, 8 * up + 4 + j)

        with nc.Block() as block:
            @block.vector
            def _(dve):
                dve.memset(va[:, :, :, AE:AW], 1.0).then_inc(ones, 1)
                dve.memset(vs[:, :, :, AE:AW], 1.0).then_inc(ones, 1)

                def statistics(b):
                    n_link = [0]

                    def link(ins):
                        n_link[0] += 1
                        ins.then_inc(stat_chain, 1)
                        dve.wait_ge(stat_chain, b * STATS + n_link[0])

                    def stand():
                        return dve.tensor_copy(work[:, 0:1], c.f("cols")[:, 0:1])

                    dve.wait_ge(summed, b * (BPS * SUMS) + BPS * SUMS)
                    link(stand())
                    if not isinstance(b, int):
                        dve.wait_ge(u_made, b * RES)
                    link(stand())
                    for i in range(BPS):
                        last = dve.bn_stats(six[:, i, :], g.x[:, bass.DynSlice(b * BPS + i, 1), :].rearrange("p o d -> p (o d)"))
                    link(last)
                    stand()
                    for i in range(BPS):
                        last = dve.bn_aggr(mv[:, i, :], six[:, i, :])
                    link(last)
                    dve.tensor_copy(mean[:, :], mv[:, :, 0])
                    link(dve.tensor_scalar(both[:, 0:BPS], mv[:, :, 1], EPS, None, ALU.add))
                    link(dve.reciprocal(both[:, BPS:], both[:, 0:BPS]))
                    link(dve.tensor_tensor(both[:, BPS:], both[:, BPS:], mv[:, :, 1], ALU.mult))
                    dve.tensor_scalar(both[:, BPS:], both[:, BPS:], EPS, None, ALU.add).then_inc(var_ready, 1)
                    dve.wait_ge(rooted, b + 1)
                    link(dve.reciprocal(inv[:, :], roots[:, :]))
                    link(dve.tensor_tensor(work[:, :], inv[:, :], inv[:, :], ALU.mult))
                    link(dve.tensor_tensor(work[:, :], work[:, :], both[:, :], ALU.mult))
                    link(dve.tensor_scalar(work[:, :], work[:, :], -0.5, 1.5, ALU.mult, ALU.add))
                    link(dve.tensor_tensor(inv[:, :], inv[:, :], work[:, :], ALU.mult))
                    dve.tensor_copy(r1[:, :], inv[:, 0:BPS])
                    link(dve.tensor_tensor(r2[:, :], inv[:, 0:BPS], inv[:, BPS:], ALU.mult))
                    assert n_link[0] == STATS, n_link[0]

                def rows_norm(b):
                    dve.tensor_tensor(hn[:, :, :], g.x[:, bass.DynSlice(b * BPS, BPS), :],
                                      mean[:, :].unsqueeze(2).broadcast_to([P, BPS, D]), ALU.subtract).then_inc(centred, 1)
                    dve.wait_ge(centred, b + 1)
                    dve.tensor_tensor(hn[:, :, :], hn[:, :, :],
                                      r2[:, :].unsqueeze(2).broadcast_to([P, BPS, D]), ALU.mult).then_inc(normed, 1)

                def token_rows(b, blk):
                    dve.wait_ge(t_made, b * BPS + blk + 1)
                    a = ROWS["bk_s"][0]
                    bank = tbank[blk]
                    for k, dst in ((1, va), (2, vs)):
                        dve.tensor_tensor(dst[:, blk, :, 0:AE], bank[:, k * D:(k + 1) * D].rearrange("p (h e) -> p h e", e=AE),
                                          g.row[:, a + k * D:a + (k + 1) * D].rearrange("p (h e) -> p h e", e=AE), ALU.add)
                    dve.tensor_tensor(kz[:, blk, :], bank[:, 0:D], g.row[:, a:a + D], ALU.add).then_inc(t_biased, 1)

                def token_keys(b, blk):
                    dve.wait_ge(k_exped, b * BPS + blk + 1)
                    i = blk % 2
                    dve.tensor_scalar(kf[:, i, :], kz[:, blk, :], LIN_ONE - 1.0, LIN_ONE - 1.0, ALU.add, ALU.max).then_inc(keyed, 1)
                    dve.wait_ge(keyed, b * NLINK + blk + 1)
                    dve.scalar_tensor_tensor(ktok[:, blk, :], ktok[:, blk, :], 1.0, kf[:, i, :], ALU.min, ALU.add).then_inc(t_ready, 1)

                def add_proj(b, blk):
                    if blk == 0:
                        dve.wait_ge(u_made, b * RES + RES)
                    dve.wait_ge(projected, b * BPS + blk + 1)
                    at = g.u[:, bass.DynSlice(b * BPS + blk, 1), :].rearrange("p o d -> p (o d)")
                    dve.tensor_tensor(at, misc[:, 0:D], at, ALU.add).then_inc(added, 1)

                def products(b, tail):
                    for k in range(NZ):
                        if k >= 2 * NCK:
                            dve.wait_ge(z_copied, b * NZ + k + 1)
                            i = k % 2
                            dve.tensor_scalar(floor[:, i, :], zbank[k % 4][:, :], g.dup_bias[:, 17 + k:18 + k], LIN_ONE - 1.0,
                                              ALU.add, ALU.max).then_inc(z_used, 1)
                            dve.wait_ge(z_used, b * 9 + k - 8 + 1)
                            if k < NS:
                                wait_split(dve, b, k - R)
                            dst = whole[:, k % R, :] if k < NS else qcT[:, :]
                            dve.scalar_tensor_tensor(dst, raised[:, i, :], 1.0, floor[:, i, :], ALU.min, ALU.add).then_inc(q_made, 1)
                        if k - 1 in BY_DVE:
                            dve.wait_ge(high_made, b * NS + k)
                            dve.wait_ge(z_copied, b * NZ + k)
                            split(dve, k - 1).then_inc(dup_v, 1)
                        if k == 5 and tail is not None:
                            add_proj(tail, BPS - 1)
                        if 5 <= k < 5 + BPS:
                            token_rows(b, k - 5)
                        if 7 <= k < 7 + BPS:
                            token_keys(b, k - 7)
                        if k == 13:
                            dve.wait_ge(va_rounded, b + 1)
                            dve.tensor_tensor(va_low[:, :, :, :], va[:, :, :, :], va_high[:, :, :, :], ALU.subtract).then_inc(va_parted, 1)
                    dve.wait_ge(st_made, b + 1)
                    dve.tensor_tensor(state[:, :, :], misc[:, 0:(BPS - 1) * AH * AW].rearrange("p (m n) -> p m n", n=AH * AW),
                                      c.f("blockdiag").unsqueeze(1).broadcast_to([P, BPS - 1, AH * AW]), ALU.mult).then_inc(st_ready, 1)

                def pairs(b, last):
                    n_link = [0]

                    def link(ins):
                        n_link[0] += 1
                        ins.then_inc(chain, 1)
                        dve.wait_ge(chain, b * CHAIN + n_link[0])

                    def row_max(n):
                        blk, pr = divmod(n, PAIRS)
                        dve.wait_ge(scored, b * NP + n + 1)
                        w = keys(blk)
                        dve.tensor_reduce(neg[:, blk, pr, :], scores[n % 2][:, 0:2 * w].rearrange("p (h k) -> p h k", h=2),
                                          AX.X, ALU.max, negate=True).then_inc(maxed, 1)

                    def part_probs(n):
                        m = 2 * keys(n // PAIRS)
                        dve.wait_ge(p_rounded, b * NP + n + 1)
                        dve.tensor_tensor(p_low[:, n % 3, 0:m // P, :], turned[n % 2][:, 0:m].rearrange("p (j q) -> p j q", q=P),
                                          p_high[:, n % 3, 0:m // P, :], ALU.subtract).then_inc(p_parted, 1)

                    def causal(m):
                        dve.wait_ge(l_scored, b * NQ + m + 1)
                        if m >= 2:
                            dve.wait_ge(l_mixed, b * NQ + m - 1)
                        dve.tensor_tensor(linT[:, m % 2], lin_bank[:, :].rearrange("p (h q) -> p h q", q=P),
                                          c.f("causal_t").unsqueeze(1).broadcast_to([P, 4, P]), ALU.mult).then_inc(l_masked, 1)

                    def outs(blk):
                        i = blk % 2
                        dve.wait_ge(mixed, b * NP + (blk + 1) * PAIRS)
                        if blk >= 2:
                            dve.wait_ge(y_turned, b * BPS + blk - 1)
                        a = win_out[:, 0:AH * AW].rearrange("p (h e) -> p h e", e=AW)
                        link(dve.reciprocal(den[:, 0, :], a[:, :, AE]))
                        dve.tensor_tensor(yy[:, i, 0, :].rearrange("p (h e) -> p h e", e=AE), a[:, :, 0:AE],
                                          den[:, 0, :].unsqueeze(2).broadcast_to([P, AH, AE]), ALU.mult).then_inc(w_out, 1)
                        dve.wait_ge(l_mixed, b * NQ + 4 * blk + 4)
                        a = lin_out[:, 0:AH * AW].rearrange("p (h e) -> p h e", e=AW)
                        link(dve.tensor_scalar(den[:, 1, :], a[:, :, AE], 1e-6, None, ALU.add))
                        link(dve.reciprocal(den[:, 1, :], den[:, 1, :]))
                        dve.tensor_tensor(yy[:, i, 1, :].rearrange("p (h e) -> p h e", e=AE), a[:, :, 0:AE],
                                          den[:, 1, :].unsqueeze(2).broadcast_to([P, AH, AE]), ALU.mult).then_inc(l_out, 1)

                    row_max(0)
                    for n in range(NP + 2):
                        if n + 1 < NP:
                            row_max(n + 1)
                        if 0 <= n - 1 < NP:
                            part_probs(n - 1)
                        if n < NP and n % 2 == 0:
                            causal(n // 2)
                        if n >= PAIRS + 1 and (n - PAIRS - 1) % PAIRS == 0:
                            outs((n - PAIRS - 1) // PAIRS)
                        if n >= PAIRS + 7 and n < NP and (n - PAIRS - 7) % PAIRS == 0:
                            add_proj(b, (n - PAIRS - 7) // PAIRS)
                        if n == NEXT_STATS and not last:
                            statistics(b + 1)
                        if n == NEXT_NORM and not last:
                            rows_norm(b + 1)
                    assert n_link[0] == CHAIN, n_link[0]

                flat = lambda t: t[:, :, :].rearrange("p i d -> p (i d)")
                dve.scalar_tensor_tensor(flat(g.x), flat(g.u), 0.5, flat(g.x), ALU.mult, ALU.add).then_inc(started, 1)
                dve.wait_ge(started, 1)
                for q in range(BPS):
                    for k in range(TOPK):
                        j = q % 2 * TOPK + k
                        dve.wait_ge(fetched[j], q // 2 * 16 + 16 + fetched_before)
                        last = dve.scalar_tensor_tensor(g.x[:, q, :], fetched_rows[:, j, :], r.weight[:, q * TOPK + k:q * TOPK + k + 1],
                                                        g.x[:, q, :], ALU.mult, ALU.add)
                        last.then_inc(summed, 1 if k < TOPK - 1 else SUMS - TOPK + 1)
                        dve.wait_ge(summed, q * SUMS + k + 1 if k < TOPK - 1 else q * SUMS + SUMS)
                statistics(0)
                rows_norm(0)
                products(0, None)
                with dve.Fori(0, NB - 1) as b:
                    pairs(b, False)
                    products(b + 1, b)
                pairs(NB - 1, True)
                add_proj(NB - 1, BPS - 1)

            @block.sync
            def _(sp):
                sp.wait_ge(zeroed, 1)

                def place(b):
                    for k in (2 * NCK - 2, 2 * NCK - 1):
                        wait_split(sp, b, k)
                    for j in range(4):
                        rows = slice(32 * j, 32 * j + 32)
                        sp.dma_start(own_a[rows, j, :, :], dup[rows, KA, :, :]).then_inc(placed, 16)

                place(0)
                with sp.Fori(0, NB - 1) as b:
                    place(b + 1)

            @block.gpsimd
            def _(pool):
                pool.memset(own_a[:, :, :, :], 0.0).then_inc(zeroed, 1)
                pool.memset(fence[:, :], 0.0).then_inc(fenced, 1)
                pool.wait_ge(fenced, 1)

                def splits(b, before):
                    mine = [k for k in range(NS) if k not in BY_DVE]
                    for i, k in enumerate(mine):
                        if i:
                            pool.wait_ge(dup_p, b * len(mine) + i)
                        elif before:
                            pool.wait_ge(dup_p, b * len(mine))
                        if k < 2 * NCK:
                            pool.wait_ge(z_copied, b * NZ + k + 1)
                        else:
                            pool.wait_ge(high_made, b * NS + k + 1)
                        pool.tensor_tensor(fence[:, 0:1], fence[:, 1:2], fence[:, 1:2], ALU.add).then_inc(fenced, 1)
                        split(pool, k).then_inc(dup_p, 1)

                def hold():
                    return pool.tensor_tensor(fence[:, 0:1], fence[:, 1:2], fence[:, 1:2], ALU.add)

                def fetch(b):
                    def gather(q):
                        a = q % 2 * TOPK
                        if isinstance(b, int) and q >= 2:
                            pool.wait_ge(summed, (q - 1) * SUMS)
                        at = bass.DynSlice(b * (BPS * TOPK) + q * TOPK, TOPK)
                        pool.tensor_copy(slots[:, a:a + TOPK], r.slot[:, at]).then_inc(idx_ready, 1)
                        pool.tensor_copy(weights[:, a:a + TOPK], r.weight[:, at]).then_inc(idx_ready, 1)
                        pool.wait_ge(idx_ready, b * (BPS * FETCH) + q * FETCH + 2)
                        hold().then_inc(idx_ready, 1)
                        for j in range(a, a + TOPK):
                            pool.indirect_dma_start(out=fetched_rows[:, j, :], out_offset=None, in_=g.y_dram,
                                                    in_offset=bass.IndirectOffsetOnAxis(ap=slots[:, j:j + 1], axis=0)).then_inc(fetched[j], 16)

                    def add_up(q):
                        a = q % 2 * TOPK
                        n = b * (BPS * SUMS) + q * SUMS
                        if isinstance(b, int):
                            return
                        rows = fetched_rows[:, a:a + TOPK, :]
                        for j in range(a, a + TOPK):
                            pool.wait_ge(fetched[j], b * 32 + (q // 2 * 16 + 16 + fetched_before))
                        pool.tensor_tensor(rows, rows, weights[:, a:a + TOPK].unsqueeze(2).broadcast_to([P, TOPK, D]), ALU.mult).then_inc(summed, 1)
                        pool.wait_ge(summed, n + 1)
                        pool.tensor_tensor(rows[:, 0:2, :], rows[:, 0:2, :], rows[:, 2:4, :], ALU.add).then_inc(summed, 1)
                        pool.wait_ge(summed, n + 2)
                        pool.tensor_tensor(rows[:, 0, :], rows[:, 0, :], rows[:, 1, :], ALU.add).then_inc(summed, 1)
                        pool.wait_ge(summed, n + 3)
                        hold().then_inc(summed, 1)
                        at = g.x[:, bass.DynSlice(b * BPS + q, 1), :].rearrange("p o d -> p (o d)")
                        pool.tensor_tensor(at, rows[:, 0, :], at, ALU.add).then_inc(summed, 1)
                        pool.wait_ge(summed, n + 5)

                    for q in range(BPS):
                        gather(q)
                        if q:
                            add_up(q - 1)
                    add_up(BPS - 1)

                def residual_rows(b):
                    wide = [P, BPS, D]
                    blks = bass.DynSlice(b * BPS, BPS)
                    pool.wait_ge(dup_p, (b + 1) * (NS - len(BY_DVE)))
                    pool.wait_ge(normed, b + 1)
                    hold().then_inc(u_made, 1)
                    pool.tensor_tensor(u_rows[:, :, :], g.x[:, blks, :], mean[:, :].unsqueeze(2).broadcast_to(wide), ALU.subtract).then_inc(u_made, 1)
                    pool.wait_ge(u_made, b * RES + 2)
                    pool.tensor_tensor(u_rows[:, :, :], u_rows[:, :, :], r1[:, :].unsqueeze(2).broadcast_to(wide), ALU.mult).then_inc(u_made, 1)
                    pool.wait_ge(u_made, b * RES + 3)
                    pool.tensor_tensor(u_rows[:, :, :], u_rows[:, :, :], c.row("bo").unsqueeze(1).broadcast_to(wide), ALU.add).then_inc(u_made, 1)
                    pool.wait_ge(u_made, b * RES + 4)
                    hold().then_inc(fenced, 1)
                    pool.tensor_copy(g.u[:, blks, :], u_rows[:, :, :]).then_inc(u_made, 1)
                    pool.wait_ge(u_made, b * RES + 5)

                pool.wait_ge(started, 1)
                fetch(0)
                pool.wait_ge(idx_ready, BPS * FETCH)
                splits(0, False)
                residual_rows(0)
                with pool.Fori(0, NB - 1) as b:
                    fetch(b + 1)
                    splits(b + 1, True)
                    residual_rows(b + 1)

            @block.scalar
            def _(act):

                def roots_of(b):
                    act.wait_ge(var_ready, b + 1)
                    act.activation(roots[:, :], both[:, :], ACT.Sqrt).then_inc(rooted, 1)

                def scale_rows(b):
                    act.wait_ge(x_turned, b + 1)
                    act.activation(xT[:, :], misc[:, :], ACT.Identity, scale=c.col("g1"), bias=c.col("b1")).then_inc(x_ready, 1)

                def copy_y(b, blk):
                    act.wait_ge(y_turned, b * BPS + blk + 1)
                    act.activation(yT[:, :, :], misc[:, 0:2 * P].rearrange("p (j q) -> p j q", q=P), ACT.Copy).then_inc(yT_ready, 1)

                def copy_m(b, blk):
                    act.wait_ge(m_made, b * BPS + blk + 1)
                    act.activation(mT[:, :], misc[:, 0:P], ACT.Identity, bias=c.col("bp_a")).then_inc(m_ready, 1)

                def products(b, tail):
                    for k in range(NZ):
                        act.wait_ge(z_made, b * NZ + k + 1)
                        bias = g.dup_bias[:, k:k + 1]
                        if k < 2 * NCK:
                            if k >= R:
                                wait_split(act, b, k - R)
                            act.activation(high[:, k % R, :], zbank[k % 4][:, :], ACT.Identity, scale=low_rows(k // NCK),
                                           bias=g.dup_bias[:, 17 + k:18 + k]).then_inc(high_made, 1)
                            act.activation(whole[:, k % R, :], zbank[k % 4][:, :], ACT.Identity, bias=bias).then_inc(z_copied, 1)
                        else:
                            if k >= 10:
                                act.wait_ge(q_made, b * 9 + k - 10 + 1)
                            act.activation(raised[:, k % 2, :], zbank[k % 4][:, :], ACT.Exp, bias=bias).then_inc(z_copied, 1)
                        if k > 2 * NCK:
                            act.wait_ge(q_made, b * 9 + k - 8)
                            wait_split(act, b, k - 1 - R)
                            act.activation(high[:, (k - 1) % R, :], whole[:, (k - 1) % R, :], ACT.Copy,
                                           scale=low_rows((k - 1) // NCK)).then_inc(high_made, 1)
                        if k == 1 and tail is not None:
                            copy_y(tail, BPS - 1)
                        if k == 3 and tail is not None:
                            copy_m(tail, BPS - 1)
                        if 6 <= k < 6 + BPS:
                            blk = k - 6
                            act.wait_ge(t_biased, b * BPS + blk + 1)
                            if blk >= 2:
                                act.wait_ge(t_ready, b * BPS + blk - 1)
                            act.activation(ktok[:, blk, :], kz[:, blk, :], ACT.Exp).then_inc(k_exped, 1)
                        if k == 11:
                            act.activation(va_high[:, :, :, :], va[:, :, :, :], ACT.Copy).then_inc(va_rounded, 1)

                def pairs(b, last):
                    def exps(n):
                        blk, pr = divmod(n, PAIRS)
                        act.wait_ge(maxed, b * NP + n + 1)
                        if n >= 2:
                            act.wait_ge(p_turned, b * NP + n - 1)
                        w = keys(blk)
                        for h in range(2):
                            last = act.activation(probs[:, n % 2, h, 0:w], scores[n % 2][:, h * w:(h + 1) * w], ACT.Exp,
                                                  bias=neg[:, blk, pr, h:h + 1])
                        last.then_inc(probed, 1)

                    def round_probs(n):
                        blk = n // PAIRS
                        act.wait_ge(p_turned, b * NP + n + 1)
                        if n >= 3:
                            act.wait_ge(mixed, b * NP + n - 2)
                        m = 2 * keys(blk)
                        act.activation(p_high[:, n % 3, 0:m // P, :], turned[n % 2][:, 0:m].rearrange("p (j q) -> p j q", q=P),
                                       ACT.Copy).then_inc(p_rounded, 1)

                    for n in range(NP + 1):
                        if n < NP:
                            exps(n)
                        if n >= 1:
                            round_probs(n - 1)
                        m = n - PAIRS - 3
                        if n < NP and m >= 0 and m % PAIRS == 0:
                            copy_y(b, m // PAIRS)
                        if n < NP and m >= 0 and m % PAIRS == 2:
                            copy_m(b, m // PAIRS)
                        if n == NEXT_STATS + 1 and not last:
                            roots_of(b + 1)
                        if n == NEXT_TURN and not last:
                            scale_rows(b + 1)

                roots_of(0)
                scale_rows(0)
                products(0, None)
                with act.Fori(0, NB - 1) as b:
                    pairs(b, False)
                    products(b + 1, b)
                pairs(NB - 1, True)
                copy_y(NB - 1, BPS - 1)
                copy_m(NB - 1, BPS - 1)

            @block.tensor
            def _(pe):
                pe.wait_ge(ones, 2)

                def turn_rows(b):
                    pe.wait_ge(normed, b + 1)
                    for j in range(BPS):
                        last = pe.transpose(misc[:, j * P:(j + 1) * P], hn[:, j, :], c.ident)
                    last.then_inc(x_turned, 1)

                def turn_y(b, blk):
                    pe.wait_ge(l_out, b * BPS + blk + 1)
                    if blk:
                        pe.wait_ge(added, b * BPS + blk)
                    for q in range(2):
                        last = pe.transpose(misc[:, q * P:(q + 1) * P], yy[:, blk % 2, q, :], c.ident)
                    last.then_inc(y_turned, 1)

                def merge(b, blk):
                    pe.wait_ge(yT_ready, b * BPS + blk + 1)
                    pe.matmul(misc[:, 0:P], g.w_p[:, :], yT[:, 0, :], start=True, stop=False)
                    pe.matmul(misc[:, 0:P], g.w_os[:, :], yT[:, 1, :], start=False, stop=True).then_inc(m_made, 1)

                def project(b, blk):
                    pe.wait_ge(m_ready, b * BPS + blk + 1)
                    pe.matmul(misc[:, 0:D], mT[:, :], g.w_o[:, :], start=True, stop=True).then_inc(projected, 1)

                def products(b, tail):
                    pe.wait_ge(x_ready, b + 1)
                    for k in range(NZ):
                        if tail is not None and k == 0:
                            pe.wait_ge(p_parted, tail * NP + NP)
                        if tail is not None and k == 2:
                            pe.wait_ge(l_masked, tail * NQ + NQ)
                        if 4 <= k < 12:
                            pe.wait_ge(z_copied, b * NZ + k - 3)
                        elif k >= 12:
                            pe.wait_ge(z_used, b * 9 + k - 12 + 1)
                        kind, ck = divmod(k, NCK)
                        lhs = g.w_dup[:, kind, ck * P:(ck + 1) * P] if k < NS else g.w_qs[:, :]
                        pe.matmul(zbank[k % 4][:, :], lhs, xT[:, :], start=True, stop=True).then_inc(z_made, 1)
                        if tail is not None:
                            if k == 1:
                                turn_y(tail, BPS - 1)
                            if k == 3:
                                merge(tail, BPS - 1)
                            if k == 4:
                                project(tail, BPS - 1)
                            if k == 6:
                                pe.wait_ge(added, tail * BPS + BPS)
                        if 3 <= k < 3 + BPS:
                            blk = k - 3
                            pe.matmul(tbank[blk][:, 0:3 * D], xT[:, blk * P:(blk + 1) * P], g.w_tok[:, :], start=True, stop=True).then_inc(t_made, 1)
                    pe.wait_ge(t_ready, b * BPS + BPS)
                    for m in range(BPS - 1):
                        for j in range(m + 1):
                            last = pe.matmul(misc[:, m * AH * AW:(m + 1) * AH * AW], ktok[:, j, :],
                                             vs[:, j].rearrange("p h e -> p (h e)"), start=j == 0, stop=j == m)
                    last.then_inc(st_made, 1)

                def pairs(b, is_last):
                    def score(n):
                        blk, pr = divmod(n, PAIRS)
                        j, ck, _ = pair_heads(pr)
                        if n == 0:
                            pe.wait_ge(placed, b * 64 + 64)
                        w = keys(blk)
                        bank = scores[n % 2]
                        pe.matmul(bank[:, 0:2 * w], c.ident_bf, c.first if blk == 0 else c.h("band_x"), start=True, stop=False)
                        for h in range(2):
                            last = pe.matmul(bank[:, h * w:(h + 1) * w], dup[:, QA, ck + h, blk * P:(blk + 1) * P],
                                             own_a[:, j, ck + h, (blk + 1) * P - w:(blk + 1) * P], start=False, stop=h == 1)
                        last.then_inc(scored, 1)

                    def turn(n):
                        blk = n // PAIRS
                        pe.wait_ge(probed, b * NP + n + 1)
                        if n >= 2:
                            pe.wait_ge(p_parted, b * NP + n - 1)
                        nk = keys(blk) // P
                        for h in range(2):
                            for j in range(nk):
                                at = (h * nk + j) * P
                                last = pe.transpose(turned[n % 2][:, at:at + P], probs[:, n % 2, h, j * P:(j + 1) * P], c.ident)
                        last.then_inc(p_turned, 1)

                    def mix(n):
                        blk, pr = divmod(n, PAIRS)
                        pe.wait_ge(p_parted, b * NP + n + 1)
                        if n == 0:
                            pe.wait_ge(va_parted, b + 1)
                        if pr == 0 and blk:
                            pe.wait_ge(w_out, b * BPS + blk)
                        nk = keys(blk) // P
                        for h, head in enumerate(pair_heads(pr)[2]):
                            for j in range(nk):
                                at = (slice(None), blk - nk + 1 + j, head, slice(None))
                                for i, (p, vv) in enumerate(((p_high, va_low), (p_low, va_high), (p_high, va_high))):
                                    last = pe.matmul(win_out[:, head * AW:(head + 1) * AW], p[:, n % 3, h * nk + j, :], vv[at],
                                                     start=j == 0 and i == 0, stop=j == nk - 1 and i == 2)
                        last.then_inc(mixed, 1)

                    def lin_score(m):
                        blk, j = divmod(m, 4)
                        if m >= 1:
                            pe.wait_ge(l_masked, b * NQ + m)
                        else:
                            wait_split(pe, b, NS - 1)
                        rows = slice(32 * j, 32 * j + 32)
                        cols = slice(blk * P, (blk + 1) * P)
                        for ck in range(4):
                            last = pe.matmul(lin_bank[:, ck * P:(ck + 1) * P], dup[rows, KS, ck, cols], dup[rows, QS, ck, cols],
                                             start=True, stop=True)
                        last.then_inc(l_scored, 1)

                    def lin_mix(m):
                        blk, j = divmod(m, 4)
                        pe.wait_ge(l_masked, b * NQ + m + 1)
                        if j == 0 and blk:
                            pe.wait_ge(l_out, b * BPS + blk)
                            pe.matmul(lin_out[:, 0:AH * AW], qcT[:, blk * P:(blk + 1) * P], state[:, blk - 1, :], start=True, stop=False)
                        for ck in range(4):
                            head = 4 * ck + j
                            last = pe.matmul(lin_out[:, head * AW:(head + 1) * AW], linT[:, m % 2, ck, :], vs[:, blk, head, :],
                                             start=blk == 0, stop=blk == 0 or (ck == 3 and j == 3))
                        last.then_inc(l_mixed, 1)

                    score(0)
                    score(1)
                    pe.wait_ge(st_ready, b + 1)
                    pe.wait_ge(q_made, b * 9 + 9)
                    for n in range(NP + 2):
                        if n < NP:
                            turn(n)
                        if n + 2 < NP:
                            score(n + 2)
                        if n < NP and n % 2 == 0:
                            lin_score(n // 2)
                        if n >= 2:
                            mix(n - 2)
                        if n >= 2 and n % 2 == 0:
                            lin_mix(n // 2 - 1)
                        if n == NEXT_TURN and not is_last:
                            pe.wait_ge(added, b * BPS + BPS - 1)
                            turn_rows(b + 1)
                        m = n - PAIRS - 2
                        if m >= 0 and n < NP:
                            if m % PAIRS == 0:
                                turn_y(b, m // PAIRS)
                            if m % PAIRS == 2:
                                merge(b, m // PAIRS)
                            if m % PAIRS == 4:
                                project(b, m // PAIRS)

                turn_rows(0)
                products(0, None)
                with pe.Fori(0, NB - 1) as b:
                    pairs(b, False)
                    products(b + 1, b)
                pairs(NB - 1, True)
                turn_y(NB - 1, BPS - 1)
                merge(NB - 1, BPS - 1)
                project(NB - 1, BPS - 1)


def mlp(nc, g, S):
    with ExitStack() as ctx:
        def sb(name, shape, dt=F32):
            return ctx.enter_context(nc.sbuf_tensor("m_" + name, shape, dt))

        NCK = DM // P
        hn = sb("hn", [P, BPS, D])
        hT = sb("hT", [P, SEQ])
        mid = sb("mid", [P, NCK, SEQ])
        c = g.c
        start, normed, turned, hT_ready, upped, gelued, downed, added, chain = (
            S("m_" + n) for n in ("start", "normed", "turned", "hT", "upped", "gelu", "downed", "added", "chain"))
        rows, ups, downs = g.bank[0], g.bank[1:5], g.bank[5:7]

        with nc.Block() as block:
            @block.vector
            def _(dve):
                dve.tensor_tensor(g.x[:, :, :], g.x[:, :, :], g.u[:, :, :], ALU.add).then_inc(start, 1)
                dve.wait_ge(start, 1)
                dve.tensor_tensor(g.x[:, :, :], g.x[:, :, :], c.row("b2m").unsqueeze(1).broadcast_to([P, NBLK, D]), ALU.add).then_inc(start, 1)
                dve.wait_ge(start, 2)

                def rows_norm(b, first=False):
                    if not first:
                        dve.wait_ge(turned, b)
                    blks = bass.DynSlice(b * BPS, BPS)
                    dve.tensor_tensor(hn[:, :, :], g.u[:, blks, :],
                                      g.stat.mean[:, blks].unsqueeze(2).broadcast_to([P, BPS, D]), ALU.subtract).then_inc(chain, 1)
                    dve.wait_ge(chain, b + 1)
                    dve.tensor_tensor(hn[:, :, :], hn[:, :, :],
                                      g.stat.r[:, blks].unsqueeze(2).broadcast_to([P, BPS, D]), ALU.mult).then_inc(normed, 1)

                def scale_rows(b, first=False):
                    dve.wait_ge(turned, b + 1)
                    if not first:
                        dve.wait_ge(upped, b * NCK)
                    dve.tensor_scalar(hT[:, :], rows[:, :], c.col("gm"), c.col("bm"), ALU.mult, ALU.add).then_inc(hT_ready, 1)

                def add_down(b):
                    for blk in range(BPS):
                        dve.wait_ge(downed, b * BPS + blk + 1)
                        at = g.x[:, bass.DynSlice(b * BPS + blk, 1), :].rearrange("p o d -> p (o d)")
                        dve.tensor_tensor(at, downs[blk % 2][:, 0:D], at, ALU.add).then_inc(added, 1)

                rows_norm(0, True)
                scale_rows(0, True)
                with dve.Fori(0, NB - 1) as b:
                    rows_norm(b + 1)
                    scale_rows(b + 1)
                    add_down(b)
                add_down(NB - 1)

            @block.scalar
            def _(act):
                with act.Fori(0, NB) as b:
                    for k in range(NCK):
                        act.wait_ge(upped, b * NCK + k + 1)
                        act.activation(mid[:, k, :], ups[k][:, :], ACT.Gelu, bias=c.col(f"b1m{k}")).then_inc(gelued, 1)

            @block.tensor
            def _(pe):

                def turn_rows(b):
                    pe.wait_ge(normed, b + 1)
                    for j in range(BPS):
                        last = pe.transpose(rows[:, j * P:(j + 1) * P], hn[:, j, :], c.ident)
                    last.then_inc(turned, 1)

                def up(b):
                    pe.wait_ge(hT_ready, b + 1)
                    for k in range(NCK):
                        pe.matmul(ups[k][:, :], g.w1[:, k * P:(k + 1) * P], hT[:, :], start=True, stop=True).then_inc(upped, 1)

                def down(b, first=False):
                    pe.wait_ge(gelued, b * NCK + NCK)
                    for blk in range(BPS):
                        if blk >= 2:
                            pe.wait_ge(added, b * BPS + blk - 1)
                        elif not first:
                            pe.wait_ge(added, b * BPS - 1 + blk)
                        for k in range(NCK):
                            last = pe.matmul(downs[blk % 2][:, 0:D], mid[:, k, blk * P:(blk + 1) * P], g.w2[:, k, :],
                                             start=k == 0, stop=k == NCK - 1)
                        last.then_inc(downed, 1)

                turn_rows(0)
                up(0)
                turn_rows(1)
                down(0, True)
                with pe.Fori(1, NB - 1) as b:
                    up(b)
                    turn_rows(b + 1)
                    down(b)
                up(NB - 1)
                down(NB - 1)


def build(nc, w, out):
    with ExitStack() as ctx:
        g = Shared()

        def sb(name, shape, dt=F32):
            return ctx.enter_context(nc.sbuf_tensor(name, shape, dt))

        half_sems = {}

        def S(name):
            if name[:3] not in ("f1_", "f2_"):
                return ctx.enter_context(nc.semaphore(name))
            if name[3:] not in half_sems:
                half_sems[name[3:]] = ctx.enter_context(nc.semaphore("ffn_" + name[3:]))
            return half_sems[name[3:]]

        g.x = sb("x", [P, NBLK, D])
        g.u = sb("u", [P, NBLK, D])
        g.w_qk = sb("w_qk", [P, NCH, P])
        g.w_rot = sb("w_rot", [P, NCH, P])
        g.w_v = sb("w_v", [P, KVH * DH])
        g.w_proj = sb("w_proj", [P, QCH, D])
        g.gate = sb("gate", [P, NE])
        g.w_up = sb("w_up", [P, NE, 2 * DFF])
        g.w_down = sb("w_down", [P, NE, D])
        g.w_dup = sb("w_dup", [P, 4, 4 * P])
        g.dup_bias = sb("dup_bias", [P, 34])
        g.w_qs = sb("w_qs", [P, D])
        g.w_tok = sb("w_tok", [P, 3 * D])
        g.w_p = sb("w_p", [P, D])
        g.w_os = sb("w_os", [P, D])
        g.w_o = sb("w_o", [P, D])
        g.w1 = sb("w1", [P, DM])
        g.w2 = sb("w2", [P, DM // P, D])
        g.const = sb("const", [P, NCONST])
        g.const_bf = sb("const_bf", [P, NCONST_BF], BF16)
        g.col = sb("col", [P, NCOL])
        g.row = sb("row", [P, NROW])
        g.neg_sink = sb("neg_sink", [P, HEADS])
        g.qk_bias = sb("qk_bias", [P, 2 * NCH])
        g.bank = [ctx.enter_context(nc.psum_tensor(f"bank{i}", [P, 512], F32)) for i in range(8)]
        st = g.stat = Shared()
        st.six = sb("st_six", [P, NBLK, 6])
        st.mv = sb("st_mv", [P, NBLK, 2])
        st.mean, st.v, st.v2, st.s, st.t, st.r, st.rr = (
            sb("st_" + n, [P, NBLK]) for n in ("mean", "var", "var2", "root", "work", "r", "rr"))

        r = g.routing = Shared()
        r.weight = ctx.enter_context(nc.sbuf_tensor("route_weight", [P, NBLK * TOPK], F32))
        r.slot = ctx.enter_context(nc.sbuf_tensor("route_slot", [P, NBLK * TOPK], U32))
        r.token = ctx.enter_context(nc.sbuf_tensor("route_token", [P, TILES], U32))
        r.owner = ctx.enter_context(nc.sbuf_tensor("route_owner", [1, P], I32))
        iota16 = g.iota16 = sb("iota16", [P, TILES + P], F16)
        g.rows_dram = nc.dram_tensor("rows", (NBLK * P, D), F32, kind="Internal").ap()
        g.y_dram = nc.dram_tensor("expert_rows", (TILES * P, D), F32, kind="Internal").ap()

        def f(name):
            a, b = CONST_F32[name]
            return g.const[:, a:b]

        def h(name):
            a, b = CONST_BF[name]
            return g.const_bf[:, a:b]

        def col(name):
            return g.col[:, COLS[name]:COLS[name] + 1]

        c = g.c = Shared()
        c.ident, c.cos, c.sin = f("ident"), f("cos"), f("sin")
        c.ident_bf, c.band, c.first = h("ident"), h("band"), h("first")
        c.col, c.f, c.h = col, f, h
        c.row = lambda name: g.row[:, ROWS[name][0]:ROWS[name][1]]
        c.row_bv = c.row("bv")
        c.iota_t16, c.iota_s16 = iota16[:, 0:TILES], iota16[:, TILES:TILES + P]

        stage = ExitStack()
        load_rest, later = setup(nc, g, w, S, stage)
        for half, tag in enumerate(("f1", "f2")):
            if tag == "f2":
                with nc.Block() as block:
                    @block.gpsimd
                    def _(pool):
                        for name, sem in half_sems.items():
                            if not name.startswith("e_gathered"):
                                pool.sem_clear(sem)
            normalise(nc, g, S, tag, g.x)
            sink_attention(nc, g, S, tag, load_rest if tag == "f1" else None)
            if tag == "f1":
                later()
                stage.close()
            route(nc, g, S, tag)
            experts(nc, g, S, tag, half)
            if tag == "f2":
                combine(nc, g, S, tag, half)
            else:
                window_and_linear(nc, g, S)
                normalise(nc, g, S, "m", g.u)
                mlp(nc, g, S)
        stored = S("stored")
        with nc.Block() as block:
            @block.sync
            def _(sp):
                sp.dma_start(out.rearrange("b (n p) d -> p (b n) d", p=P), g.x[:, :, :]).then_inc(stored, 16)
                sp.wait_ge(stored, 16)


_INS = ["L0_attn_x", "L0_attn_g1", "L0_attn_b1", "L0_attn_Wqkv_a", "L0_attn_bqkv_a", "L0_attn_Wp_a", "L0_attn_bp_a",
        "L0_attn_Wqkv_s", "L0_attn_bqkv_s", "L0_attn_Wo_s", "L0_attn_bo_s", "L0_attn_Wo", "L0_attn_bo", "L0_attn_gm",
        "L0_attn_bm", "L0_attn_W1", "L0_attn_b1m", "L0_attn_W2", "L0_attn_b2m", "L0_ffn_attn_norm_w",
        "L0_ffn_ffn_norm_w", "L0_ffn_qkv_w", "L0_ffn_qkv_b", "L0_ffn_proj_w", "L0_ffn_proj_b", "L0_ffn_attn_sink",
        "L0_ffn_gate_w", "L0_ffn_gate_b", "L0_ffn_W_up", "L0_ffn_W_down"]


def _constants():
    import numpy as np
    c = np.zeros((P, NCONST), np.float32)

    def put(name, a):
        lo, hi = CONST_F32[name]
        c[:, lo:hi] = a

    p = np.arange(P)
    put("ident", np.eye(P))
    inv = (1.0 / np.float32(150000.0) ** (np.arange(0, DH, 2, dtype=np.float32) / np.float32(DH))).astype(np.float32)
    pos = (np.arange(SEQ, dtype=np.float32) / np.float32(32.0)).astype(np.float32)
    ang = (pos[None, :] * inv[(p % DH) // 2][:, None]).astype(np.float32)
    put("cos", np.cos(ang))
    put("sin", np.sin(ang))
    put("iota_e", np.arange(NE)[None, :])
    put("iota_s", np.arange(P)[None, :])
    put("iota_t", np.arange(TILES)[None, :])
    t = (p % 32) // AE
    put("cols", np.stack([p, -(t >= 2).astype(np.float32), -(t % 2 == 1).astype(np.float32)], 1))
    put("token", p[:, None] + P * np.arange(NBLK)[None, :])
    put("scan", np.tile((np.arange(NBLK) > 0).astype(np.float32), NE)[None, :])
    hd = p // AE
    put("blockdiag", np.repeat(hd[:, None] == np.arange(AH)[None, :], AW, axis=1))
    put("causal_t", (p[:, None] <= p[None, :]))
    h = np.zeros((P, NCONST_BF), np.float32)

    def puth(name, a):
        lo, hi = CONST_BF[name]
        h[:, lo:hi] = a

    big = np.float32(-1e30)
    r, s = p[:, None], p[None, :]
    own = np.where(s <= r, 0, big)
    prev = np.where(s >= r, 0, big)
    prev_x = np.where(s > r, 0, big)
    puth("ident", np.eye(P))
    puth("before", s > r)
    puth("ones", 1.0)
    puth("band", np.concatenate([prev, own, prev, own], 1))
    puth("band_x", np.concatenate([prev_x, own, prev_x, own], 1))
    puth("first", np.concatenate([own, own], 1))
    return c, h


def kernel(**inputs):
    import numpy as _np
    import concourse.bacc as _bacc
    from concourse import mybir as _mybir
    from concourse.bass_utils import run_bass_kernel_spmd as _run

    nc = _bacc.Bacc("TRN2", target_bir_lowering=False, num_devices=1)
    arrays, w = {}, {}
    for name in _INS:
        a = _np.ascontiguousarray(inputs[name])
        arrays[f"in_{name}"] = a
        w[name] = nc.dram_tensor(f"in_{name}", a.shape, _mybir.dt.from_np(a.dtype), kind="ExternalInput").ap()
    for name, a in zip(("const", "const_bf"), _constants()):
        arrays[f"in_{name}"] = a
        w[name] = nc.dram_tensor(f"in_{name}", a.shape, _mybir.dt.from_np(a.dtype), kind="ExternalInput").ap()
    out = nc.dram_tensor("out_0_dram", (NB, SEQ, D), _mybir.dt.float32, kind="ExternalOutput").ap()
    build(nc, w, out)
    r = _run(nc, [arrays], core_ids=[0])
    return r.results[0]["out_0_dram"]
```
